# Optimizing a Trainium2 kernel written in Bass

```python
import numpy as np
import jax
import jax.numpy as jnp

def _softmax(x, axis=-1):
    return jax.nn.softmax(x, axis=axis)

def _gelu(x):
    return jax.nn.gelu(x, approximate=True)

def _silu(x):
    return jax.nn.silu(x)

def _sigmoid(x):
    return jax.nn.sigmoid(x)

def _layernorm(x, axis=-1, eps=1e-05):
    m = jnp.mean(x, axis=axis, keepdims=True)
    v = jnp.var(x, axis=axis, keepdims=True)
    return (x - m) / jnp.sqrt(v + eps)

def _scatter_add(tgt, idx, src, axis=0):
    return tgt.at[idx].add(src)

def _segment_sum(src, seg, n):
    return jax.ops.segment_sum(src, seg, n)
kernel_name = 'mk_xattn_ffn_d1_seqx_r2_00abdd'

def setup_inputs(seed: int=0):
    np.random.seed(seed)
    _w = jnp.asarray

    def _rec_inputs():
        import jax
        import jax.numpy as jnp
        _rk = jax.random.key(seed)
        x = -0.0002928 + 1 * jax.random.normal(jax.random.fold_in(_rk, 1), (8, 224, 512), jnp.float32)
        _lenS = 224 - jax.random.randint(jax.random.fold_in(_rk, 7), (8,), 0, max(1, 224 // 4) + 1, jnp.int32)
        _lenS2 = 750 - jax.random.randint(jax.random.fold_in(_rk, 8), (8,), 0, max(1, 750 // 4) + 1, jnp.int32)
        _ctx_1024P = jax.random.normal(jax.random.fold_in(_rk, 11), (8, 16, 512), jnp.float32)
        _ctx_1024c = jax.random.dirichlet(jax.random.fold_in(_rk, 511), 0.3 * jnp.ones((16,), jnp.float32), (8, 750))
        _ctx_1024t = jnp.einsum('bsk,bkd->bsd', _ctx_1024c, _ctx_1024P)
        _ctx_1024t = _ctx_1024t * jax.lax.rsqrt(jnp.mean(jnp.square(_ctx_1024t)) + 1e-12) * 0.953939
        ctx_1024 = -1.39393e-06 + 0.999914 * (_ctx_1024t + 0.3 * jax.random.normal(jax.random.fold_in(_rk, 611), (8, 750, 512), jnp.float32))
        fside_1xSxS2_0 = 0.000675642 + 1.00031 * jax.random.normal(jax.random.fold_in(_rk, 12), (1, 224, 750), jnp.float32)
        _validS = jnp.arange(224)[None, :] < _lenS[:, None]
        _validS2 = jnp.arange(750)[None, :] < _lenS2[:, None]
        _causal = jnp.tril(jnp.ones((224, 224), dtype=bool))
        mask_BxS2_bk0 = jnp.logical_not(jnp.broadcast_to(_validS2[:, :], (8, 750)))
        return (x, ctx_1024, fside_1xSxS2_0, mask_BxS2_bk0)
    x, ctx_1024, fside_1xSxS2_0, mask_BxS2_bk0 = _rec_inputs()

    def _L0_xattn_setup():
        import jax, jax.numpy as jnp
        import numpy as np
        EMBED_DIM = 512
        NUM_HEADS = 16
        HEAD_DIM = EMBED_DIM // NUM_HEADS
        SCALING = float(HEAD_DIM * 1.0) ** (-0.5)
        NEG_INF = float(np.finfo(np.float32).min)
        key = jax.random.key(seed)
        ks = jax.random.split(key, 8)
        B, T, S, E = (2, 1024, 1024, EMBED_DIM)
        return {'query': jax.random.normal(ks[0], (B, T, E), jnp.float32), 'key': jax.random.normal(ks[1], (B, S, E), jnp.float32), 'value': jax.random.normal(ks[2], (B, S, E), jnp.float32), 'attn_bias': jax.random.normal(ks[3], (1, T, S), jnp.float32), 'key_padding_mask': jax.random.randint(ks[4], (B, S), 0, 2).astype(bool), 'in_proj_w': jax.random.normal(ks[5], (3 * E, E), jnp.float32) * E ** (-0.5), 'in_proj_b': jnp.zeros((3 * E,), jnp.float32), 'out_proj_w': jax.random.normal(ks[6], (E, E), jnp.float32) * E ** (-0.5), 'out_proj_b': jnp.zeros((E,), jnp.float32)}
    _L0_xattn_all = _L0_xattn_setup()
    _L0_xattn_in = {k: v for k, v in _L0_xattn_all.items() if k in ('in_proj_w', 'in_proj_b', 'out_proj_w', 'out_proj_b')}
    del _L0_xattn_all

    def _L0_ffn_setup():
        import jax, jax.numpy as jnp
        import numpy as np
        IN_DIM, OUT_DIM, N_PROTO, RANK = (512, 512, 32, 16)
        key = jax.random.key(seed)
        ks = jax.random.split(key, 5)
        x = jax.random.normal(ks[0], (2, 2048, IN_DIM), dtype=jnp.float32)
        prototypes = jax.random.normal(ks[1], (N_PROTO, IN_DIM), dtype=jnp.float32) * 0.02
        B = jax.random.normal(ks[2], (N_PROTO, RANK, IN_DIM), dtype=jnp.float32) * 0.02
        A = jax.random.normal(ks[3], (N_PROTO, OUT_DIM, RANK), dtype=jnp.float32) * 0.02
        bias = jnp.zeros((N_PROTO, OUT_DIM), dtype=jnp.float32)
        temp = jnp.asarray(1.0, dtype=jnp.float32)
        return {'x': x, 'prototypes': prototypes, 'B': B, 'A': A, 'bias': bias, 'temp': temp}
    _L0_ffn_all = _L0_ffn_setup()
    _L0_ffn_in = {k: v for k, v in _L0_ffn_all.items() if k in ('prototypes', 'B', 'A', 'bias', 'temp')}
    del _L0_ffn_all
    return {'x': x, 'ctx_1024': ctx_1024, 'fside_1xSxS2_0': fside_1xSxS2_0, 'mask_BxS2_bk0': mask_BxS2_bk0, 'L0_xattn_in_proj_w': _L0_xattn_in['in_proj_w'], 'L0_xattn_in_proj_b': _L0_xattn_in['in_proj_b'], 'L0_xattn_out_proj_w': _L0_xattn_in['out_proj_w'], 'L0_xattn_out_proj_b': _L0_xattn_in['out_proj_b'], 'L0_ffn_prototypes': _L0_ffn_in['prototypes'], 'L0_ffn_B': _L0_ffn_in['B'], 'L0_ffn_A': _L0_ffn_in['A'], 'L0_ffn_bias': _L0_ffn_in['bias'], 'L0_ffn_temp': _L0_ffn_in['temp']}

def reference(x, ctx_1024, fside_1xSxS2_0, mask_BxS2_bk0, L0_xattn_in_proj_w, L0_xattn_in_proj_b, L0_xattn_out_proj_w, L0_xattn_out_proj_b, L0_ffn_prototypes, L0_ffn_B, L0_ffn_A, L0_ffn_bias, L0_ffn_temp):
    import jax
    import jax.numpy as jnp

    def _L0_xattn_ref(query, key, value, attn_bias, key_padding_mask, in_proj_w, in_proj_b, out_proj_w, out_proj_b):
        import jax, jax.numpy as jnp
        import numpy as np
        EMBED_DIM = 512
        NUM_HEADS = 16
        HEAD_DIM = EMBED_DIM // NUM_HEADS
        SCALING = float(HEAD_DIM * 1.0) ** (-0.5)
        NEG_INF = float(np.finfo(np.float32).min)
        B, T, E = query.shape
        S = key.shape[1]
        H, D = (NUM_HEADS, HEAD_DIM)
        w_q, w_k, w_v = (in_proj_w[:E], in_proj_w[E:2 * E], in_proj_w[2 * E:])
        b_q, b_k, b_v = (in_proj_b[:E], in_proj_b[E:2 * E], in_proj_b[2 * E:])
        q = (query @ w_q.T + b_q).reshape(B, T, H, D)
        k = (key @ w_k.T + b_k).reshape(B, S, H, D)
        v = (value @ w_v.T + b_v).reshape(B, S, H, D)
        scores = jnp.einsum('bthd,bshd->bhts', q * SCALING, k)
        scores = scores + attn_bias[None]
        scores = jnp.where(key_padding_mask[:, None, None, :], NEG_INF, scores)
        attn = jax.nn.softmax(scores, axis=-1)
        out = jnp.einsum('bhts,bshd->bthd', attn, v).reshape(B, T, E)
        return out @ out_proj_w.T + out_proj_b

    def _L0_ffn_ref(x, prototypes, B, A, bias, temp):
        import jax, jax.numpy as jnp
        import numpy as np
        IN_DIM, OUT_DIM, N_PROTO, RANK = (512, 512, 32, 16)
        lead = x.shape[:-1]
        xf = x.reshape(-1, IN_DIM)
        x2 = jnp.sum(xf * xf, axis=1, keepdims=True)
        p2 = jnp.sum(prototypes * prototypes, axis=1)
        d2 = x2 + p2[None, :] - 2.0 * (xf @ prototypes.T)
        dists = jnp.sqrt(jnp.maximum(d2, 0.0))
        t = jnp.maximum(jnp.abs(temp), 0.1)
        w = jax.nn.softmax(-dists / t, axis=1)
        topw, topi = jax.lax.top_k(w, 2)
        topw = topw / jnp.sum(topw, axis=1, keepdims=True)
        out = jnp.zeros((xf.shape[0], OUT_DIM), dtype=xf.dtype)
        for tslot in range(2):
            idx = topi[:, tslot]
            wt = topw[:, tslot:tslot + 1]
            h = jnp.einsum('nri,ni->nr', B[idx], xf)
            y = jnp.einsum('nor,nr->no', A[idx], h) + bias[idx]
            out = out + wt * y
        return out.reshape(*lead, OUT_DIM)
    x = x + _L0_xattn_ref(_layernorm(x, axis=-1), ctx_1024, ctx_1024, fside_1xSxS2_0, mask_BxS2_bk0, L0_xattn_in_proj_w, L0_xattn_in_proj_b, L0_xattn_out_proj_w, L0_xattn_out_proj_b)
    x = x + _L0_ffn_ref(_layernorm(x, axis=-1), L0_ffn_prototypes, L0_ffn_B, L0_ffn_A, L0_ffn_bias, L0_ffn_temp)
    return x

_drawn_inputs = setup_inputs


def setup_inputs(seed=0):
    import zlib

    import numpy as np

    out = dict(_drawn_inputs(seed))
    spreads = {'L0_xattn_in_proj_b': (0.0, 0.1),
     'L0_xattn_out_proj_b': (0.0, 0.1),
     'L0_ffn_bias': (0.0, 0.1)}
    factors = {}
    for name, (base, spread) in spreads.items():
        noise = np.random.default_rng([zlib.crc32(name.encode()), seed]).standard_normal(out[name].shape)
        drawn = base * np.exp(spread * noise) if base else spread * noise
        out[name] = jnp.asarray(drawn.astype(out[name].dtype))
    for name, factor in factors.items():
        out[name] = (out[name] * factor).astype(out[name].dtype)
    return out
```

```python
import numpy as np
from contextlib import ExitStack

import concourse.bass as bass
from concourse import mybir

F32 = mybir.dt.float32
F32R = mybir.dt.float32r
U8 = mybir.dt.uint8
ALU = mybir.AluOpType
ACT = mybir.ActivationFunctionType
AX = mybir.AxisListType

P = 128
B, T, E = 8, 224, 512
S = 750
H, D = 16, 32
NP, RK = 32, 16
KT = E // P
HG = P // D
NG = H // HG
TC = 2
TW = T // TC
ST = 6
SW = S // ST
SH = (376, 374)
SO = (0, 376)
UG = HG * TC
UB = H * TC
SCALE = float(D) ** -0.5
EPS = 1e-5
FMAX = float(np.finfo(np.float32).max)


def apart(eng, passed):
    eng.sem_inc(passed, 1)


def layer_norm_stats(nc, eng, x, stats, mv, veps, sem, n, passed):
    apart(eng, passed)
    for c in range(TC):
        nc.vector.bn_stats(stats[:, c, :], x[:, c, :]).then_inc(sem, 1)
    eng.wait_ge(sem, n + 2)
    apart(eng, passed)
    for c in range(TC):
        nc.vector.bn_aggr(mv[:, c, :], stats[:, c, :]).then_inc(sem, 1)
    eng.wait_ge(sem, n + 4)
    return nc.vector.tensor_scalar(veps[:, :], mv[:, :, 1], EPS, None, ALU.add)


def rsqrt_refined(nc, eng, sd, veps, r, t, sem, n):
    nc.vector.reciprocal(r[:, :], sd[:, :]).then_inc(sem, 1)
    eng.wait_ge(sem, n + 1)
    nc.vector.tensor_tensor(t[:, 0, :], r[:, :], r[:, :], ALU.mult).then_inc(sem, 1)
    eng.wait_ge(sem, n + 2)
    nc.vector.tensor_tensor(t[:, 1, :], t[:, 0, :], veps[:, :], ALU.mult).then_inc(sem, 1)
    eng.wait_ge(sem, n + 3)
    nc.vector.tensor_scalar(t[:, 2, :], t[:, 1, :], -0.5, 1.5, ALU.mult, ALU.add).then_inc(sem, 1)
    eng.wait_ge(sem, n + 4)
    nc.vector.tensor_tensor(t[:, 3, :], t[:, 2, :], r[:, :], ALU.mult).then_inc(sem, 1)
    eng.wait_ge(sem, n + 5)


def project(nc, x, ctx_t, w_in_t, b_in, bv, q_parts, k_parts, v_all, ident):
    with ExitStack() as ctx:
        def sb(name, shape, dt=F32):
            return ctx.enter_context(nc.sbuf_tensor(name, shape, dt))

        def sem(name):
            return ctx.enter_context(nc.semaphore(name))

        w_stage = [sb(f"w_stage{j}", [P, KT, E]) for j in range(3)]
        w_hi = [sb(f"w_hi{j}", [P, KT, E], F32R) for j in range(3)]
        w_lo = [sb(f"w_lo{j}", [P, KT, E], F32R) for j in range(3)]
        ctx_raw = [sb(f"ctx_raw{p}", [P, KT, S]) for p in range(2)]
        ctx_hi = [sb(f"ctx_hi{p}", [P, KT, S], F32R) for p in range(2)]
        ctx_lo = [sb(f"ctx_lo{p}", [P, KT, S], F32R) for p in range(2)]
        x_in = sb("x_in", [TW, TC, E])
        xn = sb("xn", [TW, TC, E])
        xt_hi = sb("xt_hi", [P, KT, T], F32R)
        xt_lo = sb("xt_lo", [P, KT, T], F32R)
        k_hi = [sb(f"k_hi{r}", [P, S], F32R) for r in range(2)]
        k_lo = [sb(f"k_lo{r}", [P, S], F32R) for r in range(2)]
        v_out = [sb(f"v_out{r}", [SW, E]) for r in range(2)]
        q_f = sb("q_f", [P, NG, T])
        q_hi = sb("q_hi", [P, NG, T], F32R)
        q_lo = sb("q_lo", [P, NG, T], F32R)
        bias_col = sb("bias_col", [P, 12])
        nbq = sb("nbq", [P, NG])
        bv_row = sb("bv_row", [SW, E])
        stats = sb("stats", [TW, TC, 6])
        mv = sb("mv", [TW, TC, 2])
        veps = sb("veps", [TW, TC])
        sd = sb("sd", [TW, TC])
        rstd = sb("rstd", [TW, TC])
        nwt = sb("nwt", [TW, 4, TC])
        NACC = 4
        acc = [ctx.enter_context(nc.psum_tensor(f"acc{j}", [P, 512], F32)) for j in range(NACC)]
        xt_ps = [ctx.enter_context(nc.psum_tensor(f"xt_ps{c}", [P, 512], F32)) for c in range(TC)]

        w_loaded = [sem(f"w_loaded{j}") for j in range(3)]
        bias_loaded = sem("bias_loaded")
        ctx_loaded = [sem(f"ctx_loaded{p}") for p in range(2)]
        x_loaded = sem("x_loaded")
        w_hi_ready = sem("w_hi_ready")
        w_ready = sem("w_ready")
        nbq_ready = sem("nbq_ready")
        ctx0_hi_ready = sem("ctx0_hi_ready")
        ctx_hi_done = sem("ctx_hi_done")
        ctx_ready = [sem(f"ctx_ready{p}") for p in range(2)]
        passed = sem("passed1")
        ident_zero = sem("ident_zero")
        ident_ready = sem("ident_ready")
        ln_step = sem("ln_step")
        veps_ready = sem("veps_ready")
        sd_ready = sem("sd_ready")
        xn_ready = sem("xn_ready")
        xt_ps_ready = sem("xt_ps_ready")
        xt_hi_ready = sem("xt_hi_ready")
        xt_ready = sem("xt_ready")
        acc_ready = sem("acc_ready")
        k_hi_ready = sem("k_hi_ready")
        k_ready = sem("k_ready")
        v_ready = sem("v_ready")
        q_f_ready = sem("q_f_ready")
        q_hi_ready = sem("q_hi_ready")
        q_ready = sem("q_ready")
        k_stored = [sem(f"k_stored{r}") for r in range(2)]
        v_stored = [sem(f"v_stored{r}") for r in range(2)]
        q_stored = sem("q_stored")

        KG = NG * 2
        VG = ST
        QG = NG // 2
        AG = KG + VG + QG
        W_ORDER = (1, 2, 0)

        block = ctx.enter_context(nc.Block())

        @block.sync
        def _(eng):
            for started in (*k_stored, *v_stored, q_stored):
                eng.sem_inc(started, 1)
            def load_ctx(b, p):
                eng.dma_start(ctx_raw[p][:, :, :], ctx_t[b].rearrange("(k p) s -> p k s", p=P))\
                   .then_inc(ctx_loaded[p], 16)

            def load_w(j):
                eng.dma_start(w_stage[j][:, :, :],
                              w_in_t[:, j * E:(j + 1) * E].rearrange("(k p) o -> p k o", p=P))\
                   .then_inc(w_loaded[j], 16)

            def load_x(b):
                eng.dma_start(x_in[:, :, :], x[b].rearrange("(c t) e -> t c e", c=TC)).then_inc(x_loaded, 16)

            load_w(1)
            load_ctx(0, 0)
            load_x(0)
            eng.dma_start(bias_col[:, :], b_in).then_inc(bias_loaded, 16)
            eng.dma_start(bv_row[:, :], bv.partition_broadcast(SW)).then_inc(bias_loaded, 16)
            load_w(2)
            load_ctx(1, 1)
            load_w(0)

            def stores(b, n):
                for g in range(NG):
                    eng.wait_ge(k_ready, KG * n + 2 * g + 2)
                    for part, src in enumerate((k_hi, k_lo)):
                        eng.dma_start(k_parts[b, part, g * P:(g + 1) * P, :], src[g % 2][:, :].bitcast(F32))\
                           .then_inc(k_stored[g % 2], 16)
                for s in range(ST):
                    eng.wait_ge(v_ready, 1 + ST * n + s + 1)
                    eng.dma_start(v_all[b, s * SW:(s + 1) * SW, :], v_out[s % 2][:, :])\
                       .then_inc(v_stored[s % 2], 16)
                eng.wait_ge(q_ready, n + 1)
                for part, src in enumerate((q_hi, q_lo)):
                    eng.dma_start(q_parts[b, part].rearrange("(g p) t -> p g t", p=P),
                                  src[:, :, :].bitcast(F32)).then_inc(q_stored, 16)

            with eng.Fori(0, B // 2 - 1) as i:
                for p in range(2):
                    b = 2 * i + p
                    eng.wait_ge(xn_ready, b + 1)
                    load_x(b + 1)
                    eng.wait_ge(ctx_ready[p], i + 1)
                    load_ctx(b + 2, p)
                    stores(b, b)
            for b in (B - 2, B - 1):
                if b < B - 1:
                    eng.wait_ge(xn_ready, b + 1)
                    load_x(b + 1)
                stores(b, b)
            for r in range(2):
                eng.wait_ge(k_stored[r], 1 + 32 * 2 * B)
                eng.wait_ge(v_stored[r], 1 + 16 * 3 * B)
            eng.wait_ge(q_stored, 1 + 32 * B)

        @block.gpsimd
        def _(eng):
            eng.memset(ident[:, :], 0.0).then_inc(ident_zero, 1)
            eng.wait_ge(ident_zero, 1)
            eng.affine_select(out=ident[:, :], in_=ident[:, :], compare_op=ALU.not_equal, fill=1.0,
                              base=0, pattern=[[-1, P]], channel_multiplier=1).then_inc(ident_ready, 1)

            def split(p, i, n):
                eng.wait_ge(ctx_loaded[p], 16 * (i + 1))
                apart(eng, passed)
                eng.tensor_scalar(ctx_hi[p][:, :, :], ctx_raw[p][:, :, :], 1.0, 0.0, ALU.mult, ALU.add)\
                   .then_inc(ctx_hi_done, 1)
                eng.wait_ge(ctx_hi_done, n)
                eng.tensor_tensor(ctx_lo[p][:, :, :], ctx_raw[p][:, :, :], ctx_hi[p][:, :, :].bitcast(F32),
                                  ALU.subtract).then_inc(ctx_ready[p], 1)

            split(1, 0, 1)
            with eng.Fori(1, B // 2) as i:
                for p in range(2):
                    eng.wait_ge(acc_ready, 1 + AG * (2 * i + p - 1) - QG)
                    split(p, i, 2 * i + p)

        @block.scalar
        def _(eng):
            for n, j in enumerate(W_ORDER):
                if n == 1:
                    eng.wait_ge(ctx_loaded[0], 16)
                    nc.scalar.activation(ctx_hi[0][:, :, :], ctx_raw[0][:, :, :], ACT.Copy)\
                        .then_inc(ctx0_hi_ready, 1)
                eng.wait_ge(w_loaded[j], 16)
                nc.scalar.activation(w_hi[j][:, :, :], w_stage[j][:, :, :], ACT.Copy).then_inc(w_hi_ready, 1)
            eng.wait_ge(bias_loaded, 32)
            with eng.Fori(0, B // 2) as i:
                for p in range(2):
                    b = 2 * i + p
                    eng.wait_ge(veps_ready, b + 1)
                    nc.scalar.activation(sd[:, :], veps[:, :], ACT.Sqrt).then_inc(sd_ready, 1)
                    for g in range(NG):
                        eng.wait_ge(k_stored[g % 2], 1 + 32 * (2 * b + g // 2))
                        for h in range(2):
                            eng.wait_ge(acc_ready, 1 + AG * b + 2 * g + h + 1)
                            nc.scalar.activation(k_hi[g % 2][:, SO[h]:SO[h] + SH[h]],
                                                 acc[(2 * g + h) % NACC][:, 0:SH[h]], ACT.Identity,
                                                 bias=bias_col[:, NG + g:NG + g + 1]).then_inc(k_hi_ready, 1)
                    eng.wait_ge(acc_ready, 1 + AG * b)
                    for c in range(TC):
                        eng.wait_ge(xt_ps_ready, 1 + TC * b + c + 1)
                        nc.scalar.activation(xt_hi[:, :, c * TW:(c + 1) * TW],
                                             xt_ps[c][:, 0:KT * TW].rearrange("p (k t) -> p k t", k=KT),
                                             ACT.Copy).then_inc(xt_hi_ready, 1)
                    eng.wait_ge(q_stored, 1 + 32 * b)
                    eng.wait_ge(q_f_ready, 1 + QG * b + QG)
                    nc.scalar.activation(q_hi[:, :, :], q_f[:, :, :], ACT.Copy).then_inc(q_hi_ready, 1)

        @block.vector
        def _(eng):
            for started in (v_ready, q_f_ready, xt_ready):
                eng.sem_inc(started, 1)
            for n, j in enumerate(W_ORDER):
                if n == 1:
                    eng.wait_ge(ctx0_hi_ready, 1)
                    nc.vector.tensor_tensor(ctx_lo[0][:, :, :], ctx_raw[0][:, :, :],
                                            ctx_hi[0][:, :, :].bitcast(F32), ALU.subtract)\
                        .then_inc(ctx_ready[0], 1)
                eng.wait_ge(w_hi_ready, n + 1)
                nc.vector.tensor_tensor(w_lo[j][:, :, :], w_stage[j][:, :, :], w_hi[j][:, :, :].bitcast(F32),
                                        ALU.subtract).then_inc(w_ready, 1)
            eng.wait_ge(bias_loaded, 32)
            nc.vector.tensor_scalar(nbq[:, :], bias_col[:, 0:NG], -SCALE, None, ALU.mult).then_inc(nbq_ready, 1)
            eng.wait_ge(nbq_ready, 1)
            with eng.Fori(0, B // 2) as i:
                for p in range(2):
                    b = 2 * i + p
                    eng.wait_ge(x_loaded, 16 * (b + 1))
                    layer_norm_stats(nc, eng, x_in, stats, mv, veps, ln_step, 9 * b, passed).then_inc(veps_ready, 1)
                    eng.wait_ge(sd_ready, b + 1)
                    rsqrt_refined(nc, eng, sd, veps, rstd, nwt, ln_step, 9 * b + 4)
                    eng.wait_ge(xt_ps_ready, 1 + TC * b)
                    for c in range(TC):
                        last = nc.vector.tensor_scalar(xn[:, c, :], x_in[:, c, :], mv[:, c, 0:1],
                                                       nwt[:, 3, c:c + 1], ALU.subtract, ALU.mult)
                    last.then_inc(xn_ready, 1)
                    for g in range(NG):
                        for h in range(2):
                            eng.wait_ge(k_hi_ready, KG * b + 2 * g + h + 1)
                            nc.vector.scalar_tensor_tensor(
                                k_lo[g % 2][:, SO[h]:SO[h] + SH[h]], acc[(2 * g + h) % NACC][:, 0:SH[h]],
                                bias_col[:, NG + g:NG + g + 1],
                                k_hi[g % 2][:, SO[h]:SO[h] + SH[h]].bitcast(F32), ALU.add, ALU.subtract)\
                                .then_inc(k_ready, 1)
                    for c in range(TC):
                        eng.wait_ge(xt_hi_ready, TC * b + c + 1)
                        nc.vector.tensor_tensor(xt_lo[:, :, c * TW:(c + 1) * TW],
                                                xt_ps[c][:, 0:KT * TW].rearrange("p (k t) -> p k t", k=KT),
                                                xt_hi[:, :, c * TW:(c + 1) * TW].bitcast(F32), ALU.subtract)\
                            .then_inc(xt_ready, 1)
                    for s in range(ST):
                        eng.wait_ge(v_stored[s % 2], 1 + 16 * (3 * b + s // 2))
                        eng.wait_ge(acc_ready, 1 + AG * b + KG + s + 1)
                        nc.vector.tensor_tensor(v_out[s % 2][:, :], acc[(KG + s) % NACC][0:SW, :], bv_row[:, :],
                                                ALU.add).then_inc(v_ready, 1)
                    for j in range(QG):
                        eng.wait_ge(acc_ready, 1 + AG * b + KG + VG + j + 1)
                        for m in range(2):
                            g = 2 * j + m
                            last = nc.vector.tensor_scalar(q_f[:, g, :], acc[(KG + VG + j) % NACC][:, m * T:(m + 1) * T],
                                                           -SCALE, nbq[:, g:g + 1], ALU.mult, ALU.add)
                        last.then_inc(q_f_ready, 1)
                    eng.wait_ge(q_hi_ready, b + 1)
                    nc.vector.tensor_tensor(q_lo[:, :, :], q_f[:, :, :], q_hi[:, :, :].bitcast(F32), ALU.subtract)\
                        .then_inc(q_ready, 1)

        @block.tensor
        def _(eng):
            for started in (acc_ready, xt_ps_ready):
                eng.sem_inc(started, 1)
            eng.wait_ge(ident_ready, 1)

            def three_passes(out, w_of, x_of):
                n = 0
                for k in range(KT):
                    for a, c in ((0, 0), (0, 1), (1, 0)):
                        last = nc.tensor.matmul(out, w_of(a, k), x_of(c, k), start=(n == 0), stop=(n == 3 * KT - 1))
                        n += 1
                return last

            w_part = (w_hi, w_lo)
            eng.wait_ge(w_ready, 1)
            with eng.Fori(0, B // 2) as i:
                for p in range(2):
                    b = 2 * i + p
                    ctx_part = (ctx_hi[p], ctx_lo[p])
                    eng.wait_ge(ctx_ready[p], i + 1)
                    eng.wait_ge(v_ready, 1 + ST * b)
                    for g in range(NG):
                        for h in range(2):
                            n = 2 * g + h
                            if n == 2:
                                eng.wait_ge(q_f_ready, 1 + QG * b)
                            if n >= NACC:
                                eng.wait_ge(k_ready, KG * b + n - NACC + 1)
                            three_passes(acc[n % NACC][:, 0:SH[h]],
                                         lambda a, k: w_part[a][1][:, k, g * P:(g + 1) * P],
                                         lambda c, k: ctx_part[c][:, k, SO[h]:SO[h] + SH[h]])\
                                .then_inc(acc_ready, 1)
                    eng.wait_ge(xn_ready, b + 1)
                    eng.wait_ge(xt_ready, 1 + TC * b)
                    for c in range(TC):
                        for k in range(KT):
                            last = nc.tensor.transpose(xt_ps[c][:, k * TW:(k + 1) * TW],
                                                       xn[:, c, k * P:(k + 1) * P], ident[0:TW, 0:TW])
                        last.then_inc(xt_ps_ready, 1)
                    eng.wait_ge(w_ready, 2)
                    for s in range(ST):
                        n = KG + s
                        if s < NACC:
                            eng.wait_ge(k_ready, KG * b + n - NACC + 1)
                        else:
                            eng.wait_ge(v_ready, 1 + ST * b + s - NACC + 1)
                        three_passes(acc[n % NACC][0:SW, :],
                                     lambda c, k: ctx_part[c][:, k, s * SW:(s + 1) * SW],
                                     lambda a, k: w_part[a][2][:, k, :])\
                            .then_inc(acc_ready, 1)
                    eng.wait_ge(w_ready, 3)
                    eng.wait_ge(xt_ready, 1 + TC * b + TC)
                    for j in range(QG):
                        n = KG + VG + j
                        eng.wait_ge(v_ready, 1 + ST * b + VG + j - NACC + 1)
                        for m in range(2):
                            g = 2 * j + m
                            last = three_passes(acc[n % NACC][:, m * T:(m + 1) * T],
                                                lambda a, k: w_part[a][0][:, k, g * P:(g + 1) * P],
                                                lambda c, k: (xt_hi, xt_lo)[c][:, k, :])
                        last.then_inc(acc_ready, 1)


def attend(nc, bias, mask, q_parts, k_parts, v_all, attn_t, ident):
    with ExitStack() as ctx:
        def sb(name, shape, dt=F32):
            return ctx.enter_context(nc.sbuf_tensor(name, shape, dt))

        def sem(name):
            return ctx.enter_context(nc.semaphore(name))

        def ps(name, shape):
            return ctx.enter_context(nc.psum_tensor(name, shape, F32))

        NBLK = 3
        SCORE_AT = 512 - SH[0]
        BT = ST // 2
        GB = NG * 2
        UP = UB * 2
        NSC = 4
        neg_bias = sb("neg_bias", [TW, TC, S])
        masked_bias = [sb(f"masked_bias{p}", [TW, TC, S]) for p in range(2)]
        mask_u8 = sb("mask_u8", [TW, 2, S], U8)
        mask_keep = sb("mask_keep", [TW, S])
        mask_big = sb("mask_big", [TW, S])
        k_st = [sb(f"k_st{p}", [NBLK * D, HG, S], F32R) for p in range(2)]
        q_st = [sb(f"q_st{p}", [NBLK * D, HG, T], F32R) for p in range(2)]
        v_g = [sb(f"v_g{p}", [SW, ST, P]) for p in range(2)]
        scores = sb("scores", [TW, NSC, S])
        neg_max = sb("neg_max", [TW, UP])
        sums = sb("sums", [TW, UP])
        rsum = sb("rsum", [TW, UG])
        rsum_wide = sb("rsum_wide", [TW, TC, HG, D])
        rsum_t = sb("rsum_t", [P, T])
        probs_t = sb("probs_t", [SW, HG, ST, T])
        attn = [sb(f"attn{p}", [P, T]) for p in range(2)]
        score_ps = [ps(f"score_ps{j}", [TW, 1024]) for j in range(2)]
        prob_ps = [ps(f"prob_ps{j}", [P, 512]) for j in range(2)]
        out_ps = ps("out_ps", [P, 512])

        bias_loaded = sem("bias_loaded2")
        passed = sem("passed2")
        bias_negated = sem("bias_negated")
        mask_loaded = [sem(f"mask_loaded{p}") for p in range(2)]
        mask_step = sem("mask_step")
        masked_ready = [sem(f"masked_ready{p}") for p in range(2)]
        group_loaded = [sem(f"group_loaded{p}") for p in range(2)]
        score_ready = sem("score_ready")
        added = sem("added")
        exp_done = sem("exp_done")
        prob_ps_ready = sem("prob_ps_ready")
        prob_copied = [sem(f"prob_copied{j}") for j in range(2)]
        rsum_ready = sem("rsum_ready")
        rsum_wide_ready = sem("rsum_wide_ready")
        out_ready = sem("out_ready")
        rsum_t_ready = sem("rsum_t_ready")
        attn_ready = sem("attn_ready")
        attn_stored = [sem(f"attn_stored{p}") for p in range(2)]
        LOADS = 16 * (2 * NBLK + 1)

        block = ctx.enter_context(nc.Block())

        @block.sync
        def _(eng):
            for started in (*attn_stored,):
                eng.sem_inc(started, 1)
            def load_group(b, g):
                p = g % 2
                for j in range(NBLK):
                    rows = slice(j * D, (j + 1) * D)
                    eng.dma_start(k_st[p][rows, :, :].bitcast(F32),
                                  k_parts[b, (0, 1, 0)[j], g * P:(g + 1) * P, :].rearrange("(r d) s -> d r s", d=D))\
                       .then_inc(group_loaded[p], 16)
                    eng.dma_start(q_st[p][rows, :, :].bitcast(F32),
                                  q_parts[b, (0, 0, 1)[j], g * P:(g + 1) * P, :].rearrange("(r d) t -> d r t", d=D))\
                       .then_inc(group_loaded[p], 16)
                eng.dma_start(v_g[p][:, :, :],
                              v_all[b, :, g * P:(g + 1) * P].rearrange("(s p) d -> p s d", p=SW))\
                   .then_inc(group_loaded[p], 16)

            def pair(i, more):
                for n in range(GB):
                    b, g = 2 * i + n // NG, n % NG
                    if n + 2 < GB or more:
                        eng.wait_ge(out_ready, 1 + GB * i + n + 1)
                        load_group(2 * i + (n + 2) // NG, (n + 2) % NG)
                    eng.wait_ge(attn_ready, 1 + GB * i + n + 1)
                    eng.dma_start(attn_t[b, g * P:(g + 1) * P, :], attn[n % 2][:, :])\
                       .then_inc(attn_stored[n % 2], 16)

            eng.dma_start(neg_bias[:, :, :], bias.rearrange("(c t) s -> t c s", c=TC)).then_inc(bias_loaded, 16)
            load_group(0, 0)
            load_group(0, 1)
            with eng.Fori(0, B // 2 - 1) as i:
                pair(i, True)
            pair(B // 2 - 1, False)
            for p in range(2):
                eng.wait_ge(attn_stored[p], 1 + 16 * B * NG // 2)

        @block.gpsimd
        def _(eng):
            for started in (*masked_ready, rsum_wide_ready):
                eng.sem_inc(started, 1)
            def load_mask(b, p):
                eng.dma_start(mask_u8[:, p, :], mask[b].partition_broadcast(TW)).then_inc(mask_loaded[p], 16)

            def masked(i, p):
                n = 4 * (2 * i + p)
                eng.wait_ge(masked_ready[1 - p], 1 + i + p)
                eng.wait_ge(mask_loaded[p], 16 * (i + 1))
                apart(eng, passed)
                eng.tensor_scalar(mask_keep[:, :], mask_u8[:, p, :], -1.0, 1.0, ALU.mult, ALU.add)\
                   .then_inc(mask_step, 1)
                eng.tensor_scalar(mask_big[:, :], mask_u8[:, p, :], FMAX, 0.0, ALU.mult, ALU.add)\
                   .then_inc(mask_step, 1)
                eng.wait_ge(mask_step, n + 2)
                for c in range(TC):
                    eng.tensor_tensor(masked_bias[p][:, c, :], neg_bias[:, c, :], mask_keep[:, :], ALU.mult)\
                       .then_inc(mask_step, 1)
                for c in range(TC):
                    eng.wait_ge(mask_step, n + 3 + c)
                    last = eng.tensor_tensor(masked_bias[p][:, c, :], masked_bias[p][:, c, :], mask_big[:, :],
                                             ALU.add)
                last.then_inc(masked_ready[p], 1)

            def widen(i, n):
                eng.wait_ge(rsum_ready, GB * i + n + 1)
                eng.wait_ge(out_ready, 1 + GB * i + n)
                apart(eng, passed)
                eng.tensor_copy(rsum_wide[:, :, :, :],
                                rsum[:, :].rearrange("t (r c) -> t c r", c=TC).unsqueeze(3)
                                .broadcast_to([TW, TC, HG, D])).then_inc(rsum_wide_ready, 1)

            load_mask(0, 0)
            load_mask(1, 1)
            eng.wait_ge(bias_negated, 1)
            for p in range(2):
                masked(0, p)

            def pair(i, more):
                for n in range(GB):
                    widen(i, n)
                    if n == NG + 2 and more:
                        load_mask(2 * i + 2, 0)
                        load_mask(2 * i + 3, 1)
                        masked(i + 1, 0)
                if more:
                    eng.wait_ge(added, 1 + UP * (i + 1))
                    masked(i + 1, 1)

            with eng.Fori(0, B // 2 - 1) as i:
                pair(i, True)
            pair(B // 2 - 1, False)

        @block.scalar
        def _(eng):
            for started in (prob_copied[1],):
                eng.sem_inc(started, 1)
            with eng.Fori(0, B // 2) as i:
                def exp(w):
                    eng.wait_ge(added, 1 + UP * i + w + 1)
                    nc.scalar.activation(scores[:, w % NSC, :], scores[:, w % NSC, :], ACT.Exp,
                                         bias=neg_max[:, w:w + 1], scale=-1.0,
                                         accum_out=sums[:, w:w + 1]).then_inc(exp_done, 1)

                exp(0)
                exp(1)
                for w in range(UP):
                    if w + 2 < UP:
                        exp(w + 2)
                    n, h, c = w // UG, w // TC % HG, w % TC
                    if w % UG == 0:
                        eng.wait_ge(out_ready, 1 + GB * i + n)
                    eng.wait_ge(prob_ps_ready, 1 + 2 * (UP * i + w) + 2)
                    nc.scalar.activation(probs_t[:, h, BT:ST, c * TW:(c + 1) * TW],
                                         prob_ps[1][0:SW, 0:BT * TW].rearrange("p (s t) -> p s t", s=BT),
                                         ACT.Copy).then_inc(prob_copied[1], 1)
                    if w % UG == UG - 1:
                        eng.wait_ge(out_ready, 1 + GB * i + n + 1)
                        nc.scalar.activation(rsum_t[:, :], out_ps[:, 256:256 + T], ACT.Copy)\
                            .then_inc(rsum_t_ready, 1)

        @block.vector
        def _(eng):
            for started in (added, prob_copied[0], attn_ready):
                eng.sem_inc(started, 1)
            eng.wait_ge(bias_loaded, 16)
            nc.vector.tensor_scalar(neg_bias[:, :, :], neg_bias[:, :, :], -1.0, FMAX, ALU.mult, ALU.min)\
                .then_inc(bias_negated, 1)
            with eng.Fori(0, B // 2) as i:
                def add(w):
                    p, c = w // UB, w % TC
                    if w % UB == 0:
                        eng.wait_ge(masked_ready[p], 1 + i + 1)
                    eng.wait_ge(prob_ps_ready, 1 + 2 * (UP * i + max(0, w - NSC + 1)))
                    eng.wait_ge(score_ready, UP * i + w + 1)
                    apart(eng, passed)
                    nc.vector.tensor_tensor_reduce(
                        out=scores[:, w % NSC, :], in0=score_ps[w % 2][:, SCORE_AT:SCORE_AT + S],
                        in1=masked_bias[p][:, c, :],
                        scale=1.0, scalar=FMAX, op0=ALU.add, op1=ALU.min,
                        accum_out=neg_max[:, w:w + 1]).then_inc(added, 1)

                add(0)
                add(1)
                for w in range(UP):
                    n, h, c = w // UG, w // TC % HG, w % TC
                    if w + 2 < UP:
                        add(w + 2)
                    if w % UG == 0:
                        eng.wait_ge(out_ready, 1 + GB * i + n)
                    eng.wait_ge(prob_ps_ready, 1 + 2 * (UP * i + w) + 1)
                    nc.vector.tensor_copy(probs_t[:, h, 0:BT, c * TW:(c + 1) * TW],
                                          prob_ps[0][0:SW, 0:BT * TW].rearrange("p (s t) -> p s t", s=BT))\
                        .then_inc(prob_copied[0], 1)
                    if w % UG == UG - 2:
                        eng.wait_ge(exp_done, UP * i + w + 2)
                        eng.wait_ge(rsum_wide_ready, 1 + GB * i + n)
                        nc.vector.reciprocal(rsum[:, :], sums[:, n * UG:(n + 1) * UG]).then_inc(rsum_ready, 1)
                    if w % UG == UG - 1:
                        eng.wait_ge(rsum_t_ready, GB * i + n + 1)
                        eng.wait_ge(attn_stored[n % 2], 1 + 16 * (NG * i + n // 2))
                        nc.vector.tensor_tensor(attn[n % 2][:, :], out_ps[:, 0:T], rsum_t[:, :], ALU.mult)\
                            .then_inc(attn_ready, 1)

        @block.tensor
        def _(eng):
            for started in (out_ready, prob_ps_ready):
                eng.sem_inc(started, 1)
            with eng.Fori(0, B // 2) as i:
                def score(w):
                    n, h, c = w // UG, w // TC % HG, w % TC
                    p = n % 2
                    if w % UG == 0:
                        eng.wait_ge(group_loaded[p], LOADS * (NG * i + n // 2 + 1))
                    eng.wait_ge(added, 1 + UP * i + max(0, w - 1))
                    for half in range(2):
                        at = SCORE_AT + SO[half]
                        last = nc.tensor.matmul(score_ps[w % 2][:, at:at + SH[half]],
                                                q_st[p][:, h, c * TW:(c + 1) * TW],
                                                k_st[p][:, h, SO[half]:SO[half] + SH[half]], start=True, stop=True)
                    last.then_inc(score_ready, 1)

                score(0)
                score(1)
                for w in range(UP):
                    n = w // UG
                    if w + 2 < UP:
                        score(w + 2)
                    eng.wait_ge(exp_done, UP * i + w + 1)
                    for j in range(2):
                        eng.wait_ge(prob_copied[j], 1 + UP * i + w)
                        for s in range(BT):
                            last = nc.tensor.transpose(prob_ps[j][0:SW, s * TW:(s + 1) * TW],
                                                       scores[:, w % NSC, (BT * j + s) * SW:(BT * j + s + 1) * SW],
                                                       ident[0:TW, 0:TW])
                        last.then_inc(prob_ps_ready, 1)
                    if w % UG == UG - 1:
                        eng.wait_ge(attn_ready, 1 + GB * i + n)
                        for j in range(2):
                            eng.wait_ge(prob_copied[j], 1 + UP * i + w + 1)
                            for s in range(BT * j, BT * (j + 1)):
                                for h in range(HG):
                                    nc.tensor.matmul(out_ps[h * D:(h + 1) * D, 0:T],
                                                     v_g[n % 2][:, s, h * D:(h + 1) * D], probs_t[:, h, s, :],
                                                     start=(s == 0), stop=(s == ST - 1))
                        eng.wait_ge(rsum_wide_ready, 1 + GB * i + n + 1)
                        for c in range(TC):
                            last = nc.tensor.transpose(out_ps[:, 256 + c * TW:256 + (c + 1) * TW],
                                                       rsum_wide[:, c, :, :].rearrange("t r d -> t (r d)"),
                                                       ident[0:TW, 0:TW])
                        last.then_inc(out_ready, 1)


def finish(nc, x, attn_t, w_out_t, b_out, protos, protos_t, fb_t, fa_t, f_bias, temp, out, ident):
    with ExitStack() as ctx:
        def sb(name, shape, dt=F32):
            return ctx.enter_context(nc.sbuf_tensor(name, shape, dt))

        def sem(name):
            return ctx.enter_context(nc.semaphore(name))

        def ps(name, shape):
            return ctx.enter_context(nc.psum_tensor(name, shape, F32))

        PM = P // RK
        MT = NP // PM
        W_NAMES = ("out", "fb", "fa")
        w_stage = [sb(f"stage_{n}", [P, KT, E]) for n in W_NAMES]
        w_hi = [sb(f"hi_{n}", [P, KT, E], F32R) for n in W_NAMES]
        w_lo = [sb(f"lo_{n}", [P, KT, E], F32R) for n in W_NAMES]
        pt_stage = sb("pt_stage", [P, KT, NP])
        pt_hi = sb("pt_hi", [P, KT, NP], F32R)
        pt_lo = sb("pt_lo", [P, KT, NP], F32R)
        protos_sb = sb("protos_sb", [NP, E])
        squares = sb("squares", [TW, E])
        p2 = sb("p2", [NP, 1])
        bst_raw = sb("bst_raw", [P, E])
        bst_hi = sb("bst_hi", [P, E], F32R)
        bst = sb("bst", [P, E], F32R)
        bo_row = sb("bo_row", [TW, E])
        temp_col = sb("temp_col", [TW, 1])
        t_neg = sb("t_neg", [TW, 1])
        t_abs = sb("t_abs", [TW, 1])
        inv_t = sb("inv_t", [TW, 1])
        iota = sb("iota", [TW, NP])
        at_in = sb("at_in", [P, NG, T])
        at_hi = sb("at_hi", [P, NG, T], F32R)
        at_lo = sb("at_lo", [P, NG, T], F32R)
        x_res = sb("x_res", [TW, TC, E])
        xb = sb("xb", [TW, TC, E])
        x1 = sb("x1", [TW, B, TC, E])
        y2 = sb("y2", [TW, TC, E])
        yt_hi = sb("yt_hi", [P, KT, T], F32R)
        yt_lo = sb("yt_lo", [P, KT, T], F32R)
        stats = sb("stats2", [TW, TC, 6])
        mv = sb("mv2", [TW, TC, 2])
        veps = sb("veps2", [TW, TC])
        sd = sb("sd2", [TW, TC])
        rstd = sb("rstd2", [TW, TC])
        nwt = sb("nwt2", [TW, 4, TC])
        x2 = sb("x2", [TW, TC])
        dot = sb("dot", [NP, T])
        d2 = sb("d2", [TW, TC, NP])
        dist = sb("dist", [TW, TC, NP])
        near = sb("near", [TW, TC, NP])
        top = sb("top", [TW, TC, 8])
        top_at = sb("top_at", [TW, TC, 8], mybir.dt.uint32)
        top_f = sb("top_f", [TW, TC, 2])
        gap = sb("gap", [TW, TC])
        ez = sb("ez", [TW, TC])
        ez1 = sb("ez1", [TW, TC])
        wt = sb("wt", [TW, 2, TC])
        pick = sb("pick", [TW, 2, TC, NP])
        route = sb("route", [TW, TC, NP])
        route_st = sb("route_st", [TW, TC, 4, NP], F32R)
        route_wide = sb("route_wide", [TW, TC, NP, RK])
        route_t = sb("route_t", [P, T], F32R)
        h_sb = sb("h_sb", [P, MT, T])
        gated = sb("gated", [P, MT, T])
        g_hi = sb("g_hi", [P, MT, T], F32R)
        g_lo = sb("g_lo", [P, MT, T], F32R)
        y_out = [sb(f"y_out{c}", [TW, E]) for c in range(TC)]
        big = [ps(f"big{c}", [P, 512]) for c in range(TC)]
        tr = [ps(f"tr{c}", [P, 512]) for c in range(TC)]
        dot_ps = ps("dot_ps", [P, 512])
        route_ps = ps("route_ps", [P, 512])
        h_ps = [ps(f"h_ps{j}", [P, 512]) for j in range(2)]

        loaded = [sem(f"loaded_{n}") for n in W_NAMES]
        small_loaded = sem("small_loaded")
        w_hi_ready = sem("w_hi_ready3")
        w_ready = sem("w_ready3")
        small_step = sem("small_step")
        small_ready = sem("small_ready")
        p2_ready = sem("p2_ready")
        passed = sem("passed3")
        iota_ready = sem("iota_ready")
        at_loaded = sem("at_loaded")
        xr_loaded = sem("xr_loaded")
        at_hi_ready = sem("at_hi_ready")
        at_ready = sem("at_ready")
        xb_ready = sem("xb_ready")
        o_ready = sem("o_ready")
        x1_ready = sem("x1_ready")
        ln_step = sem("ln_step3")
        veps_ready = sem("veps_ready3")
        sd_ready = sem("sd_ready3")
        y2_ready = sem("y2_ready")
        x2_ready = sem("x2_ready")
        yt_ps_ready = sem("yt_ps_ready")
        yt_hi_ready = sem("yt_hi_ready")
        yt_ready = sem("yt_ready")
        dot_ps_ready = sem("dot_ps_ready")
        dot_ready = sem("dot_ready")
        dot_t_ready = sem("dot_t_ready")
        d2_ready = sem("d2_ready")
        dist_ready = sem("dist_ready")
        top_step = sem("top_step")
        gap_ready = sem("gap_ready")
        ez_ready = sem("ez_ready")
        route_ready = sem("route_ready")
        route_st_ready = sem("route_st_ready")
        wide_ready = sem("wide_ready")
        route_ps_ready = sem("route_ps_ready")
        route_t_ready = sem("route_t_ready")
        wide_ps_ready = sem("wide_ps_ready")
        h_ps_ready = sem("h_ps_ready")
        h_ready = sem("h_ready")
        gated_ready = sem("gated_ready")
        g_hi_ready = sem("g_hi_ready")
        g_ready = sem("g_ready")
        y_ps_ready = sem("y_ps_ready")
        y_ready = sem("y_ready")
        y_stored = [sem(f"y_stored{c}") for c in range(TC)]
        TOPS = 10
        LAST = B - 1

        block = ctx.enter_context(nc.Block())

        @block.sync
        def _(eng):
            for started in (*y_stored,):
                eng.sem_inc(started, 1)
            def load(b):
                eng.dma_start(at_in[:, :, :], attn_t[b].rearrange("(g p) t -> p g t", p=P)).then_inc(at_loaded, 16)
                eng.dma_start(x_res[:, :, :], x[b].rearrange("(c t) e -> t c e", c=TC)).then_inc(xr_loaded, 16)

            def store(b):
                for c in range(TC):
                    eng.wait_ge(y_ready, 1 + TC * b + c + 1)
                    eng.dma_start(out[b, c * TW:(c + 1) * TW, :], y_out[c][:, :]).then_inc(y_stored[c], 16)

            load(0)
            for j, w in enumerate((w_out_t, fb_t, fa_t)):
                eng.dma_start(w_stage[j][:, :, :], w.rearrange("(k p) o -> p k o", p=P)).then_inc(loaded[j], 16)
                if j == 0:
                    eng.dma_start(bo_row[:, :], b_out.partition_broadcast(TW)).then_inc(small_loaded, 16)
                    eng.dma_start(pt_stage[:, :, :], protos_t.rearrange("(k p) n -> p k n", p=P))\
                       .then_inc(small_loaded, 16)
                    eng.dma_start(protos_sb[:, :], protos).then_inc(small_loaded, 16)
                    for r in range(4):
                        eng.dma_start(bst_raw[r * NP:(r + 1) * NP, :], f_bias).then_inc(small_loaded, 16)
                    eng.dma_start(temp_col[:, :], temp.partition_broadcast(TW)).then_inc(small_loaded, 16)
            with eng.Fori(0, LAST) as b:
                eng.wait_ge(xb_ready, b + 1)
                load(b + 1)
                store(b)
            store(LAST)
            for c in range(TC):
                eng.wait_ge(y_stored[c], 1 + 16 * B)

        @block.gpsimd
        def _(eng):
            eng.iota(iota[:, :], [[1, NP]], 0, 0, allow_small_or_imprecise_dtypes=True).then_inc(iota_ready, 1)
            eng.wait_ge(small_loaded, 16 * 8)
            with eng.Fori(0, B) as b:
                eng.wait_ge(at_loaded, 16 * (b + 1))
                eng.wait_ge(o_ready, 1 + TC * b)
                apart(eng, passed)
                eng.tensor_scalar(at_hi[:, :, :], at_in[:, :, :], 1.0, 0.0, ALU.mult, ALU.add)\
                   .then_inc(at_hi_ready, 1)
                eng.wait_ge(at_hi_ready, b + 1)
                eng.tensor_tensor(at_lo[:, :, :], at_in[:, :, :], at_hi[:, :, :].bitcast(F32), ALU.subtract)\
                   .then_inc(at_ready, 1)
                eng.wait_ge(xr_loaded, 16 * (b + 1))
                eng.wait_ge(x1_ready, 1 + TC * b)
                for c in range(TC):
                    last = eng.tensor_tensor(xb[:, c, :], x_res[:, c, :], bo_row[:, :], ALU.add)
                last.then_inc(xb_ready, 1)

        @block.scalar
        def _(eng):
            for started in (wide_ready, g_hi_ready, x2_ready):
                eng.sem_inc(started, 1)
            for j in range(3):
                eng.wait_ge(loaded[j], 16)
                nc.scalar.activation(w_hi[j][:, :, :], w_stage[j][:, :, :], ACT.Copy).then_inc(w_hi_ready, 1)
                if j == 0:
                    eng.wait_ge(small_loaded, 16 * 8)
                    nc.scalar.activation(pt_hi[:, :, :], pt_stage[:, :, :], ACT.Copy).then_inc(small_step, 1)
                    nc.scalar.activation(bst_hi[:, :], bst_raw[:, :], ACT.Copy).then_inc(small_step, 1)
                    nc.scalar.activation(squares[0:NP, :], protos_sb[:, :], ACT.Square,
                                         accum_out=p2[:, :]).then_inc(p2_ready, 1)
                    eng.wait_ge(p2_ready, 1)

            def norm(b):
                eng.wait_ge(veps_ready, b + 1)
                nc.scalar.activation(sd[:, :], veps[:, :], ACT.Sqrt).then_inc(sd_ready, 1)
                eng.wait_ge(y2_ready, b + 1)
                for c in range(TC):
                    if c == 0:
                        eng.wait_ge(x2_ready, 1 + TC * b)
                    else:
                        eng.wait_ge(x2_ready, 1 + TC * b + 1)
                    nc.scalar.activation(squares[:, :], y2[:, c, :], ACT.Square,
                                         accum_out=x2[:, c:c + 1]).then_inc(x2_ready, 1)
                for c in range(TC):
                    eng.wait_ge(yt_ps_ready, TC * b + c + 1)
                    nc.scalar.activation(yt_hi[:, :, c * TW:(c + 1) * TW],
                                         tr[c][:, 0:KT * TW].rearrange("p (k t) -> p k t", k=KT),
                                         ACT.Copy).then_inc(yt_hi_ready, 1)

            def route_part(b):
                def copy_h(j):
                    eng.wait_ge(h_ps_ready, 2 * b + j + 1)
                    nc.scalar.activation(h_sb[:, 2 * j:2 * j + 2, :],
                                         h_ps[j][:, 0:2 * T].rearrange("p (m t) -> p m t", m=2),
                                         ACT.Copy).then_inc(h_ready, 1)

                copy_h(0)
                eng.wait_ge(d2_ready, b + 1)
                nc.scalar.activation(dist[:, :, :], d2[:, :, :], ACT.Sqrt).then_inc(dist_ready, 1)
                copy_h(1)
                eng.wait_ge(gap_ready, b + 1)
                nc.scalar.activation(ez[:, :], gap[:, :], ACT.Exp, scale=inv_t[:, 0:1]).then_inc(ez_ready, 1)
                eng.wait_ge(route_ready, b + 1)
                nc.scalar.activation(route_wide[:, :, :, :],
                                     route[:, :, :].unsqueeze(3).broadcast_to([TW, TC, NP, RK]),
                                     ACT.Copy).then_inc(wide_ready, 1)

            def experts(b):
                eng.wait_ge(route_ps_ready, 1 + b + 1)
                nc.scalar.activation(route_t[:, :], route_ps[:, 0:T], ACT.Copy).then_inc(route_t_ready, 1)
                eng.wait_ge(gated_ready, b + 1)
                nc.scalar.activation(g_hi[:, :, :], gated[:, :, :], ACT.Copy).then_inc(g_hi_ready, 1)

            eng.wait_ge(small_ready, 1)
            norm(0)
            route_part(0)
            with eng.Fori(0, LAST) as b:
                experts(b)
                norm(b + 1)
                route_part(b + 1)
            experts(LAST)

        @block.vector
        def _(eng):
            for started in (x1_ready, y_ready):
                eng.sem_inc(started, 1)
            for j in range(3):
                eng.wait_ge(w_hi_ready, j + 1)
                nc.vector.tensor_tensor(w_lo[j][:, :, :], w_stage[j][:, :, :], w_hi[j][:, :, :].bitcast(F32),
                                        ALU.subtract).then_inc(w_ready, 1)
                if j == 0:
                    eng.wait_ge(small_step, 2)
                    nc.vector.tensor_tensor(pt_lo[:, :, :], pt_stage[:, :, :], pt_hi[:, :, :].bitcast(F32),
                                            ALU.subtract)
                    for r in range(4):
                        rows = slice(r * NP, (r + 1) * NP)
                        if r % 2 == 0:
                            nc.vector.tensor_copy(bst[rows, :], bst_hi[rows, :].bitcast(F32))
                        else:
                            nc.vector.tensor_tensor(bst[rows, :], bst_raw[rows, :], bst_hi[rows, :].bitcast(F32),
                                                    ALU.subtract)
                    nc.vector.tensor_scalar(t_neg[:, :], temp_col[:, :], -1.0, 0.1, ALU.mult, ALU.max)\
                        .then_inc(small_step, 1)
                    eng.wait_ge(small_step, 3)
                    nc.vector.tensor_tensor(t_abs[:, :], temp_col[:, :], t_neg[:, :], ALU.max)\
                        .then_inc(small_step, 1)
                    eng.wait_ge(small_step, 4)
                    nc.vector.reciprocal(inv_t[:, :], t_abs[:, :]).then_inc(small_ready, 1)
            eng.wait_ge(p2_ready, 1)
            eng.wait_ge(iota_ready, 1)

            def residual(b, c):
                if c == 0:
                    eng.wait_ge(xb_ready, b + 1)
                eng.wait_ge(o_ready, 1 + TC * b + c + 1)
                nc.vector.tensor_tensor(x1_of(b)[:, c, :], big[c][0:TW, :], xb[:, c, :], ALU.add)\
                    .then_inc(x1_ready, 1)

            def x1_of(b):
                return x1[:, bass.DynSlice(b, 1), :, :].rearrange("t b c e -> t (b c) e")

            def norm(b):
                eng.wait_ge(x1_ready, 1 + TC * (b + 1))
                layer_norm_stats(nc, eng, x1_of(b), stats, mv, veps, ln_step, 9 * b, passed)\
                    .then_inc(veps_ready, 1)

            def normalise(b):
                eng.wait_ge(sd_ready, b + 1)
                rsqrt_refined(nc, eng, sd, veps, rstd, nwt, ln_step, 9 * b + 4)
                for c in range(TC):
                    last = nc.vector.tensor_scalar(y2[:, c, :], x1_of(b)[:, c, :], mv[:, c, 0:1],
                                                   nwt[:, 3, c:c + 1], ALU.subtract, ALU.mult)
                last.then_inc(y2_ready, 1)

            def yt_low(b):
                for c in range(TC):
                    eng.wait_ge(yt_hi_ready, TC * b + c + 1)
                    nc.vector.tensor_tensor(yt_lo[:, :, c * TW:(c + 1) * TW],
                                            tr[c][:, 0:KT * TW].rearrange("p (k t) -> p k t", k=KT),
                                            yt_hi[:, :, c * TW:(c + 1) * TW].bitcast(F32), ALU.subtract)\
                        .then_inc(yt_ready, 1)

            def routing(b):
                n = TOPS * b
                eng.wait_ge(dot_ps_ready, b + 1)
                nc.vector.tensor_scalar(dot[:, :], dot_ps[0:NP, 0:T], -2.0, p2[:, 0:1], ALU.mult, ALU.add)\
                    .then_inc(dot_ready, 1)
                eng.wait_ge(dot_t_ready, b + 1)
                eng.wait_ge(x2_ready, 1 + TC * (b + 1))
                for c in range(TC):
                    last = nc.vector.tensor_scalar(d2[:, c, :], dot_ps[0:TW, 256 + c * NP:256 + (c + 1) * NP],
                                                   x2[:, c:c + 1], 0.0, ALU.add, ALU.max)
                last.then_inc(d2_ready, 1)
                eng.wait_ge(dist_ready, b + 1)
                nc.vector.tensor_scalar(near[:, :, :], dist[:, :, :], -1.0, None, ALU.mult).then_inc(top_step, 1)
                eng.wait_ge(top_step, n + 1)
                apart(eng, passed)
                for c in range(TC):
                    nc.vector.max(top[:, c, :], near[:, c, :]).then_inc(top_step, 1)
                eng.wait_ge(top_step, n + 3)
                nc.vector.tensor_tensor(gap[:, :], top[:, :, 1], top[:, :, 0], ALU.subtract).then_inc(gap_ready, 1)
                for c in range(TC):
                    nc.vector.max_index(top_at[:, c, :], top[:, c, :], near[:, c, :]).then_inc(top_step, 1)
                eng.wait_ge(top_step, n + 5)
                nc.vector.tensor_copy(top_f[:, :, :], top_at[:, :, 0:2]).then_inc(top_step, 1)
                eng.wait_ge(ez_ready, b + 1)
                nc.vector.tensor_scalar(ez1[:, :], ez[:, :], 1.0, None, ALU.add).then_inc(top_step, 1)
                eng.wait_ge(top_step, n + 7)
                nc.vector.reciprocal(wt[:, 0, :], ez1[:, :]).then_inc(top_step, 1)
                eng.wait_ge(top_step, n + 8)
                nc.vector.tensor_tensor(wt[:, 1, :], wt[:, 0, :], ez[:, :], ALU.mult).then_inc(top_step, 1)
                eng.wait_ge(top_step, n + 9)
                for j in range(2):
                    for c in range(TC):
                        last = nc.vector.tensor_scalar(pick[:, j, c, :], iota[:, :], top_f[:, c, j:j + 1],
                                                       wt[:, j, c:c + 1], ALU.is_equal, ALU.mult)
                last.then_inc(top_step, 1)
                eng.wait_ge(top_step, n + 10)
                eng.wait_ge(wide_ready, 1 + b)
                nc.vector.tensor_tensor(route[:, :, :], pick[:, 0, :, :], pick[:, 1, :, :], ALU.add)\
                    .then_inc(route_ready, 1)
                eng.wait_ge(route_ready, b + 1)
                eng.wait_ge(route_ps_ready, 1 + b)
                two = [TW, TC, 2, NP]
                nc.vector.tensor_copy(route_st[:, :, 0:2, :], route[:, :, :].unsqueeze(2).broadcast_to(two))\
                    .then_inc(route_st_ready, 1)
                eng.wait_ge(route_st_ready, 2 * b + 1)
                nc.vector.tensor_tensor(route_st[:, :, 2:4, :], route[:, :, :].unsqueeze(2).broadcast_to(two),
                                        route_st[:, :, 0:2, :].bitcast(F32), ALU.subtract)\
                    .then_inc(route_st_ready, 1)

            def gate(b):
                eng.wait_ge(h_ready, 2 * b + 2)
                eng.wait_ge(g_hi_ready, 1 + b)
                for c in range(TC):
                    eng.wait_ge(wide_ps_ready, TC * b + c + 1)
                    last = nc.vector.tensor_tensor(gated[:, :, c * TW:(c + 1) * TW],
                                                   tr[c][:, 0:MT * TW].rearrange("p (m t) -> p m t", m=MT),
                                                   h_sb[:, :, c * TW:(c + 1) * TW], ALU.mult)
                last.then_inc(gated_ready, 1)

            def gated_low(b):
                eng.wait_ge(g_hi_ready, 1 + b + 1)
                nc.vector.tensor_tensor(g_lo[:, :, :], gated[:, :, :], g_hi[:, :, :].bitcast(F32), ALU.subtract)\
                    .then_inc(g_ready, 1)

            def result(b, c):
                eng.wait_ge(y_ps_ready, TC * b + c + 1)
                eng.wait_ge(y_stored[c], 1 + 16 * b)
                nc.vector.tensor_tensor(y_out[c][:, :], big[c][0:TW, :], x1_of(b)[:, c, :], ALU.add)\
                    .then_inc(y_ready, 1)

            residual(0, 0)
            residual(0, 1)
            norm(0)
            normalise(0)
            yt_low(0)
            routing(0)
            with eng.Fori(0, LAST) as b:
                residual(b + 1, 0)
                gate(b)
                residual(b + 1, 1)
                norm(b + 1)
                gated_low(b)
                normalise(b + 1)
                result(b, 0)
                yt_low(b + 1)
                result(b, 1)
                routing(b + 1)
            gate(LAST)
            gated_low(LAST)
            result(LAST, 0)
            result(LAST, 1)

        @block.tensor
        def _(eng):
            for started in (o_ready, route_ps_ready):
                eng.sem_inc(started, 1)
            def three_passes(out_ap, left, right, tiles, first=True, last=True):
                n = 0
                for k in range(tiles):
                    for a, c in ((0, 0), (0, 1), (1, 0)):
                        ins = nc.tensor.matmul(out_ap, left(a, k), right(c, k), start=(first and n == 0),
                                               stop=(last and n == 3 * tiles - 1))
                        n += 1
                return ins

            def w_of(j):
                return lambda a, k: (w_hi, w_lo)[a][j][:, k, :]

            def project_out(b, c):
                if c == 0:
                    eng.wait_ge(at_ready, b + 1)
                three_passes(big[c][0:TW, :], lambda a, k: (at_hi, at_lo)[a][:, k, c * TW:(c + 1) * TW], w_of(0), NG)\
                    .then_inc(o_ready, 1)

            def transpose_y(b):
                eng.wait_ge(y2_ready, b + 1)
                for c in range(TC):
                    for k in range(KT):
                        last = nc.tensor.transpose(tr[c][:, k * TW:(k + 1) * TW], y2[:, c, k * P:(k + 1) * P],
                                                   ident[0:TW, 0:TW])
                    last.then_inc(yt_ps_ready, 1)

            def distances(b):
                eng.wait_ge(yt_ready, TC * (b + 1))
                three_passes(dot_ps[0:NP, 0:T], lambda a, k: (pt_hi, pt_lo)[a][:, k, :],
                             lambda c, k: (yt_hi, yt_lo)[c][:, k, :], KT).then_inc(dot_ps_ready, 1)

            def down(b, j):
                for m in range(2):
                    tile = 2 * j + m
                    last = three_passes(h_ps[j][:, m * T:(m + 1) * T],
                                        lambda a, k: (w_hi, w_lo)[a][1][:, k, tile * P:(tile + 1) * P],
                                        lambda c, k: (yt_hi, yt_lo)[c][:, k, :], KT)
                last.then_inc(h_ps_ready, 1)

            def transpose_dot(b):
                eng.wait_ge(dot_ready, b + 1)
                apart(eng, passed)
                for c in range(TC):
                    last = nc.tensor.transpose(dot_ps[0:TW, 256 + c * NP:256 + (c + 1) * NP],
                                               dot[:, c * TW:(c + 1) * TW], ident[0:NP, 0:NP])
                last.then_inc(dot_t_ready, 1)

            def transpose_routes(b):
                eng.wait_ge(wide_ready, 1 + b + 1)
                for c in range(TC):
                    for m in range(MT):
                        last = nc.tensor.transpose(
                            tr[c][:, m * TW:(m + 1) * TW],
                            route_wide[:, c, m * PM:(m + 1) * PM, :].rearrange("t n r -> t (n r)"),
                            ident[0:TW, 0:TW])
                    last.then_inc(wide_ps_ready, 1)
                eng.wait_ge(route_st_ready, 2 * b + 2)
                for c in range(TC):
                    last = nc.tensor.transpose(route_ps[:, c * TW:(c + 1) * TW],
                                               route_st[:, c, :, :].rearrange("t r n -> t (r n)").bitcast(F32),
                                               ident[0:TW, 0:TW])
                last.then_inc(route_ps_ready, 1)

            def up(b, c, more):
                if more:
                    eng.wait_ge(x1_ready, 1 + TC * (b + 1) + c + 1)
                if c == 0:
                    eng.wait_ge(route_t_ready, b + 1)
                    eng.wait_ge(g_ready, b + 1)
                three_passes(big[c][0:TW, :], lambda a, k: (g_hi, g_lo)[a][:, k, c * TW:(c + 1) * TW],
                             w_of(2), MT, last=False)
                nc.tensor.matmul(big[c][0:TW, :], route_t[:, c * TW:(c + 1) * TW], bst[:, :],
                                 start=False, stop=True).then_inc(y_ps_ready, 1)

            def second_half(b):
                distances(b)
                if b is not zero:
                    eng.wait_ge(h_ready, 2 * b - 1)
                down(b, 0)
                transpose_dot(b)
                if b is not zero:
                    eng.wait_ge(h_ready, 2 * b)
                down(b, 1)

            zero = 0
            eng.wait_ge(w_ready, 1)
            project_out(zero, 0)
            project_out(zero, 1)
            transpose_y(zero)
            eng.wait_ge(small_ready, 1)
            eng.wait_ge(w_ready, 2)
            second_half(zero)
            eng.wait_ge(w_ready, 3)
            with eng.Fori(0, LAST) as b:
                eng.wait_ge(y_ready, 1 + TC * b)
                project_out(b + 1, 0)
                transpose_routes(b)
                project_out(b + 1, 1)
                up(b, 0, True)
                eng.wait_ge(gated_ready, b + 1)
                transpose_y(b + 1)
                up(b, 1, True)
                second_half(b + 1)
            transpose_routes(LAST)
            up(LAST, 0, False)
            up(LAST, 1, False)


def build(nc, x, ctx_t, bias, mask, w_in_t, b_in, bv, w_out_t, b_out, protos, protos_t, fb_t, fa_t, f_bias, temp,
          out):
    q_parts = nc.dram_tensor("q_parts", [B, 2, E, T], F32, kind="Internal").ap()
    k_parts = nc.dram_tensor("k_parts", [B, 2, E, S], F32, kind="Internal").ap()
    v_all = nc.dram_tensor("v_all", [B, S, E], F32, kind="Internal").ap()
    attn_t = nc.dram_tensor("attn_t", [B, E, T], F32, kind="Internal").ap()
    with nc.sbuf_tensor("ident", [P, P], F32) as ident:
        project(nc, x, ctx_t, w_in_t, b_in, bv, q_parts, k_parts, v_all, ident)
        attend(nc, bias, mask, q_parts, k_parts, v_all, attn_t, ident)
        finish(nc, x, attn_t, w_out_t, b_out, protos, protos_t, fb_t, fa_t, f_bias, temp, out, ident)


def kernel(**inputs):
    import concourse.bacc as bacc
    from concourse.bass_utils import run_bass_kernel_spmd

    w_in, b_in = inputs["L0_xattn_in_proj_w"], inputs["L0_xattn_in_proj_b"]
    fa, fb = inputs["L0_ffn_A"], inputs["L0_ffn_B"]
    laid = {
        "x": inputs["x"],
        "ctx_t": inputs["ctx_1024"].transpose(0, 2, 1),
        "bias": inputs["fside_1xSxS2_0"].reshape(T, S),
        "mask": inputs["mask_BxS2_bk0"],
        "w_in_t": w_in.T,
        "b_in": b_in.reshape(3 * KT, P).T,
        "bv": b_in[2 * E:],
        "w_out_t": inputs["L0_xattn_out_proj_w"].T,
        "b_out": inputs["L0_xattn_out_proj_b"],
        "protos": inputs["L0_ffn_prototypes"],
        "protos_t": inputs["L0_ffn_prototypes"].T,
        "fb_t": fb.reshape(NP * RK, E).T,
        "fa_t": fa.transpose(0, 2, 1).reshape(NP * RK, E),
        "f_bias": inputs["L0_ffn_bias"],
        "temp": inputs["L0_ffn_temp"].reshape(1),
    }
    nc = bacc.Bacc("TRN2", target_bir_lowering=False, num_devices=1)
    arrays, args = {}, []
    for name, a in laid.items():
        a = np.ascontiguousarray(a)
        arrays[f"in_{name}"] = a
        args.append(nc.dram_tensor(f"in_{name}", a.shape, mybir.dt.from_np(a.dtype), kind="ExternalInput").ap())
    out = nc.dram_tensor("out", (B, T, E), F32, kind="ExternalOutput").ap()
    build(nc, *args, out)
    r = run_bass_kernel_spmd(nc, [arrays], core_ids=[0])
    return r.results[0]["out"]
```

```python
import numpy as np
from contextlib import ExitStack

import concourse.bass as bass
from concourse import mybir

F32 = mybir.dt.float32
F32R = mybir.dt.float32r
U8 = mybir.dt.uint8
ALU = mybir.AluOpType
ACT = mybir.ActivationFunctionType
AX = mybir.AxisListType

P = 128
B, T, E = 8, 224, 512
S = 750
H, D = 16, 32
NP, RK = 32, 16
KT = E // P
HG = P // D
NG = H // HG
TC = 2
TW = T // TC
ST = 6
SW = S // ST
SH = (376, 374)
SO = (0, 376)
UG = HG * TC
UB = H * TC
SCALE = float(D) ** -0.5
EPS = 1e-5
FMAX = float(np.finfo(np.float32).max)


def apart(eng, passed):
    eng.sem_inc(passed, 1)


def layer_norm_stats(nc, eng, x, stats, mv, veps, sem, n, passed):
    apart(eng, passed)
    for c in range(TC):
        nc.vector.bn_stats(stats[:, c, :], x[:, c, :]).then_inc(sem, 1)
    eng.wait_ge(sem, n + 2)
    apart(eng, passed)
    for c in range(TC):
        nc.vector.bn_aggr(mv[:, c, :], stats[:, c, :]).then_inc(sem, 1)
    eng.wait_ge(sem, n + 4)
    return nc.vector.tensor_scalar(veps[:, :], mv[:, :, 1], EPS, None, ALU.add)


def rsqrt_refined(nc, eng, sd, veps, r, t, sem, n):
    nc.vector.reciprocal(r[:, :], sd[:, :]).then_inc(sem, 1)
    eng.wait_ge(sem, n + 1)
    nc.vector.tensor_tensor(t[:, 0, :], r[:, :], r[:, :], ALU.mult).then_inc(sem, 1)
    eng.wait_ge(sem, n + 2)
    nc.vector.tensor_tensor(t[:, 1, :], t[:, 0, :], veps[:, :], ALU.mult).then_inc(sem, 1)
    eng.wait_ge(sem, n + 3)
    nc.vector.tensor_scalar(t[:, 2, :], t[:, 1, :], -0.5, 1.5, ALU.mult, ALU.add).then_inc(sem, 1)
    eng.wait_ge(sem, n + 4)
    nc.vector.tensor_tensor(t[:, 3, :], t[:, 2, :], r[:, :], ALU.mult).then_inc(sem, 1)
    eng.wait_ge(sem, n + 5)


def project(nc, x, ctx_t, w_in_t, b_in, bv, q_parts, k_parts, v_all, ident):
    with ExitStack() as ctx:
        def sb(name, shape, dt=F32):
            return ctx.enter_context(nc.sbuf_tensor(name, shape, dt))

        def sem(name):
            return ctx.enter_context(nc.semaphore(name))

        w_stage = [sb(f"w_stage{j}", [P, KT, E]) for j in range(3)]
        w_hi = [sb(f"w_hi{j}", [P, KT, E], F32R) for j in range(3)]
        w_lo = [sb(f"w_lo{j}", [P, KT, E], F32R) for j in range(3)]
        ctx_raw = [sb(f"ctx_raw{p}", [P, KT, S]) for p in range(2)]
        ctx_hi = [sb(f"ctx_hi{p}", [P, KT, S], F32R) for p in range(2)]
        ctx_lo = [sb(f"ctx_lo{p}", [P, KT, S], F32R) for p in range(2)]
        x_in = sb("x_in", [TW, TC, E])
        xn = sb("xn", [TW, TC, E])
        xt_hi = sb("xt_hi", [P, KT, T], F32R)
        xt_lo = sb("xt_lo", [P, KT, T], F32R)
        k_hi = [sb(f"k_hi{r}", [P, S], F32R) for r in range(2)]
        k_lo = [sb(f"k_lo{r}", [P, S], F32R) for r in range(2)]
        v_out = [sb(f"v_out{r}", [SW, E]) for r in range(2)]
        q_f = sb("q_f", [P, NG, T])
        q_hi = sb("q_hi", [P, NG, T], F32R)
        q_lo = sb("q_lo", [P, NG, T], F32R)
        bias_col = sb("bias_col", [P, 12])
        nbq = sb("nbq", [P, NG])
        bv_row = sb("bv_row", [SW, E])
        stats = sb("stats", [TW, TC, 6])
        mv = sb("mv", [TW, TC, 2])
        veps = sb("veps", [TW, TC])
        sd = sb("sd", [TW, TC])
        rstd = sb("rstd", [TW, TC])
        nwt = sb("nwt", [TW, 4, TC])
        NACC = 4
        acc = [ctx.enter_context(nc.psum_tensor(f"acc{j}", [P, 512], F32)) for j in range(NACC)]
        xt_ps = [ctx.enter_context(nc.psum_tensor(f"xt_ps{c}", [P, 512], F32)) for c in range(TC)]

        w_loaded = [sem(f"w_loaded{j}") for j in range(3)]
        bias_loaded = sem("bias_loaded")
        ctx_loaded = [sem(f"ctx_loaded{p}") for p in range(2)]
        x_loaded = sem("x_loaded")
        w_hi_ready = sem("w_hi_ready")
        w_ready = sem("w_ready")
        nbq_ready = sem("nbq_ready")
        ctx0_hi_ready = sem("ctx0_hi_ready")
        ctx_hi_done = sem("ctx_hi_done")
        ctx_ready = [sem(f"ctx_ready{p}") for p in range(2)]
        passed = sem("passed1")
        ident_zero = sem("ident_zero")
        ident_ready = sem("ident_ready")
        ln_step = sem("ln_step")
        veps_ready = sem("veps_ready")
        sd_ready = sem("sd_ready")
        xn_ready = sem("xn_ready")
        xt_ps_ready = sem("xt_ps_ready")
        xt_hi_ready = sem("xt_hi_ready")
        xt_ready = sem("xt_ready")
        acc_ready = sem("acc_ready")
        k_hi_ready = sem("k_hi_ready")
        k_ready = sem("k_ready")
        v_ready = sem("v_ready")
        q_f_ready = sem("q_f_ready")
        q_hi_ready = sem("q_hi_ready")
        q_ready = sem("q_ready")
        k_stored = [sem(f"k_stored{r}") for r in range(2)]
        v_stored = [sem(f"v_stored{r}") for r in range(2)]
        q_stored = sem("q_stored")

        KG = NG * 2
        VG = ST
        QG = NG // 2
        AG = KG + VG + QG
        W_ORDER = (1, 2, 0)

        block = ctx.enter_context(nc.Block())

        @block.sync
        def _(eng):
            for started in (*k_stored, *v_stored, q_stored):
                eng.sem_inc(started, 1)
            def load_ctx(b, p):
                eng.dma_start(ctx_raw[p][:, :, :], ctx_t[b].rearrange("(k p) s -> p k s", p=P))\
                   .then_inc(ctx_loaded[p], 16)

            def load_w(j):
                eng.dma_start(w_stage[j][:, :, :],
                              w_in_t[:, j * E:(j + 1) * E].rearrange("(k p) o -> p k o", p=P))\
                   .then_inc(w_loaded[j], 16)

            def load_x(b):
                eng.dma_start(x_in[:, :, :], x[b].rearrange("(c t) e -> t c e", c=TC)).then_inc(x_loaded, 16)

            load_w(1)
            load_ctx(0, 0)
            load_x(0)
            eng.dma_start(bias_col[:, :], b_in).then_inc(bias_loaded, 16)
            eng.dma_start(bv_row[:, :], bv.partition_broadcast(SW)).then_inc(bias_loaded, 16)
            load_w(2)
            load_ctx(1, 1)
            load_w(0)

            def stores(b, n):
                for g in range(NG):
                    eng.wait_ge(k_ready, KG * n + 2 * g + 2)
                    for part, src in enumerate((k_hi, k_lo)):
                        eng.dma_start(k_parts[b, part, g * P:(g + 1) * P, :], src[g % 2][:, :].bitcast(F32))\
                           .then_inc(k_stored[g % 2], 16)
                for s in range(ST):
                    eng.wait_ge(v_ready, 1 + ST * n + s + 1)
                    eng.dma_start(v_all[b, s * SW:(s + 1) * SW, :], v_out[s % 2][:, :])\
                       .then_inc(v_stored[s % 2], 16)
                eng.wait_ge(q_ready, n + 1)
                for part, src in enumerate((q_hi, q_lo)):
                    eng.dma_start(q_parts[b, part].rearrange("(g p) t -> p g t", p=P),
                                  src[:, :, :].bitcast(F32)).then_inc(q_stored, 16)

            with eng.Fori(0, B // 2 - 1) as i:
                for p in range(2):
                    b = 2 * i + p
                    eng.wait_ge(xn_ready, b + 1)
                    load_x(b + 1)
                    eng.wait_ge(ctx_ready[p], i + 1)
                    load_ctx(b + 2, p)
                    stores(b, b)
            for b in (B - 2, B - 1):
                if b < B - 1:
                    eng.wait_ge(xn_ready, b + 1)
                    load_x(b + 1)
                stores(b, b)
            for r in range(2):
                eng.wait_ge(k_stored[r], 1 + 32 * 2 * B)
                eng.wait_ge(v_stored[r], 1 + 16 * 3 * B)
            eng.wait_ge(q_stored, 1 + 32 * B)

        @block.gpsimd
        def _(eng):
            eng.memset(ident[:, :], 0.0).then_inc(ident_zero, 1)
            eng.wait_ge(ident_zero, 1)
            eng.affine_select(out=ident[:, :], in_=ident[:, :], compare_op=ALU.not_equal, fill=1.0,
                              base=0, pattern=[[-1, P]], channel_multiplier=1).then_inc(ident_ready, 1)

            def split(p, i, n):
                eng.wait_ge(ctx_loaded[p], 16 * (i + 1))
                apart(eng, passed)
                eng.tensor_scalar(ctx_hi[p][:, :, :], ctx_raw[p][:, :, :], 1.0, 0.0, ALU.mult, ALU.add)\
                   .then_inc(ctx_hi_done, 1)
                eng.wait_ge(ctx_hi_done, n)
                eng.tensor_tensor(ctx_lo[p][:, :, :], ctx_raw[p][:, :, :], ctx_hi[p][:, :, :].bitcast(F32),
                                  ALU.subtract).then_inc(ctx_ready[p], 1)

            split(1, 0, 1)
            with eng.Fori(1, B // 2) as i:
                for p in range(2):
                    eng.wait_ge(acc_ready, 1 + AG * (2 * i + p - 1) - QG)
                    split(p, i, 2 * i + p)

        @block.scalar
        def _(eng):
            for n, j in enumerate(W_ORDER):
                if n == 1:
                    eng.wait_ge(ctx_loaded[0], 16)
                    nc.scalar.activation(ctx_hi[0][:, :, :], ctx_raw[0][:, :, :], ACT.Copy)\
                        .then_inc(ctx0_hi_ready, 1)
                eng.wait_ge(w_loaded[j], 16)
                nc.scalar.activation(w_hi[j][:, :, :], w_stage[j][:, :, :], ACT.Copy).then_inc(w_hi_ready, 1)
            eng.wait_ge(bias_loaded, 32)
            with eng.Fori(0, B // 2) as i:
                for p in range(2):
                    b = 2 * i + p
                    eng.wait_ge(veps_ready, b + 1)
                    nc.scalar.activation(sd[:, :], veps[:, :], ACT.Sqrt).then_inc(sd_ready, 1)
                    for g in range(NG):
                        eng.wait_ge(k_stored[g % 2], 1 + 32 * (2 * b + g // 2))
                        for h in range(2):
                            eng.wait_ge(acc_ready, 1 + AG * b + 2 * g + h + 1)
                            nc.scalar.activation(k_hi[g % 2][:, SO[h]:SO[h] + SH[h]],
                                                 acc[(2 * g + h) % NACC][:, 0:SH[h]], ACT.Identity,
                                                 bias=bias_col[:, NG + g:NG + g + 1]).then_inc(k_hi_ready, 1)
                    eng.wait_ge(acc_ready, 1 + AG * b)
                    for c in range(TC):
                        eng.wait_ge(xt_ps_ready, 1 + TC * b + c + 1)
                        nc.scalar.activation(xt_hi[:, :, c * TW:(c + 1) * TW],
                                             xt_ps[c][:, 0:KT * TW].rearrange("p (k t) -> p k t", k=KT),
                                             ACT.Copy).then_inc(xt_hi_ready, 1)
                    eng.wait_ge(q_stored, 1 + 32 * b)
                    eng.wait_ge(q_f_ready, 1 + QG * b + QG)
                    nc.scalar.activation(q_hi[:, :, :], q_f[:, :, :], ACT.Copy).then_inc(q_hi_ready, 1)

        @block.vector
        def _(eng):
            for started in (v_ready, q_f_ready, xt_ready):
                eng.sem_inc(started, 1)
            for n, j in enumerate(W_ORDER):
                if n == 1:
                    eng.wait_ge(ctx0_hi_ready, 1)
                    nc.vector.tensor_tensor(ctx_lo[0][:, :, :], ctx_raw[0][:, :, :],
                                            ctx_hi[0][:, :, :].bitcast(F32), ALU.subtract)\
                        .then_inc(ctx_ready[0], 1)
                eng.wait_ge(w_hi_ready, n + 1)
                nc.vector.tensor_tensor(w_lo[j][:, :, :], w_stage[j][:, :, :], w_hi[j][:, :, :].bitcast(F32),
                                        ALU.subtract).then_inc(w_ready, 1)
            eng.wait_ge(bias_loaded, 32)
            nc.vector.tensor_scalar(nbq[:, :], bias_col[:, 0:NG], -SCALE, None, ALU.mult).then_inc(nbq_ready, 1)
            eng.wait_ge(nbq_ready, 1)
            with eng.Fori(0, B // 2) as i:
                for p in range(2):
                    b = 2 * i + p
                    eng.wait_ge(x_loaded, 16 * (b + 1))
                    layer_norm_stats(nc, eng, x_in, stats, mv, veps, ln_step, 9 * b, passed).then_inc(veps_ready, 1)
                    eng.wait_ge(sd_ready, b + 1)
                    rsqrt_refined(nc, eng, sd, veps, rstd, nwt, ln_step, 9 * b + 4)
                    eng.wait_ge(xt_ps_ready, 1 + TC * b)
                    for c in range(TC):
                        last = nc.vector.tensor_scalar(xn[:, c, :], x_in[:, c, :], mv[:, c, 0:1],
                                                       nwt[:, 3, c:c + 1], ALU.subtract, ALU.mult)
                    last.then_inc(xn_ready, 1)
                    for g in range(NG):
                        for h in range(2):
                            eng.wait_ge(k_hi_ready, KG * b + 2 * g + h + 1)
                            nc.vector.scalar_tensor_tensor(
                                k_lo[g % 2][:, SO[h]:SO[h] + SH[h]], acc[(2 * g + h) % NACC][:, 0:SH[h]],
                                bias_col[:, NG + g:NG + g + 1],
                                k_hi[g % 2][:, SO[h]:SO[h] + SH[h]].bitcast(F32), ALU.add, ALU.subtract)\
                                .then_inc(k_ready, 1)
                    for c in range(TC):
                        eng.wait_ge(xt_hi_ready, TC * b + c + 1)
                        nc.vector.tensor_tensor(xt_lo[:, :, c * TW:(c + 1) * TW],
                                                xt_ps[c][:, 0:KT * TW].rearrange("p (k t) -> p k t", k=KT),
                                                xt_hi[:, :, c * TW:(c + 1) * TW].bitcast(F32), ALU.subtract)\
                            .then_inc(xt_ready, 1)
                    for s in range(ST):
                        eng.wait_ge(v_stored[s % 2], 1 + 16 * (3 * b + s // 2))
                        eng.wait_ge(acc_ready, 1 + AG * b + KG + s + 1)
                        nc.vector.tensor_tensor(v_out[s % 2][:, :], acc[(KG + s) % NACC][0:SW, :], bv_row[:, :],
                                                ALU.add).then_inc(v_ready, 1)
                    for j in range(QG):
                        eng.wait_ge(acc_ready, 1 + AG * b + KG + VG + j + 1)
                        for m in range(2):
                            g = 2 * j + m
                            last = nc.vector.tensor_scalar(q_f[:, g, :], acc[(KG + VG + j) % NACC][:, m * T:(m + 1) * T],
                                                           -SCALE, nbq[:, g:g + 1], ALU.mult, ALU.add)
                        last.then_inc(q_f_ready, 1)
                    eng.wait_ge(q_hi_ready, b + 1)
                    nc.vector.tensor_tensor(q_lo[:, :, :], q_f[:, :, :], q_hi[:, :, :].bitcast(F32), ALU.subtract)\
                        .then_inc(q_ready, 1)

        @block.tensor
        def _(eng):
            for started in (acc_ready, xt_ps_ready):
                eng.sem_inc(started, 1)
            eng.wait_ge(ident_ready, 1)

            def three_passes(out, w_of, x_of):
                n = 0
                for k in range(KT):
                    for a, c in ((0, 0), (0, 1), (1, 0)):
                        last = nc.tensor.matmul(out, w_of(a, k), x_of(c, k), start=(n == 0), stop=(n == 3 * KT - 1))
                        n += 1
                return last

            w_part = (w_hi, w_lo)
            eng.wait_ge(w_ready, 1)
            with eng.Fori(0, B // 2) as i:
                for p in range(2):
                    b = 2 * i + p
                    ctx_part = (ctx_hi[p], ctx_lo[p])
                    eng.wait_ge(ctx_ready[p], i + 1)
                    eng.wait_ge(v_ready, 1 + ST * b)
                    for g in range(NG):
                        for h in range(2):
                            n = 2 * g + h
                            if n == 2:
                                eng.wait_ge(q_f_ready, 1 + QG * b)
                            if n >= NACC:
                                eng.wait_ge(k_ready, KG * b + n - NACC + 1)
                            three_passes(acc[n % NACC][:, 0:SH[h]],
                                         lambda a, k: w_part[a][1][:, k, g * P:(g + 1) * P],
                                         lambda c, k: ctx_part[c][:, k, SO[h]:SO[h] + SH[h]])\
                                .then_inc(acc_ready, 1)
                    eng.wait_ge(xn_ready, b + 1)
                    eng.wait_ge(xt_ready, 1 + TC * b)
                    for c in range(TC):
                        for k in range(KT):
                            last = nc.tensor.transpose(xt_ps[c][:, k * TW:(k + 1) * TW],
                                                       xn[:, c, k * P:(k + 1) * P], ident[0:TW, 0:TW])
                        last.then_inc(xt_ps_ready, 1)
                    eng.wait_ge(w_ready, 2)
                    for s in range(ST):
                        n = KG + s
                        if s < NACC:
                            eng.wait_ge(k_ready, KG * b + n - NACC + 1)
                        else:
                            eng.wait_ge(v_ready, 1 + ST * b + s - NACC + 1)
                        three_passes(acc[n % NACC][0:SW, :],
                                     lambda c, k: ctx_part[c][:, k, s * SW:(s + 1) * SW],
                                     lambda a, k: w_part[a][2][:, k, :])\
                            .then_inc(acc_ready, 1)
                    eng.wait_ge(w_ready, 3)
                    eng.wait_ge(xt_ready, 1 + TC * b + TC)
                    for j in range(QG):
                        n = KG + VG + j
                        eng.wait_ge(v_ready, 1 + ST * b + VG + j - NACC + 1)
                        for m in range(2):
                            g = 2 * j + m
                            last = three_passes(acc[n % NACC][:, m * T:(m + 1) * T],
                                                lambda a, k: w_part[a][0][:, k, g * P:(g + 1) * P],
                                                lambda c, k: (xt_hi, xt_lo)[c][:, k, :])
                        last.then_inc(acc_ready, 1)


def attend(nc, bias, mask, q_parts, k_parts, v_all, attn_t, ident, w_dram, w_hi, w_lo):
    with ExitStack() as ctx:
        def sb(name, shape, dt=F32):
            return ctx.enter_context(nc.sbuf_tensor(name, shape, dt))

        def sem(name):
            return ctx.enter_context(nc.semaphore(name))

        def ps(name, shape):
            return ctx.enter_context(nc.psum_tensor(name, shape, F32))

        NBLK = 3
        SCORE_AT = 512 - SH[0]
        BT = ST // 2
        GB = NG * 2
        UP = UB * 2
        NSC = 4
        NPB = 3
        w_stage = sb("w_stage", [P, KT, E])
        neg_bias = sb("neg_bias", [TW, TC, S])
        masked_bias = [sb(f"masked_bias{p}", [TW, TC, S]) for p in range(2)]
        mask_u8 = sb("mask_u8", [TW, 2, S], U8)
        mask_keep = sb("mask_keep", [TW, S])
        mask_big = sb("mask_big", [TW, S])
        k_st = [sb(f"k_st{p}", [NBLK * D, HG, S], F32R) for p in range(2)]
        q_st = [sb(f"q_st{p}", [NBLK * D, HG, T], F32R) for p in range(2)]
        v_g = [sb(f"v_g{p}", [SW, ST, P]) for p in range(2)]
        scores = sb("scores", [TW, NSC, S])
        neg_max = sb("neg_max", [TW, UP])
        sums = sb("sums", [TW, UP])
        rsum = sb("rsum", [TW, UG])
        rsum_wide = sb("rsum_wide", [TW, TC, HG, D])
        rsum_t = sb("rsum_t", [P, T])
        probs_t = [sb(f"probs_t{p}", [SW, HG, ST, T]) for p in range(2)]
        attn = [sb(f"attn{p}", [P, T]) for p in range(2)]
        score_ps = [ps(f"score_ps{j}", [TW, 1024]) for j in range(2)]
        prob_ps = [ps(f"prob_ps{j}", [P, 512]) for j in range(NPB)]
        out_ps = ps("out_ps", [P, 512])

        w_loaded = sem("w_loaded")
        w_hi_done = sem("w_hi_done")
        w_lo_done = sem("w_lo_done")
        bias_loaded = sem("bias_loaded2")
        passed = sem("passed2")
        bias_negated = sem("bias_negated")
        mask_loaded = [sem(f"mask_loaded{p}") for p in range(2)]
        mask_step = sem("mask_step")
        masked_ready = [sem(f"masked_ready{p}") for p in range(2)]
        kq_loaded = [sem(f"kq_loaded{p}") for p in range(2)]
        v_loaded = [sem(f"v_loaded{p}") for p in range(2)]
        score_ready = sem("score_ready")
        added = sem("added")
        exp_done = sem("exp_done")
        prob_ps_ready = sem("prob_ps_ready")
        prob_copied = [sem(f"prob_copied{j}") for j in range(2)]
        rsum_ready = sem("rsum_ready")
        rsum_wide_ready = sem("rsum_wide_ready")
        out_ready = sem("out_ready")
        rsum_t_ready = sem("rsum_t_ready")
        attn_ready = sem("attn_ready")
        attn_stored = [sem(f"attn_stored{p}") for p in range(2)]
        KQ_LOADS = 16 * 2 * NBLK

        block = ctx.enter_context(nc.Block())

        @block.sync
        def _(eng):
            for started in (*attn_stored,):
                eng.sem_inc(started, 1)
            def load_kq(b, g):
                p = g % 2
                for j in range(NBLK):
                    rows = slice(j * D, (j + 1) * D)
                    eng.dma_start(k_st[p][rows, :, :].bitcast(F32),
                                  k_parts[b, (0, 1, 0)[j], g * P:(g + 1) * P, :].rearrange("(r d) s -> d r s", d=D))\
                       .then_inc(kq_loaded[p], 16)
                    eng.dma_start(q_st[p][rows, :, :].bitcast(F32),
                                  q_parts[b, (0, 0, 1)[j], g * P:(g + 1) * P, :].rearrange("(r d) t -> d r t", d=D))\
                       .then_inc(kq_loaded[p], 16)

            def load_v(b, g):
                eng.dma_start(v_g[g % 2][:, :, :],
                              v_all[b, :, g * P:(g + 1) * P].rearrange("(s p) d -> p s d", p=SW))\
                   .then_inc(v_loaded[g % 2], 16)

            def batch_group(i, n):
                return 2 * i + n // NG, n % NG

            def after_output(i, n, more):
                if n + 2 < GB or more:
                    eng.wait_ge(out_ready, 1 + GB * i + n + 1)
                    load_v(*batch_group(i, n + 2))
                b, g = batch_group(i, n)
                eng.wait_ge(attn_ready, 1 + GB * i + n + 1)
                eng.dma_start(attn_t[b, g * P:(g + 1) * P, :], attn[n % 2][:, :]).then_inc(attn_stored[n % 2], 16)

            def pair(i, more):
                for n in range(GB):
                    if n + 2 < GB or more:
                        eng.wait_ge(score_ready, UP * i + UG * (n + 1))
                        load_kq(*batch_group(i, n + 2))
                    if n:
                        after_output(i, n - 1, more)
                after_output(i, GB - 1, more)

            eng.dma_start(neg_bias[:, :, :], bias.rearrange("(c t) s -> t c s", c=TC)).then_inc(bias_loaded, 16)
            for g in range(2):
                load_kq(0, g)
                load_v(0, g)
            with eng.Fori(0, B // 2 - 1) as i:
                pair(i, True)
            pair(B // 2 - 1, False)
            for p in range(2):
                eng.wait_ge(attn_stored[p], 1 + 16 * B * NG // 2)

        @block.gpsimd
        def _(eng):
            for started in (*masked_ready, rsum_wide_ready, w_lo_done):
                eng.sem_inc(started, 1)
            def load_mask(b, p):
                eng.dma_start(mask_u8[:, p, :], mask[b].partition_broadcast(TW)).then_inc(mask_loaded[p], 16)

            def masked(i, p):
                n = 4 * (2 * i + p)
                eng.wait_ge(masked_ready[1 - p], 1 + i + p)
                eng.wait_ge(mask_loaded[p], 16 * (i + 1))
                apart(eng, passed)
                eng.tensor_scalar(mask_keep[:, :], mask_u8[:, p, :], -1.0, 1.0, ALU.mult, ALU.add)\
                   .then_inc(mask_step, 1)
                eng.tensor_scalar(mask_big[:, :], mask_u8[:, p, :], FMAX, 0.0, ALU.mult, ALU.add)\
                   .then_inc(mask_step, 1)
                eng.wait_ge(mask_step, n + 2)
                for c in range(TC):
                    eng.tensor_tensor(masked_bias[p][:, c, :], neg_bias[:, c, :], mask_keep[:, :], ALU.mult)\
                       .then_inc(mask_step, 1)
                for c in range(TC):
                    eng.wait_ge(mask_step, n + 3 + c)
                    last = eng.tensor_tensor(masked_bias[p][:, c, :], masked_bias[p][:, c, :], mask_big[:, :],
                                             ALU.add)
                last.then_inc(masked_ready[p], 1)

            def widen(i, n):
                eng.wait_ge(rsum_ready, GB * i + n + 1)
                eng.wait_ge(out_ready, 1 + GB * i + n)
                apart(eng, passed)
                eng.tensor_copy(rsum_wide[:, :, :, :],
                                rsum[:, :].rearrange("t (r c) -> t c r", c=TC).unsqueeze(3)
                                .broadcast_to([TW, TC, HG, D])).then_inc(rsum_wide_ready, 1)

            load_mask(0, 0)
            load_mask(1, 1)
            eng.wait_ge(bias_negated, 1)
            for p in range(2):
                masked(0, p)
            for j, w in enumerate(w_dram):
                eng.wait_ge(w_lo_done, 1 + j)
                eng.dma_start(w_stage[:, :, :], w.rearrange("(k p) o -> p k o", p=P)).then_inc(w_loaded, 16)
                eng.wait_ge(w_loaded, 16 * (j + 1))
                eng.tensor_scalar(w_hi[j][:, :, :], w_stage[:, :, :], 1.0, 0.0, ALU.mult, ALU.add)\
                   .then_inc(w_hi_done, 1)
                eng.wait_ge(w_hi_done, j + 1)
                eng.tensor_tensor(w_lo[j][:, :, :], w_stage[:, :, :], w_hi[j][:, :, :].bitcast(F32),
                                  ALU.subtract).then_inc(w_lo_done, 1)

            def pair(i, more):
                for n in range(GB):
                    widen(i, n)
                    if n == NG + 2 and more:
                        load_mask(2 * i + 2, 0)
                        load_mask(2 * i + 3, 1)
                        masked(i + 1, 0)
                if more:
                    eng.wait_ge(added, 1 + UP * (i + 1))
                    masked(i + 1, 1)

            with eng.Fori(0, B // 2 - 1) as i:
                pair(i, True)
            pair(B // 2 - 1, False)

        @block.scalar
        def _(eng):
            for started in (prob_copied[1],):
                eng.sem_inc(started, 1)
            with eng.Fori(0, B // 2) as i:
                def exp(w):
                    eng.wait_ge(added, 1 + UP * i + w + 1)
                    nc.scalar.activation(scores[:, w % NSC, :], scores[:, w % NSC, :], ACT.Exp,
                                         bias=neg_max[:, w:w + 1], scale=-1.0,
                                         accum_out=sums[:, w:w + 1]).then_inc(exp_done, 1)

                def sums_out(n):
                    eng.wait_ge(out_ready, 1 + GB * i + n + 1)
                    nc.scalar.activation(rsum_t[:, :], out_ps[:, 256:256 + T], ACT.Copy).then_inc(rsum_t_ready, 1)

                exp(0)
                exp(1)
                for w in range(UP):
                    n, h, c = w // UG, w // TC % HG, w % TC
                    if w % UG == 0:
                        eng.wait_ge(out_ready, 1 + GB * i + max(0, n - 1))
                    if w % UG == UG - 1 and n:
                        sums_out(n - 1)
                    eng.wait_ge(prob_ps_ready, 1 + 2 * (UP * i + w) + 2)
                    nc.scalar.activation(probs_t[n % 2][:, h, BT:ST, c * TW:(c + 1) * TW],
                                         prob_ps[(2 * w + 1) % NPB][0:SW, 0:BT * TW]
                                         .rearrange("p (s t) -> p s t", s=BT),
                                         ACT.Copy).then_inc(prob_copied[1], 1)
                    if w + 2 < UP:
                        exp(w + 2)
                sums_out(GB - 1)

        @block.vector
        def _(eng):
            for started in (added, prob_copied[0], attn_ready):
                eng.sem_inc(started, 1)
            eng.wait_ge(bias_loaded, 16)
            nc.vector.tensor_scalar(neg_bias[:, :, :], neg_bias[:, :, :], -1.0, FMAX, ALU.mult, ALU.min)\
                .then_inc(bias_negated, 1)
            with eng.Fori(0, B // 2) as i:
                def add(w):
                    p, c = w // UB, w % TC
                    if w % UB == 0:
                        eng.wait_ge(masked_ready[p], 1 + i + 1)
                    eng.wait_ge(prob_ps_ready, 1 + 2 * (UP * i + max(0, w - NSC + 1)))
                    eng.wait_ge(score_ready, UP * i + w + 1)
                    apart(eng, passed)
                    nc.vector.tensor_tensor_reduce(
                        out=scores[:, w % NSC, :], in0=score_ps[w % 2][:, SCORE_AT:SCORE_AT + S],
                        in1=masked_bias[p][:, c, :],
                        scale=1.0, scalar=FMAX, op0=ALU.add, op1=ALU.min,
                        accum_out=neg_max[:, w:w + 1]).then_inc(added, 1)

                def output(n):
                    eng.wait_ge(rsum_t_ready, GB * i + n + 1)
                    eng.wait_ge(attn_stored[n % 2], 1 + 16 * (NG * i + n // 2))
                    nc.vector.tensor_tensor(attn[n % 2][:, :], out_ps[:, 0:T], rsum_t[:, :], ALU.mult)\
                        .then_inc(attn_ready, 1)

                add(0)
                add(1)
                for w in range(UP):
                    n, h, c = w // UG, w // TC % HG, w % TC
                    if w + 2 < UP:
                        add(w + 2)
                    if w % UG == 0:
                        eng.wait_ge(out_ready, 1 + GB * i + max(0, n - 1))
                    eng.wait_ge(prob_ps_ready, 1 + 2 * (UP * i + w) + 1)
                    nc.vector.tensor_copy(probs_t[n % 2][:, h, 0:BT, c * TW:(c + 1) * TW],
                                          prob_ps[2 * w % NPB][0:SW, 0:BT * TW]
                                          .rearrange("p (s t) -> p s t", s=BT)).then_inc(prob_copied[0], 1)
                    if w % UG == UG - 2:
                        eng.wait_ge(exp_done, UP * i + w + 2)
                        eng.wait_ge(rsum_wide_ready, 1 + GB * i + n)
                        nc.vector.reciprocal(rsum[:, :], sums[:, n * UG:(n + 1) * UG]).then_inc(rsum_ready, 1)
                    if w % UG == UG - 1 and n:
                        output(n - 1)
                output(GB - 1)

        @block.tensor
        def _(eng):
            for started in (out_ready, prob_ps_ready):
                eng.sem_inc(started, 1)
            with eng.Fori(0, B // 2) as i:
                def score(w):
                    n, h, c = w // UG, w // TC % HG, w % TC
                    p = n % 2
                    if w % UG == 0:
                        eng.wait_ge(kq_loaded[p], KQ_LOADS * (NG * i + n // 2 + 1))
                    eng.wait_ge(added, 1 + UP * i + max(0, w - 1))
                    for half in range(2):
                        at = SCORE_AT + SO[half]
                        last = nc.tensor.matmul(score_ps[w % 2][:, at:at + SH[half]],
                                                q_st[p][:, h, c * TW:(c + 1) * TW],
                                                k_st[p][:, h, SO[half]:SO[half] + SH[half]], start=True, stop=True)
                    last.then_inc(score_ready, 1)

                def turn(w):
                    eng.wait_ge(exp_done, UP * i + w + 1)
                    for j in range(2):
                        q = 2 * w + j
                        if q < NPB:
                            for e in range(2):
                                eng.wait_ge(prob_copied[e], 1 + UP * i)
                        else:
                            eng.wait_ge(prob_copied[(q - NPB) % 2], 1 + UP * i + (q - NPB) // 2 + 1)
                        for s in range(BT):
                            last = nc.tensor.transpose(prob_ps[q % NPB][0:SW, s * TW:(s + 1) * TW],
                                                       scores[:, w % NSC, (BT * j + s) * SW:(BT * j + s + 1) * SW],
                                                       ident[0:TW, 0:TW])
                        last.then_inc(prob_ps_ready, 1)

                def weigh(n, s):
                    if s == 0:
                        eng.wait_ge(v_loaded[n % 2], 16 * (NG * i + n // 2 + 1))
                        eng.wait_ge(attn_ready, 1 + GB * i + n)
                        for j in range(2):
                            eng.wait_ge(prob_copied[j], 1 + UP * i + UG * (n + 1))
                    for h in range(HG):
                        nc.tensor.matmul(out_ps[h * D:(h + 1) * D, 0:T], v_g[n % 2][:, s, h * D:(h + 1) * D],
                                         probs_t[n % 2][:, h, s, :], start=(s == 0), stop=(s == ST - 1))

                def turn_sums(n):
                    eng.wait_ge(rsum_wide_ready, 1 + GB * i + n + 1)
                    for c in range(TC):
                        last = nc.tensor.transpose(out_ps[:, 256 + c * TW:256 + (c + 1) * TW],
                                                   rsum_wide[:, c, :, :].rearrange("t r d -> t (r d)"),
                                                   ident[0:TW, 0:TW])
                    last.then_inc(out_ready, 1)

                score(0)
                score(1)
                for w in range(UP):
                    n, u = w // UG, w % UG
                    if w + 2 < UP:
                        score(w + 2)
                    turn(w)
                    if n and 1 <= u <= ST:
                        weigh(n - 1, u - 1)
                    if n and u == ST:
                        turn_sums(n - 1)
                for s in range(ST):
                    weigh(GB - 1, s)
                turn_sums(GB - 1)


def finish(nc, x, attn_t, b_out, protos, protos_t, f_bias, temp, out, ident, w_hi, w_lo):
    with ExitStack() as ctx:
        def sb(name, shape, dt=F32):
            return ctx.enter_context(nc.sbuf_tensor(name, shape, dt))

        def sem(name):
            return ctx.enter_context(nc.semaphore(name))

        def ps(name, shape):
            return ctx.enter_context(nc.psum_tensor(name, shape, F32))

        PM = P // RK
        MT = NP // PM
        pt_stage = sb("pt_stage", [P, KT, NP])
        pt_hi = sb("pt_hi", [P, KT, NP], F32R)
        pt_lo = sb("pt_lo", [P, KT, NP], F32R)
        protos_sb = sb("protos_sb", [NP, E])
        squares = sb("squares", [TW, E])
        p2 = sb("p2", [NP, 1])
        bst_raw = sb("bst_raw", [P, E])
        bst_hi = sb("bst_hi", [P, E], F32R)
        bst = sb("bst", [P, E], F32R)
        bo_row = sb("bo_row", [TW, E])
        temp_col = sb("temp_col", [TW, 1])
        t_neg = sb("t_neg", [TW, 1])
        t_abs = sb("t_abs", [TW, 1])
        inv_t = sb("inv_t", [TW, 1])
        iota = sb("iota", [TW, NP])
        at_in = sb("at_in", [P, NG, T])
        at_hi = sb("at_hi", [P, NG, T], F32R)
        at_lo = sb("at_lo", [P, NG, T], F32R)
        x_res = sb("x_res", [TW, TC, E])
        xb = sb("xb", [TW, TC, E])
        x1 = sb("x1", [TW, B, TC, E])
        y2 = sb("y2", [TW, TC, E])
        yt_hi = sb("yt_hi", [P, KT, T], F32R)
        yt_lo = sb("yt_lo", [P, KT, T], F32R)
        stats = sb("stats2", [TW, TC, 6])
        mv = sb("mv2", [TW, TC, 2])
        veps = sb("veps2", [TW, TC])
        sd = sb("sd2", [TW, TC])
        rstd = sb("rstd2", [TW, TC])
        nwt = sb("nwt2", [TW, 4, TC])
        x2 = sb("x2", [TW, TC])
        dot = sb("dot", [NP, T])
        d2 = sb("d2", [TW, TC, NP])
        dist = sb("dist", [TW, TC, NP])
        near = sb("near", [TW, TC, NP])
        top = sb("top", [TW, TC, 8])
        top_at = sb("top_at", [TW, TC, 8], mybir.dt.uint32)
        top_f = sb("top_f", [TW, TC, 2])
        gap = sb("gap", [TW, TC])
        ez = sb("ez", [TW, TC])
        ez1 = sb("ez1", [TW, TC])
        wt = sb("wt", [TW, 2, TC])
        pick = sb("pick", [TW, 2, TC, NP])
        route = sb("route", [TW, TC, NP])
        route_st = sb("route_st", [TW, TC, 4, NP], F32R)
        route_wide = sb("route_wide", [TW, TC, NP, RK])
        route_t = sb("route_t", [P, T], F32R)
        h_sb = sb("h_sb", [P, MT, T])
        gated = sb("gated", [P, MT, T])
        g_hi = sb("g_hi", [P, MT, T], F32R)
        g_lo = sb("g_lo", [P, MT, T], F32R)
        y_out = [sb(f"y_out{c}", [TW, E]) for c in range(TC)]
        big = [ps(f"big{c}", [P, 512]) for c in range(TC)]
        tr = [ps(f"tr{c}", [P, 512]) for c in range(TC)]
        dot_ps = ps("dot_ps", [P, 512])
        route_ps = ps("route_ps", [P, 512])
        h_ps = [ps(f"h_ps{j}", [P, 512]) for j in range(2)]

        small_loaded = sem("small_loaded")
        small_step = sem("small_step")
        small_ready = sem("small_ready")
        p2_ready = sem("p2_ready")
        passed = sem("passed3")
        iota_ready = sem("iota_ready")
        at_loaded = sem("at_loaded")
        xr_loaded = sem("xr_loaded")
        at_hi_ready = sem("at_hi_ready")
        at_ready = sem("at_ready")
        xb_ready = sem("xb_ready")
        o_ready = sem("o_ready")
        x1_ready = sem("x1_ready")
        ln_step = sem("ln_step3")
        veps_ready = sem("veps_ready3")
        sd_ready = sem("sd_ready3")
        y2_ready = sem("y2_ready")
        x2_ready = sem("x2_ready")
        yt_ps_ready = sem("yt_ps_ready")
        yt_hi_ready = sem("yt_hi_ready")
        yt_ready = sem("yt_ready")
        dot_ps_ready = sem("dot_ps_ready")
        dot_ready = sem("dot_ready")
        dot_t_ready = sem("dot_t_ready")
        d2_ready = sem("d2_ready")
        dist_ready = sem("dist_ready")
        top_step = sem("top_step")
        gap_ready = sem("gap_ready")
        ez_ready = sem("ez_ready")
        route_ready = sem("route_ready")
        route_st_ready = sem("route_st_ready")
        wide_ready = sem("wide_ready")
        route_ps_ready = sem("route_ps_ready")
        route_t_ready = sem("route_t_ready")
        wide_ps_ready = sem("wide_ps_ready")
        h_ps_ready = sem("h_ps_ready")
        h_ready = sem("h_ready")
        gated_ready = sem("gated_ready")
        g_hi_ready = sem("g_hi_ready")
        g_ready = sem("g_ready")
        y_ps_ready = sem("y_ps_ready")
        y_ready = sem("y_ready")
        y_stored = [sem(f"y_stored{c}") for c in range(TC)]
        TOPS = 10
        LAST = B - 1

        block = ctx.enter_context(nc.Block())

        @block.sync
        def _(eng):
            for started in (*y_stored,):
                eng.sem_inc(started, 1)
            def load(b):
                eng.dma_start(at_in[:, :, :], attn_t[b].rearrange("(g p) t -> p g t", p=P)).then_inc(at_loaded, 16)
                eng.dma_start(x_res[:, :, :], x[b].rearrange("(c t) e -> t c e", c=TC)).then_inc(xr_loaded, 16)

            def store(b):
                for c in range(TC):
                    eng.wait_ge(y_ready, 1 + TC * b + c + 1)
                    eng.dma_start(out[b, c * TW:(c + 1) * TW, :], y_out[c][:, :]).then_inc(y_stored[c], 16)

            load(0)
            eng.dma_start(bo_row[:, :], b_out.partition_broadcast(TW)).then_inc(small_loaded, 16)
            eng.dma_start(pt_stage[:, :, :], protos_t.rearrange("(k p) n -> p k n", p=P)).then_inc(small_loaded, 16)
            eng.dma_start(protos_sb[:, :], protos).then_inc(small_loaded, 16)
            for r in range(4):
                eng.dma_start(bst_raw[r * NP:(r + 1) * NP, :], f_bias).then_inc(small_loaded, 16)
            eng.dma_start(temp_col[:, :], temp.partition_broadcast(TW)).then_inc(small_loaded, 16)
            eng.wait_ge(xb_ready, 1)
            load(1)
            with eng.Fori(0, LAST - 1) as b:
                eng.wait_ge(xb_ready, b + 2)
                load(b + 2)
                store(b)
            store(LAST - 1)
            store(LAST)
            for c in range(TC):
                eng.wait_ge(y_stored[c], 1 + 16 * B)

        @block.gpsimd
        def _(eng):
            eng.iota(iota[:, :], [[1, NP]], 0, 0, allow_small_or_imprecise_dtypes=True).then_inc(iota_ready, 1)
            eng.wait_ge(small_loaded, 16 * 8)
            with eng.Fori(0, B) as b:
                eng.wait_ge(at_loaded, 16 * (b + 1))
                eng.wait_ge(o_ready, 1 + TC * b)
                apart(eng, passed)
                eng.tensor_scalar(at_hi[:, :, :], at_in[:, :, :], 1.0, 0.0, ALU.mult, ALU.add)\
                   .then_inc(at_hi_ready, 1)
                eng.wait_ge(at_hi_ready, b + 1)
                eng.tensor_tensor(at_lo[:, :, :], at_in[:, :, :], at_hi[:, :, :].bitcast(F32), ALU.subtract)\
                   .then_inc(at_ready, 1)
                eng.wait_ge(xr_loaded, 16 * (b + 1))
                eng.wait_ge(x1_ready, 1 + TC * b)
                for c in range(TC):
                    last = eng.tensor_tensor(xb[:, c, :], x_res[:, c, :], bo_row[:, :], ALU.add)
                last.then_inc(xb_ready, 1)

        @block.scalar
        def _(eng):
            for started in (wide_ready, g_hi_ready, x2_ready):
                eng.sem_inc(started, 1)
            eng.wait_ge(small_loaded, 16 * 8)
            nc.scalar.activation(pt_hi[:, :, :], pt_stage[:, :, :], ACT.Copy).then_inc(small_step, 1)
            nc.scalar.activation(bst_hi[:, :], bst_raw[:, :], ACT.Copy).then_inc(small_step, 1)
            nc.scalar.activation(squares[0:NP, :], protos_sb[:, :], ACT.Square, accum_out=p2[:, :])\
                .then_inc(p2_ready, 1)
            eng.wait_ge(p2_ready, 1)

            def norm(b):
                eng.wait_ge(veps_ready, b + 1)
                nc.scalar.activation(sd[:, :], veps[:, :], ACT.Sqrt).then_inc(sd_ready, 1)
                eng.wait_ge(y2_ready, b + 1)
                for c in range(TC):
                    eng.wait_ge(yt_ps_ready, TC * b + c + 1)
                    nc.scalar.activation(yt_hi[:, :, c * TW:(c + 1) * TW],
                                         tr[c][:, 0:KT * TW].rearrange("p (k t) -> p k t", k=KT),
                                         ACT.Copy).then_inc(yt_hi_ready, 1)
                for c in range(TC):
                    eng.wait_ge(x2_ready, 1 + TC * b + c)
                    nc.scalar.activation(squares[:, :], y2[:, c, :], ACT.Square,
                                         accum_out=x2[:, c:c + 1]).then_inc(x2_ready, 1)

            def route_part(b):
                def copy_h(j):
                    eng.wait_ge(h_ps_ready, 2 * b + j + 1)
                    nc.scalar.activation(h_sb[:, 2 * j:2 * j + 2, :],
                                         h_ps[j][:, 0:2 * T].rearrange("p (m t) -> p m t", m=2),
                                         ACT.Copy).then_inc(h_ready, 1)

                copy_h(0)
                eng.wait_ge(d2_ready, b + 1)
                nc.scalar.activation(dist[:, :, :], d2[:, :, :], ACT.Sqrt).then_inc(dist_ready, 1)
                copy_h(1)
                eng.wait_ge(gap_ready, b + 1)
                nc.scalar.activation(ez[:, :], gap[:, :], ACT.Exp, scale=inv_t[:, 0:1]).then_inc(ez_ready, 1)
                eng.wait_ge(route_ready, b + 1)
                nc.scalar.activation(route_wide[:, :, :, :],
                                     route[:, :, :].unsqueeze(3).broadcast_to([TW, TC, NP, RK]),
                                     ACT.Copy).then_inc(wide_ready, 1)

            def experts(b):
                eng.wait_ge(route_ps_ready, 1 + b + 1)
                nc.scalar.activation(route_t[:, :], route_ps[:, 0:T], ACT.Copy).then_inc(route_t_ready, 1)
                eng.wait_ge(gated_ready, b + 1)
                nc.scalar.activation(g_hi[:, :, :], gated[:, :, :], ACT.Copy).then_inc(g_hi_ready, 1)

            eng.wait_ge(small_ready, 1)
            norm(0)
            route_part(0)
            with eng.Fori(0, LAST) as b:
                norm(b + 1)
                experts(b)
                route_part(b + 1)
            experts(LAST)

        @block.vector
        def _(eng):
            for started in (x1_ready, y_ready):
                eng.sem_inc(started, 1)
            eng.wait_ge(small_step, 2)
            nc.vector.tensor_tensor(pt_lo[:, :, :], pt_stage[:, :, :], pt_hi[:, :, :].bitcast(F32), ALU.subtract)
            for r in range(4):
                rows = slice(r * NP, (r + 1) * NP)
                if r % 2 == 0:
                    nc.vector.tensor_copy(bst[rows, :], bst_hi[rows, :].bitcast(F32))
                else:
                    nc.vector.tensor_tensor(bst[rows, :], bst_raw[rows, :], bst_hi[rows, :].bitcast(F32),
                                            ALU.subtract)
            nc.vector.tensor_scalar(t_neg[:, :], temp_col[:, :], -1.0, 0.1, ALU.mult, ALU.max)\
                .then_inc(small_step, 1)
            eng.wait_ge(small_step, 3)
            nc.vector.tensor_tensor(t_abs[:, :], temp_col[:, :], t_neg[:, :], ALU.max).then_inc(small_step, 1)
            eng.wait_ge(small_step, 4)
            nc.vector.reciprocal(inv_t[:, :], t_abs[:, :]).then_inc(small_ready, 1)
            eng.wait_ge(p2_ready, 1)
            eng.wait_ge(iota_ready, 1)

            def residual(b, c):
                if c == 0:
                    eng.wait_ge(xb_ready, b + 1)
                eng.wait_ge(o_ready, 1 + TC * b + c + 1)
                nc.vector.tensor_tensor(x1_of(b)[:, c, :], big[c][0:TW, :], xb[:, c, :], ALU.add)\
                    .then_inc(x1_ready, 1)

            def x1_of(b):
                return x1[:, bass.DynSlice(b, 1), :, :].rearrange("t b c e -> t (b c) e")

            def norm(b):
                eng.wait_ge(x1_ready, 1 + TC * (b + 1))
                layer_norm_stats(nc, eng, x1_of(b), stats, mv, veps, ln_step, 9 * b, passed)\
                    .then_inc(veps_ready, 1)

            def normalise(b):
                eng.wait_ge(sd_ready, b + 1)
                rsqrt_refined(nc, eng, sd, veps, rstd, nwt, ln_step, 9 * b + 4)
                for c in range(TC):
                    last = nc.vector.tensor_scalar(y2[:, c, :], x1_of(b)[:, c, :], mv[:, c, 0:1],
                                                   nwt[:, 3, c:c + 1], ALU.subtract, ALU.mult)
                last.then_inc(y2_ready, 1)

            def yt_low(b):
                for c in range(TC):
                    eng.wait_ge(yt_hi_ready, TC * b + c + 1)
                    nc.vector.tensor_tensor(yt_lo[:, :, c * TW:(c + 1) * TW],
                                            tr[c][:, 0:KT * TW].rearrange("p (k t) -> p k t", k=KT),
                                            yt_hi[:, :, c * TW:(c + 1) * TW].bitcast(F32), ALU.subtract)\
                        .then_inc(yt_ready, 1)

            def routing(b):
                n = TOPS * b
                eng.wait_ge(dot_ps_ready, b + 1)
                nc.vector.tensor_scalar(dot[:, :], dot_ps[0:NP, 0:T], -2.0, p2[:, 0:1], ALU.mult, ALU.add)\
                    .then_inc(dot_ready, 1)
                eng.wait_ge(dot_t_ready, b + 1)
                eng.wait_ge(x2_ready, 1 + TC * (b + 1))
                for c in range(TC):
                    last = nc.vector.tensor_scalar(d2[:, c, :], dot_ps[0:TW, 256 + c * NP:256 + (c + 1) * NP],
                                                   x2[:, c:c + 1], 0.0, ALU.add, ALU.max)
                last.then_inc(d2_ready, 1)
                eng.wait_ge(dist_ready, b + 1)
                nc.vector.tensor_scalar(near[:, :, :], dist[:, :, :], -1.0, None, ALU.mult).then_inc(top_step, 1)
                eng.wait_ge(top_step, n + 1)
                apart(eng, passed)
                for c in range(TC):
                    nc.vector.max(top[:, c, :], near[:, c, :]).then_inc(top_step, 1)
                eng.wait_ge(top_step, n + 3)
                nc.vector.tensor_tensor(gap[:, :], top[:, :, 1], top[:, :, 0], ALU.subtract).then_inc(gap_ready, 1)
                for c in range(TC):
                    nc.vector.max_index(top_at[:, c, :], top[:, c, :], near[:, c, :]).then_inc(top_step, 1)
                eng.wait_ge(top_step, n + 5)
                nc.vector.tensor_copy(top_f[:, :, :], top_at[:, :, 0:2]).then_inc(top_step, 1)
                eng.wait_ge(ez_ready, b + 1)
                nc.vector.tensor_scalar(ez1[:, :], ez[:, :], 1.0, None, ALU.add).then_inc(top_step, 1)
                eng.wait_ge(top_step, n + 7)
                nc.vector.reciprocal(wt[:, 0, :], ez1[:, :]).then_inc(top_step, 1)
                eng.wait_ge(top_step, n + 8)
                nc.vector.tensor_tensor(wt[:, 1, :], wt[:, 0, :], ez[:, :], ALU.mult).then_inc(top_step, 1)
                eng.wait_ge(top_step, n + 9)
                for j in range(2):
                    for c in range(TC):
                        last = nc.vector.tensor_scalar(pick[:, j, c, :], iota[:, :], top_f[:, c, j:j + 1],
                                                       wt[:, j, c:c + 1], ALU.is_equal, ALU.mult)
                last.then_inc(top_step, 1)
                eng.wait_ge(top_step, n + 10)
                eng.wait_ge(wide_ready, 1 + b)
                nc.vector.tensor_tensor(route[:, :, :], pick[:, 0, :, :], pick[:, 1, :, :], ALU.add)\
                    .then_inc(route_ready, 1)
                eng.wait_ge(route_ready, b + 1)
                eng.wait_ge(route_ps_ready, 1 + b)
                two = [TW, TC, 2, NP]
                nc.vector.tensor_copy(route_st[:, :, 0:2, :], route[:, :, :].unsqueeze(2).broadcast_to(two))\
                    .then_inc(route_st_ready, 1)
                eng.wait_ge(route_st_ready, 2 * b + 1)
                nc.vector.tensor_tensor(route_st[:, :, 2:4, :], route[:, :, :].unsqueeze(2).broadcast_to(two),
                                        route_st[:, :, 0:2, :].bitcast(F32), ALU.subtract)\
                    .then_inc(route_st_ready, 1)

            def gate(b):
                eng.wait_ge(h_ready, 2 * b + 2)
                eng.wait_ge(g_hi_ready, 1 + b)
                for c in range(TC):
                    eng.wait_ge(wide_ps_ready, TC * b + c + 1)
                    last = nc.vector.tensor_tensor(gated[:, :, c * TW:(c + 1) * TW],
                                                   tr[c][:, 0:MT * TW].rearrange("p (m t) -> p m t", m=MT),
                                                   h_sb[:, :, c * TW:(c + 1) * TW], ALU.mult)
                last.then_inc(gated_ready, 1)

            def gated_low(b):
                eng.wait_ge(g_hi_ready, 1 + b + 1)
                nc.vector.tensor_tensor(g_lo[:, :, :], gated[:, :, :], g_hi[:, :, :].bitcast(F32), ALU.subtract)\
                    .then_inc(g_ready, 1)

            def result(b, c):
                eng.wait_ge(y_ps_ready, TC * b + c + 1)
                eng.wait_ge(y_stored[c], 1 + 16 * b)
                nc.vector.tensor_tensor(y_out[c][:, :], h_ps[c][0:TW, :], x1_of(b)[:, c, :], ALU.add)\
                    .then_inc(y_ready, 1)

            residual(0, 0)
            residual(0, 1)
            norm(0)
            normalise(0)
            yt_low(0)
            routing(0)

            def turn_of(b, before):
                residual(b + 1, 0)
                if before:
                    result(b - 1, 0)
                residual(b + 1, 1)
                norm(b + 1)
                normalise(b + 1)
                if before:
                    result(b - 1, 1)
                yt_low(b + 1)
                gate(b)
                gated_low(b)
                routing(b + 1)

            turn_of(0, False)
            with eng.Fori(1, LAST) as b:
                turn_of(b, True)
            for c in range(TC):
                result(LAST - 1, c)
            gate(LAST)
            gated_low(LAST)
            for c in range(TC):
                result(LAST, c)

        @block.tensor
        def _(eng):
            for started in (o_ready, route_ps_ready):
                eng.sem_inc(started, 1)
            def three_passes(out_ap, left, right, tiles, first=True, last=True):
                n = 0
                for k in range(tiles):
                    for a, c in ((0, 0), (0, 1), (1, 0)):
                        ins = nc.tensor.matmul(out_ap, left(a, k), right(c, k), start=(first and n == 0),
                                               stop=(last and n == 3 * tiles - 1))
                        n += 1
                return ins

            def w_of(j):
                return lambda a, k: (w_hi, w_lo)[a][j][:, k, :]

            def project_out(b, c, first=False):
                if c == 0:
                    eng.wait_ge(at_ready, b + 1)
                if not first:
                    eng.wait_ge(x1_ready, 1 + TC * (b - 1) + c + 1)
                three_passes(big[c][0:TW, :], lambda a, k: (at_hi, at_lo)[a][:, k, c * TW:(c + 1) * TW], w_of(0), NG)\
                    .then_inc(o_ready, 1)

            def transpose_y(b):
                eng.wait_ge(y2_ready, b + 1)
                if not isinstance(b, int) or b > 1:
                    eng.wait_ge(gated_ready, b - 1)
                for c in range(TC):
                    for k in range(KT):
                        last = nc.tensor.transpose(tr[c][:, k * TW:(k + 1) * TW], y2[:, c, k * P:(k + 1) * P],
                                                   ident[0:TW, 0:TW])
                    last.then_inc(yt_ps_ready, 1)

            def distances(b):
                eng.wait_ge(yt_ready, TC * (b + 1))
                three_passes(dot_ps[0:NP, 0:T], lambda a, k: (pt_hi, pt_lo)[a][:, k, :],
                             lambda c, k: (yt_hi, yt_lo)[c][:, k, :], KT).then_inc(dot_ps_ready, 1)

            def down(b, j):
                for m in range(2):
                    tile = 2 * j + m
                    last = three_passes(h_ps[j][:, m * T:(m + 1) * T],
                                        lambda a, k: (w_hi, w_lo)[a][1][:, k, tile * P:(tile + 1) * P],
                                        lambda c, k: (yt_hi, yt_lo)[c][:, k, :], KT)
                last.then_inc(h_ps_ready, 1)

            def transpose_dot(b):
                eng.wait_ge(dot_ready, b + 1)
                apart(eng, passed)
                for c in range(TC):
                    last = nc.tensor.transpose(dot_ps[0:TW, 256 + c * NP:256 + (c + 1) * NP],
                                               dot[:, c * TW:(c + 1) * TW], ident[0:NP, 0:NP])
                last.then_inc(dot_t_ready, 1)

            def transpose_routes(b):
                eng.wait_ge(wide_ready, 1 + b + 1)
                for c in range(TC):
                    for m in range(MT):
                        last = nc.tensor.transpose(
                            tr[c][:, m * TW:(m + 1) * TW],
                            route_wide[:, c, m * PM:(m + 1) * PM, :].rearrange("t n r -> t (n r)"),
                            ident[0:TW, 0:TW])
                    last.then_inc(wide_ps_ready, 1)
                eng.wait_ge(route_st_ready, 2 * b + 2)
                for c in range(TC):
                    last = nc.tensor.transpose(route_ps[:, c * TW:(c + 1) * TW],
                                               route_st[:, c, :, :].rearrange("t r n -> t (r n)").bitcast(F32),
                                               ident[0:TW, 0:TW])
                last.then_inc(route_ps_ready, 1)

            def up(b, c):
                if c == 0:
                    eng.wait_ge(route_t_ready, b + 1)
                    eng.wait_ge(g_ready, b + 1)
                three_passes(h_ps[c][0:TW, :], lambda a, k: (g_hi, g_lo)[a][:, k, c * TW:(c + 1) * TW],
                             w_of(2), MT, last=False)
                nc.tensor.matmul(h_ps[c][0:TW, :], route_t[:, c * TW:(c + 1) * TW], bst[:, :],
                                 start=False, stop=True).then_inc(y_ps_ready, 1)

            def turn_of(b, before):
                project_out(b + 1, 0)
                if before:
                    eng.wait_ge(h_ready, 2 * b + 2)
                    up(b - 1, 0)
                project_out(b + 1, 1)
                if before:
                    up(b - 1, 1)
                else:
                    eng.wait_ge(yt_ready, TC)
                    eng.wait_ge(h_ready, 2)
                transpose_y(b + 1)
                eng.wait_ge(yt_ready, TC * (b + 2))
                distances(b + 1)
                transpose_routes(b)
                if before:
                    eng.wait_ge(y_ready, 1 + TC * b)
                down(b + 1, 0)
                transpose_dot(b + 1)
                down(b + 1, 1)

            for c in range(TC):
                project_out(0, c, True)
            transpose_y(0)
            eng.wait_ge(small_ready, 1)
            distances(0)
            down(0, 0)
            transpose_dot(0)
            down(0, 1)
            turn_of(0, False)
            with eng.Fori(1, LAST) as b:
                turn_of(b, True)
            eng.wait_ge(h_ready, 2 * LAST + 2)
            for c in range(TC):
                up(LAST - 1, c)
            transpose_routes(LAST)
            eng.wait_ge(y_ready, 1 + TC * LAST)
            for c in range(TC):
                up(LAST, c)


def build(nc, x, ctx_t, bias, mask, w_in_t, b_in, bv, w_out_t, b_out, protos, protos_t, fb_t, fa_t, f_bias, temp,
          out):
    q_parts = nc.dram_tensor("q_parts", [B, 2, E, T], F32, kind="Internal").ap()
    k_parts = nc.dram_tensor("k_parts", [B, 2, E, S], F32, kind="Internal").ap()
    v_all = nc.dram_tensor("v_all", [B, S, E], F32, kind="Internal").ap()
    attn_t = nc.dram_tensor("attn_t", [B, E, T], F32, kind="Internal").ap()
    with ExitStack() as ctx:
        ident = ctx.enter_context(nc.sbuf_tensor("ident", [P, P], F32))
        project(nc, x, ctx_t, w_in_t, b_in, bv, q_parts, k_parts, v_all, ident)
        w_hi = [ctx.enter_context(nc.sbuf_tensor(f"{n}_hi", [P, KT, E], F32R)) for n in ("out", "down", "up")]
        w_lo = [ctx.enter_context(nc.sbuf_tensor(f"{n}_lo", [P, KT, E], F32R)) for n in ("out", "down", "up")]
        attend(nc, bias, mask, q_parts, k_parts, v_all, attn_t, ident, (w_out_t, fb_t, fa_t), w_hi, w_lo)
        finish(nc, x, attn_t, b_out, protos, protos_t, f_bias, temp, out, ident, w_hi, w_lo)


def kernel(**inputs):
    import concourse.bacc as bacc
    from concourse.bass_utils import run_bass_kernel_spmd

    w_in, b_in = inputs["L0_xattn_in_proj_w"], inputs["L0_xattn_in_proj_b"]
    fa, fb = inputs["L0_ffn_A"], inputs["L0_ffn_B"]
    laid = {
        "x": inputs["x"],
        "ctx_t": inputs["ctx_1024"].transpose(0, 2, 1),
        "bias": inputs["fside_1xSxS2_0"].reshape(T, S),
        "mask": inputs["mask_BxS2_bk0"],
        "w_in_t": w_in.T,
        "b_in": b_in.reshape(3 * KT, P).T,
        "bv": b_in[2 * E:],
        "w_out_t": inputs["L0_xattn_out_proj_w"].T,
        "b_out": inputs["L0_xattn_out_proj_b"],
        "protos": inputs["L0_ffn_prototypes"],
        "protos_t": inputs["L0_ffn_prototypes"].T,
        "fb_t": fb.reshape(NP * RK, E).T,
        "fa_t": fa.transpose(0, 2, 1).reshape(NP * RK, E),
        "f_bias": inputs["L0_ffn_bias"],
        "temp": inputs["L0_ffn_temp"].reshape(1),
    }
    nc = bacc.Bacc("TRN2", target_bir_lowering=False, num_devices=1)
    arrays, args = {}, []
    for name, a in laid.items():
        a = np.ascontiguousarray(a)
        arrays[f"in_{name}"] = a
        args.append(nc.dram_tensor(f"in_{name}", a.shape, mybir.dt.from_np(a.dtype), kind="ExternalInput").ap())
    out = nc.dram_tensor("out", (B, T, E), F32, kind="ExternalOutput").ap()
    build(nc, *args, out)
    r = run_bass_kernel_spmd(nc, [arrays], core_ids=[0])
    return r.results[0]["out"]
```

```python
import numpy as np
from contextlib import ExitStack

import concourse.bass as bass
from concourse import mybir

F32 = mybir.dt.float32
F32R = mybir.dt.float32r
U8 = mybir.dt.uint8
ALU = mybir.AluOpType
ACT = mybir.ActivationFunctionType
AX = mybir.AxisListType

P = 128
B, T, E = 8, 224, 512
S = 750
H, D = 16, 32
NP, RK = 32, 16
KT = E // P
HG = P // D
NG = H // HG
TC = 2
TW = T // TC
ST = 6
SW = S // ST
SH = (376, 374)
SO = (0, 376)
UG = HG * TC
UB = H * TC
SCALE = float(D) ** -0.5
EPS = 1e-5
FMAX = float(np.finfo(np.float32).max)


def apart(eng, passed):
    eng.sem_inc(passed, 1)


def layer_norm_stats(nc, eng, x, stats, mv, veps, sem, n, passed):
    apart(eng, passed)
    for c in range(TC):
        nc.vector.bn_stats(stats[:, c, :], x[:, c, :]).then_inc(sem, 1)
    eng.wait_ge(sem, n + 2)
    apart(eng, passed)
    for c in range(TC):
        nc.vector.bn_aggr(mv[:, c, :], stats[:, c, :]).then_inc(sem, 1)
    eng.wait_ge(sem, n + 4)
    return nc.vector.tensor_scalar(veps[:, :], mv[:, :, 1], EPS, None, ALU.add)


def rsqrt_refined(nc, eng, sd, veps, r, t, sem, n):
    nc.vector.reciprocal(r[:, :], sd[:, :]).then_inc(sem, 1)
    eng.wait_ge(sem, n + 1)
    nc.vector.tensor_tensor(t[:, 0, :], r[:, :], r[:, :], ALU.mult).then_inc(sem, 1)
    eng.wait_ge(sem, n + 2)
    nc.vector.tensor_tensor(t[:, 1, :], t[:, 0, :], veps[:, :], ALU.mult).then_inc(sem, 1)
    eng.wait_ge(sem, n + 3)
    nc.vector.tensor_scalar(t[:, 2, :], t[:, 1, :], -0.5, 1.5, ALU.mult, ALU.add).then_inc(sem, 1)
    eng.wait_ge(sem, n + 4)
    nc.vector.tensor_tensor(t[:, 3, :], t[:, 2, :], r[:, :], ALU.mult).then_inc(sem, 1)
    eng.wait_ge(sem, n + 5)


def cut(tensor, at, shape):
    flat = tensor[:, :, :].rearrange("p a b -> p (a b)")
    return flat[0:shape[0], at:at + shape[1] * shape[2]].rearrange("p (a b) -> p a b", a=shape[1])


class Shared:

    def __init__(self, nc, ctx):
        def sb(name, shape, dt=F32):
            return ctx.enter_context(nc.sbuf_tensor(name, shape, dt))

        self.ident = sb("ident", [P, P])
        self.w_hi = [sb(f"w_hi{j}", [P, KT, E], F32R) for j in range(3)]
        self.w_lo = [sb(f"w_lo{j}", [P, KT, E], F32R) for j in range(3)]
        self.w_stage = sb("w_stage", [P, KT, E])
        self.x_in = cut(self.w_stage, 0, [TW, TC, E])
        self.xn = cut(self.w_stage, TC * E, [TW, TC, E])
        self.at_in = cut(self.w_stage, 0, [P, NG, T])
        self.x_res = cut(self.w_stage, TC * E, [TW, TC, E])
        self.at_hi = sb("at_hi", [P, KT, T], F32R)
        self.at_lo = sb("at_lo", [P, KT, T], F32R)
        self.bo_row = sb("bo_row", [TW, E])
        self.xb = sb("xb", [TW, TC, E])
        self.at_loaded = ctx.enter_context(nc.semaphore("at_loaded"))
        self.xr_loaded = ctx.enter_context(nc.semaphore("xr_loaded"))
        self.bo_loaded = ctx.enter_context(nc.semaphore("bo_loaded"))
        self.at_hi_ready = ctx.enter_context(nc.semaphore("at_hi_ready"))
        self.at_ready = ctx.enter_context(nc.semaphore("at_ready"))
        self.xb_ready = ctx.enter_context(nc.semaphore("xb_ready"))
        self.attn_stored = [ctx.enter_context(nc.semaphore(f"attn_stored{p}")) for p in range(2)]

    def until_attended(self, nc, ctx):
        def sb(name, shape, dt=F32):
            return ctx.enter_context(nc.sbuf_tensor(name, shape, dt))

        def sem(name):
            return ctx.enter_context(nc.semaphore(name))

        NBLK = self.NBLK = 3
        self.w_in_stage = [sb(f"w_in_stage{j}", [P, KT, E]) for j in range(3)]
        self.neg_bias = cut(self.w_in_stage[0], 0, [TW, TC, S])
        self.masked_bias = [cut(self.w_in_stage[1 + p], 0, [TW, TC, S]) for p in range(2)]
        self.ctx_raw = [sb(f"ctx_raw{p}", [P, KT, S]) for p in range(2)]
        self.ctx_hi0 = sb("ctx_hi0", [P, KT, S], F32R)
        self.ctx_lo0 = sb("ctx_lo0", [P, KT, S], F32R)
        self.k_st = [t[0:NBLK * D, :, :] for t in (self.ctx_hi0, self.ctx_lo0)]
        self.q_st = [sb("q_st0", [NBLK * D, HG, T], F32R)]
        self.v_g = [cut(self.ctx_raw[0], p * ST * P, [SW, ST, P]) for p in range(2)]
        mask_tiles = cut(self.ctx_raw[1], 0, [TW, 2, S])
        self.mask_keep, self.mask_big = mask_tiles[:, 0, :], mask_tiles[:, 1, :]
        self.mask_u8 = sb("mask_u8", [TW, 2, S], U8)
        self.bias_loaded = sem("neg_bias_loaded")
        self.bias_negated = sem("bias_negated")
        self.mask_loaded = [sem(f"mask_loaded{p}") for p in range(2)]
        self.mask_step = sem("mask_step")
        self.masked_ready = [sem(f"masked_ready{p}") for p in range(2)]
        self.kq_loaded = [sem(f"kq_loaded{p}") for p in range(2)]
        self.v_loaded = [sem(f"v_loaded{p}") for p in range(2)]
        self.k_stored = [sem(f"k_stored{r}") for r in range(2)]
        self.v_stored = [sem(f"v_stored{r}") for r in range(2)]
        self.q_stored = sem("q_stored")


def load_k(eng, sh, k_parts, b, g):
    p = g % 2
    for j in range(sh.NBLK):
        eng.dma_start(sh.k_st[p][j * D:(j + 1) * D, :, :].bitcast(F32),
                      k_parts[b, (0, 1, 0)[j], g * P:(g + 1) * P, :].rearrange("(r d) s -> d r s", d=D))\
           .then_inc(sh.kq_loaded[p], 16)


def load_q(eng, sh, q_parts, b, g):
    p = g % 2
    for j in range(sh.NBLK):
        eng.dma_start(sh.q_st[p][j * D:(j + 1) * D, :, :].bitcast(F32),
                      q_parts[b, (0, 0, 1)[j], g * P:(g + 1) * P, :].rearrange("(r d) t -> d r t", d=D))\
           .then_inc(sh.kq_loaded[p], 16)


def load_v(eng, sh, v_all, b, g):
    eng.dma_start(sh.v_g[g % 2], v_all[b, :, g * P:(g + 1) * P].rearrange("(s p) d -> p s d", p=SW))\
       .then_inc(sh.v_loaded[g % 2], 16)


def load_mask(eng, sh, mask, b, p):
    eng.dma_start(sh.mask_u8[:, p, :], mask[b].partition_broadcast(TW)).then_inc(sh.mask_loaded[p], 16)


def mask_bias(eng, sh, i, p, passed):
    n = 4 * (2 * i + p)
    eng.wait_ge(sh.masked_ready[1 - p], 1 + i + p)
    eng.wait_ge(sh.mask_loaded[p], 16 * (i + 1))
    apart(eng, passed)
    eng.tensor_scalar(sh.mask_keep, sh.mask_u8[:, p, :], -1.0, 1.0, ALU.mult, ALU.add).then_inc(sh.mask_step, 1)
    eng.tensor_scalar(sh.mask_big, sh.mask_u8[:, p, :], FMAX, 0.0, ALU.mult, ALU.add).then_inc(sh.mask_step, 1)
    eng.wait_ge(sh.mask_step, n + 2)
    for c in range(TC):
        eng.tensor_tensor(sh.masked_bias[p][:, c, :], sh.neg_bias[:, c, :], sh.mask_keep, ALU.mult)\
           .then_inc(sh.mask_step, 1)
    for c in range(TC):
        eng.wait_ge(sh.mask_step, n + 3 + c)
        last = eng.tensor_tensor(sh.masked_bias[p][:, c, :], sh.masked_bias[p][:, c, :], sh.mask_big, ALU.add)
    last.then_inc(sh.masked_ready[p], 1)


def project(nc, x, ctx_t, w_in_t, b_in, bv, bias, mask, q_parts, k_parts, v_all, sh):
    with ExitStack() as ctx:
        def sb(name, shape, dt=F32):
            return ctx.enter_context(nc.sbuf_tensor(name, shape, dt))

        def sem(name):
            return ctx.enter_context(nc.semaphore(name))

        ident, w_stage, ctx_raw, x_in, xn = sh.ident, sh.w_in_stage, sh.ctx_raw, sh.x_in, sh.xn
        w_hi, w_lo = sh.w_hi, sh.w_lo
        xt_hi, xt_lo = sh.at_hi, sh.at_lo
        ctx_hi = [sh.ctx_hi0, sb("ctx_hi1", [P, KT, S], F32R)]
        ctx_lo = [sh.ctx_lo0, sb("ctx_lo1", [P, KT, S], F32R)]
        k_stored, v_stored, q_stored = sh.k_stored, sh.v_stored, sh.q_stored
        k_hi = [sb(f"k_hi{r}", [P, S], F32R) for r in range(2)]
        k_lo = [sb(f"k_lo{r}", [P, S], F32R) for r in range(2)]
        v_out = [sb(f"v_out{r}", [SW, E]) for r in range(2)]
        q_f = sb("q_f", [P, NG, T])
        q_hi = sb("q_hi", [P, NG, T], F32R)
        q_lo = sb("q_lo", [P, NG, T], F32R)
        bias_col = sb("bias_col", [P, 12])
        nbq = sb("nbq", [P, NG])
        bv_row = sb("bv_row", [SW, E])
        stats = sb("stats", [TW, TC, 6])
        mv = sb("mv", [TW, TC, 2])
        veps = sb("veps", [TW, TC])
        sd = sb("sd", [TW, TC])
        rstd = sb("rstd", [TW, TC])
        nwt = sb("nwt", [TW, 4, TC])
        NACC = 4
        acc = [ctx.enter_context(nc.psum_tensor(f"acc{j}", [P, 512], F32)) for j in range(NACC)]
        xt_ps = [ctx.enter_context(nc.psum_tensor(f"xt_ps{c}", [P, 512], F32)) for c in range(TC)]

        wk_loaded = [sem(f"wk_loaded{k}") for k in range(KT)]
        w_loaded = [sem(f"w_loaded{j}") for j in range(3)]
        bias_loaded = sem("bias_loaded")
        ctx_loaded = [[sem(f"ctx_loaded{p}_{k}") for k in range(KT)] for p in range(2)]
        x_loaded = sem("x_loaded")
        wk_hi_ready = sem("wk_hi_ready")
        wk_ready = sem("wk_ready")
        wv_hi_ready = sem("wv_hi_ready")
        wv_ready = sem("wv_ready")
        wq_ready = sem("wq_ready")
        nbq_ready = sem("nbq_ready")
        ctx0_hi_ready = sem("ctx0_hi_ready")
        ctx_hi_done = sem("ctx_hi_done")
        ctx_ready = [sem(f"ctx_ready{p}") for p in range(2)]
        passed = sem("passed1")
        passed_pe = sem("passed_pe")
        ident_zero = sem("ident_zero")
        ident_ready = sem("ident_ready")
        ln_step = sem("ln_step")
        veps_ready = sem("veps_ready")
        sd_ready = sem("sd_ready")
        xn_ready = sem("xn_ready")
        xt_ps_ready = sem("xt_ps_ready")
        xt_hi_ready = sem("xt_hi_ready")
        xt_ready = sem("xt_ready")
        acc_ready = sem("acc_ready")
        k_hi_ready = sem("k_hi_ready")
        k_ready = sem("k_ready")
        v_ready = sem("v_ready")
        q_f_ready = sem("q_f_ready")
        q_hi_ready = sem("q_hi_ready")
        q_ready = sem("q_ready")

        KG = NG * 2
        VG = ST
        QG = NG // 2
        AG = KG + VG + QG

        block = ctx.enter_context(nc.Block())

        def load_ctx(eng, b, p, k):
            eng.dma_start(ctx_raw[p][:, k, :], ctx_t[b, k * P:(k + 1) * P, :]).then_inc(ctx_loaded[p][k], 16)

        @block.sync
        def _(eng):
            for started in (*k_stored, *v_stored, q_stored):
                eng.sem_inc(started, 1)

            def load_w(j):
                eng.dma_start(w_stage[j][:, :, :],
                              w_in_t[:, j * E:(j + 1) * E].rearrange("(k p) o -> p k o", p=P))\
                   .then_inc(w_loaded[j], 16)

            def load_x(b):
                eng.dma_start(x_in, x[b].rearrange("(c t) e -> t c e", c=TC)).then_inc(x_loaded, 16)

            for k in range(KT):
                eng.dma_start(w_stage[1][:, k, :], w_in_t[k * P:(k + 1) * P, E:2 * E]).then_inc(wk_loaded[k], 16)
                load_ctx(eng, 0, 0, k)
            eng.dma_start(bias_col[:, :], b_in).then_inc(bias_loaded, 16)
            eng.dma_start(bv_row[:, :], bv.partition_broadcast(SW)).then_inc(bias_loaded, 16)
            load_w(2)
            load_x(0)
            load_w(0)
            for k in range(KT):
                load_ctx(eng, 1, 1, k)

            def store_keys(b, g):
                eng.wait_ge(k_ready, KG * b + 2 * g + 2)
                for part, src in enumerate((k_hi, k_lo)):
                    eng.dma_start(k_parts[b, part, g * P:(g + 1) * P, :], src[g % 2][:, :].bitcast(F32))\
                       .then_inc(k_stored[g % 2], 16)

            def first_operands(g):
                if g == 0:
                    for r in range(2):
                        eng.wait_ge(k_stored[r], 1 + 32 * 2)
                        eng.wait_ge(v_stored[r], 1 + 16 * 3)
                        eng.wait_ge(ctx_ready[r], KT * B // 2)
                    eng.wait_ge(q_stored, 1 + 32)
                    eng.wait_ge(acc_ready, 1 + AG * (B - 1) - QG)
                load_k(eng, sh, k_parts, 0, g)
                if g == 0:
                    load_q(eng, sh, q_parts, 0, g)
                load_v(eng, sh, v_all, 0, g)

            def stores(b, more, ahead=None):
                for g in range(NG):
                    store_keys(b, g)
                    if g == 1 and more:
                        eng.wait_ge(xn_ready, b + 1)
                        load_x(b + 1)
                for s in range(ST):
                    eng.wait_ge(v_ready, 1 + ST * b + s + 1)
                    eng.dma_start(v_all[b, s * SW:(s + 1) * SW, :], v_out[s % 2][:, :])\
                       .then_inc(v_stored[s % 2], 16)
                    if not more and s < 2:
                        first_operands(s)
                    if ahead is not None and s < KT:
                        p, i = ahead
                        eng.wait_ge(ctx_ready[p], KT * i + s + 1)
                        load_ctx(eng, b + 2, p, s)
                eng.wait_ge(q_ready, QG * (b + 1))
                for part, src in enumerate((q_hi, q_lo)):
                    eng.dma_start(q_parts[b, part].rearrange("(g p) t -> p g t", p=P),
                                  src[:, :, :].bitcast(F32)).then_inc(q_stored, 16)

            with eng.Fori(0, B // 2 - 1) as i:
                for p in range(2):
                    stores(2 * i + p, True, (p, i))
            stores(B - 2, True)
            stores(B - 1, False)

        @block.gpsimd
        def _(eng):
            for started in sh.masked_ready:
                eng.sem_inc(started, 1)
            eng.memset(ident[:, :], 0.0).then_inc(ident_zero, 1)
            eng.wait_ge(ident_zero, 1)
            eng.affine_select(out=ident[:, :], in_=ident[:, :], compare_op=ALU.not_equal, fill=1.0,
                              base=0, pattern=[[-1, P]], channel_multiplier=1).then_inc(ident_ready, 1)
            for p in range(2):
                load_mask(eng, sh, mask, p, p)

            def split(p, i, n):
                for k in range(KT):
                    eng.wait_ge(ctx_loaded[p][k], 16 * (i + 1))
                    apart(eng, passed)
                    eng.tensor_scalar(ctx_hi[p][:, k, :], ctx_raw[p][:, k, :], 1.0, 0.0, ALU.mult, ALU.add)\
                       .then_inc(ctx_hi_done, 1)
                    eng.wait_ge(ctx_hi_done, KT * n + k + 1)
                    eng.tensor_tensor(ctx_lo[p][:, k, :], ctx_raw[p][:, k, :], ctx_hi[p][:, k, :].bitcast(F32),
                                      ALU.subtract).then_inc(ctx_ready[p], 1)

            eng.wait_ge(w_loaded[0], 16)
            eng.tensor_scalar(w_hi[0][:, :, :], w_stage[0][:, :, :], 1.0, 0.0, ALU.mult, ALU.add).then_inc(wq_ready, 1)
            eng.wait_ge(wq_ready, 1)
            eng.tensor_tensor(w_lo[0][:, :, :], w_stage[0][:, :, :], w_hi[0][:, :, :].bitcast(F32),
                              ALU.subtract).then_inc(wq_ready, 1)
            eng.wait_ge(wq_ready, 2)
            eng.dma_start(sh.neg_bias, bias.rearrange("(c t) s -> t c s", c=TC)).then_inc(sh.bias_loaded, 16)
            split(1, 0, 0)
            with eng.Fori(1, B // 2 - 1) as i:
                for p in range(2):
                    eng.wait_ge(acc_ready, 1 + AG * (2 * i + p - 1) - QG)
                    split(p, i, 2 * i + p - 1)
            eng.wait_ge(sh.bias_loaded, 16)
            eng.tensor_scalar(sh.neg_bias, sh.neg_bias, -1.0, FMAX, ALU.mult, ALU.min).then_inc(sh.bias_negated, 1)
            for p in range(2):
                eng.wait_ge(acc_ready, 1 + AG * (B - 3 + p) - QG)
                split(p, B // 2 - 1, B - 3 + p)
            eng.wait_ge(acc_ready, 1 + AG * (B - 1) - QG)
            eng.wait_ge(sh.bias_negated, 1)
            for p in range(2):
                mask_bias(eng, sh, 0, p, passed)

        @block.scalar
        def _(eng):
            for k in range(KT):
                eng.wait_ge(wk_loaded[k], 16)
                nc.scalar.activation(w_hi[1][:, k, :], w_stage[1][:, k, :], ACT.Copy).then_inc(wk_hi_ready, 1)
                eng.wait_ge(ctx_loaded[0][k], 16)
                nc.scalar.activation(ctx_hi[0][:, k, :], ctx_raw[0][:, k, :], ACT.Copy).then_inc(ctx0_hi_ready, 1)
            eng.wait_ge(w_loaded[2], 16)
            nc.scalar.activation(w_hi[2][:, :, :], w_stage[2][:, :, :], ACT.Copy).then_inc(wv_hi_ready, 1)
            eng.wait_ge(bias_loaded, 32)
            with eng.Fori(0, B // 2) as i:
                for p in range(2):
                    b = 2 * i + p
                    for g in range(NG):
                        if g == 1:
                            eng.wait_ge(veps_ready, b + 1)
                            nc.scalar.activation(sd[:, :], veps[:, :], ACT.Sqrt).then_inc(sd_ready, 1)
                        eng.wait_ge(k_stored[g % 2], 1 + 32 * (2 * b + g // 2))
                        for h in range(2):
                            eng.wait_ge(acc_ready, 1 + AG * b + 2 * g + h + 1)
                            nc.scalar.activation(k_hi[g % 2][:, SO[h]:SO[h] + SH[h]],
                                                 acc[(2 * g + h) % NACC][:, 0:SH[h]], ACT.Identity,
                                                 bias=bias_col[:, NG + g:NG + g + 1]).then_inc(k_hi_ready, 1)
                    eng.wait_ge(acc_ready, 1 + AG * b)
                    for c in range(TC):
                        eng.wait_ge(xt_ps_ready, 1 + TC * b + c + 1)
                        nc.scalar.activation(xt_hi[:, :, c * TW:(c + 1) * TW],
                                             xt_ps[c][:, 0:KT * TW].rearrange("p (k t) -> p k t", k=KT),
                                             ACT.Copy).then_inc(xt_hi_ready, 1)
                    eng.wait_ge(q_stored, 1 + 32 * b)
                    for j in range(QG):
                        eng.wait_ge(q_f_ready, 1 + QG * b + j + 1)
                        nc.scalar.activation(q_hi[:, 2 * j:2 * j + 2, :], q_f[:, 2 * j:2 * j + 2, :], ACT.Copy)\
                            .then_inc(q_hi_ready, 1)

        @block.vector
        def _(eng):
            for started in (v_ready, q_f_ready, xt_ready):
                eng.sem_inc(started, 1)
            for k in range(KT):
                eng.wait_ge(wk_hi_ready, k + 1)
                nc.vector.tensor_tensor(w_lo[1][:, k, :], w_stage[1][:, k, :], w_hi[1][:, k, :].bitcast(F32),
                                        ALU.subtract).then_inc(wk_ready, 1)
                eng.wait_ge(ctx0_hi_ready, k + 1)
                nc.vector.tensor_tensor(ctx_lo[0][:, k, :], ctx_raw[0][:, k, :], ctx_hi[0][:, k, :].bitcast(F32),
                                        ALU.subtract).then_inc(ctx_ready[0], 1)
            eng.wait_ge(wv_hi_ready, 1)
            nc.vector.tensor_tensor(w_lo[2][:, :, :], w_stage[2][:, :, :], w_hi[2][:, :, :].bitcast(F32),
                                    ALU.subtract).then_inc(wv_ready, 1)
            eng.wait_ge(bias_loaded, 32)
            nc.vector.tensor_scalar(nbq[:, :], bias_col[:, 0:NG], -SCALE, None, ALU.mult).then_inc(nbq_ready, 1)
            eng.wait_ge(nbq_ready, 1)
            with eng.Fori(0, B // 2) as i:
                for p in range(2):
                    b = 2 * i + p
                    for g in range(NG):
                        for h in range(2):
                            eng.wait_ge(k_hi_ready, KG * b + 2 * g + h + 1)
                            nc.vector.scalar_tensor_tensor(
                                k_lo[g % 2][:, SO[h]:SO[h] + SH[h]], acc[(2 * g + h) % NACC][:, 0:SH[h]],
                                bias_col[:, NG + g:NG + g + 1],
                                k_hi[g % 2][:, SO[h]:SO[h] + SH[h]].bitcast(F32), ALU.add, ALU.subtract)\
                                .then_inc(k_ready, 1)
                            if (g, h) == (0, 1):
                                eng.wait_ge(x_loaded, 16 * (b + 1))
                                layer_norm_stats(nc, eng, x_in, stats, mv, veps, ln_step, 9 * b, passed)\
                                    .then_inc(veps_ready, 1)
                            if (g, h) == (1, 0):
                                eng.wait_ge(sd_ready, b + 1)
                                rsqrt_refined(nc, eng, sd, veps, rstd, nwt, ln_step, 9 * b + 4)
                            if (g, h) == (1, 1):
                                eng.wait_ge(xt_ps_ready, 1 + TC * b)
                                for c in range(TC):
                                    last = nc.vector.tensor_scalar(xn[:, c, :], x_in[:, c, :], mv[:, c, 0:1],
                                                                   nwt[:, 3, c:c + 1], ALU.subtract, ALU.mult)
                                last.then_inc(xn_ready, 1)
                    for c in range(TC):
                        eng.wait_ge(xt_hi_ready, TC * b + c + 1)
                        nc.vector.tensor_tensor(xt_lo[:, :, c * TW:(c + 1) * TW],
                                                xt_ps[c][:, 0:KT * TW].rearrange("p (k t) -> p k t", k=KT),
                                                xt_hi[:, :, c * TW:(c + 1) * TW].bitcast(F32), ALU.subtract)\
                            .then_inc(xt_ready, 1)
                    for s in range(ST):
                        eng.wait_ge(v_stored[s % 2], 1 + 16 * (3 * b + s // 2))
                        eng.wait_ge(acc_ready, 1 + AG * b + KG + s + 1)
                        nc.vector.tensor_tensor(v_out[s % 2][:, :], acc[(KG + s) % NACC][0:SW, :], bv_row[:, :],
                                                ALU.add).then_inc(v_ready, 1)
                    for j in range(QG):
                        eng.wait_ge(acc_ready, 1 + AG * b + KG + VG + j + 1)
                        for m in range(2):
                            g = 2 * j + m
                            last = nc.vector.tensor_scalar(q_f[:, g, :], acc[(KG + VG + j) % NACC][:, m * T:(m + 1) * T],
                                                           -SCALE, nbq[:, g:g + 1], ALU.mult, ALU.add)
                        last.then_inc(q_f_ready, 1)
                        eng.wait_ge(q_hi_ready, QG * b + j + 1)
                        nc.vector.tensor_tensor(q_lo[:, 2 * j:2 * j + 2, :], q_f[:, 2 * j:2 * j + 2, :],
                                                q_hi[:, 2 * j:2 * j + 2, :].bitcast(F32), ALU.subtract)\
                            .then_inc(q_ready, 1)

        @block.tensor
        def _(eng):
            for started in (acc_ready, xt_ps_ready):
                eng.sem_inc(started, 1)
            eng.wait_ge(ident_ready, 1)

            def three_passes(out, w_of, x_of, before=None):
                n = 0
                for k in range(KT):
                    if before:
                        before(k)
                    for a, c in ((0, 0), (0, 1), (1, 0)):
                        last = nc.tensor.matmul(out, w_of(a, k), x_of(c, k), start=(n == 0), stop=(n == 3 * KT - 1))
                        n += 1
                return last

            w_part = (w_hi, w_lo)
            with eng.Fori(0, B // 2) as i:
                for p in range(2):
                    b = 2 * i + p
                    ctx_part = (ctx_hi[p], ctx_lo[p])

                    def tile_ready(k):
                        eng.wait_ge(wk_ready, k + 1)
                        eng.wait_ge(ctx_ready[p], KT * i + k + 1)
                        apart(eng, passed_pe)

                    eng.wait_ge(v_ready, 1 + ST * b)
                    for g in range(NG):
                        for h in range(2):
                            n = 2 * g + h
                            if n == 2:
                                eng.wait_ge(q_f_ready, 1 + QG * b)
                            if n >= NACC:
                                eng.wait_ge(k_ready, KG * b + n - NACC + 1)
                            three_passes(acc[n % NACC][:, 0:SH[h]],
                                         lambda a, k: w_part[a][1][:, k, g * P:(g + 1) * P],
                                         lambda c, k: ctx_part[c][:, k, SO[h]:SO[h] + SH[h]],
                                         tile_ready if n == 0 else None)\
                                .then_inc(acc_ready, 1)
                    eng.wait_ge(xn_ready, b + 1)
                    eng.wait_ge(xt_ready, 1 + TC * b)
                    for c in range(TC):
                        for k in range(KT):
                            last = nc.tensor.transpose(xt_ps[c][:, k * TW:(k + 1) * TW],
                                                       xn[:, c, k * P:(k + 1) * P], ident[0:TW, 0:TW])
                        last.then_inc(xt_ps_ready, 1)
                    eng.wait_ge(wv_ready, 1)
                    for s in range(ST):
                        n = KG + s
                        if s < NACC:
                            eng.wait_ge(k_ready, KG * b + n - NACC + 1)
                        else:
                            eng.wait_ge(v_ready, 1 + ST * b + s - NACC + 1)
                        three_passes(acc[n % NACC][0:SW, :],
                                     lambda c, k: ctx_part[c][:, k, s * SW:(s + 1) * SW],
                                     lambda a, k: w_part[a][2][:, k, :])\
                            .then_inc(acc_ready, 1)
                    eng.wait_ge(wq_ready, 2)
                    eng.wait_ge(xt_ready, 1 + TC * b + TC)
                    for j in range(QG):
                        n = KG + VG + j
                        eng.wait_ge(v_ready, 1 + ST * b + VG + j - NACC + 1)
                        for m in range(2):
                            g = 2 * j + m
                            last = three_passes(acc[n % NACC][:, m * T:(m + 1) * T],
                                                lambda a, k: w_part[a][0][:, k, g * P:(g + 1) * P],
                                                lambda c, k: (xt_hi, xt_lo)[c][:, k, :])
                        last.then_inc(acc_ready, 1)


def load_attended(eng, sh, x, attn_t, b, at_loaded, xr_loaded):
    eng.dma_start(sh.at_in, attn_t[b].rearrange("(g p) t -> p g t", p=P)).then_inc(at_loaded, 16)
    eng.dma_start(sh.x_res, x[b].rearrange("(c t) e -> t c e", c=TC)).then_inc(xr_loaded, 16)


def split_attended(eng, sh, at_loaded, xr_loaded, loads, b, passed):
    eng.wait_ge(at_loaded, 16 * loads)
    apart(eng, passed)
    eng.tensor_scalar(sh.at_hi[:, :, :], sh.at_in, 1.0, 0.0, ALU.mult, ALU.add).then_inc(sh.at_hi_ready, 1)
    eng.wait_ge(sh.at_hi_ready, b + 1)
    eng.tensor_tensor(sh.at_lo[:, :, :], sh.at_in, sh.at_hi[:, :, :].bitcast(F32), ALU.subtract)\
       .then_inc(sh.at_ready, 1)
    eng.wait_ge(xr_loaded, 16 * loads)


def add_output_bias(eng, sh):
    for c in range(TC):
        last = eng.tensor_tensor(sh.xb[:, c, :], sh.x_res[:, c, :], sh.bo_row[:, :], ALU.add)
    last.then_inc(sh.xb_ready, 1)


def attend(nc, mask, x, b_out, q_parts, k_parts, v_all, attn_t, w_dram, sh):
    with ExitStack() as ctx:
        def sb(name, shape, dt=F32):
            return ctx.enter_context(nc.sbuf_tensor(name, shape, dt))

        def sem(name):
            return ctx.enter_context(nc.semaphore(name))

        def ps(name, shape):
            return ctx.enter_context(nc.psum_tensor(name, shape, F32))

        NBLK = sh.NBLK
        SCORE_AT = 512 - SH[0]
        BT = ST // 2
        GB = NG * 2
        UP = UB * 2
        NSC = 4
        NPB = 3
        ident, w_stage, w_hi, w_lo = sh.ident, sh.w_stage, sh.w_hi, sh.w_lo
        sh.q_st.append(sb("q_st1", [NBLK * D, HG, T], F32R))
        masked_bias, k_st, q_st, v_g = sh.masked_bias, sh.k_st, sh.q_st, sh.v_g
        masked_ready, kq_loaded, v_loaded = sh.masked_ready, sh.kq_loaded, sh.v_loaded
        scores = sb("scores", [TW, NSC, S])
        neg_max = sb("neg_max", [TW, UP])
        sums = sb("sums", [TW, UP])
        rsum = sb("rsum", [TW, UG])
        rsum_wide = sb("rsum_wide", [TW, TC, HG, D])
        rsum_t = sb("rsum_t", [P, T])
        probs_t = [sb(f"probs_t{p}", [SW, HG, ST, T]) for p in range(2)]
        attn = [sb(f"attn{p}", [P, T]) for p in range(2)]
        score_ps = [ps(f"score_ps{j}", [TW, 1024]) for j in range(2)]
        prob_ps = [ps(f"prob_ps{j}", [P, 512]) for j in range(NPB)]
        out_ps = ps("out_ps", [P, 512])

        w_loaded = sem("w_loaded")
        w_hi_done = sem("w_hi_done")
        w_lo_done = sem("w_lo_done")
        passed = sem("passed2")
        score_ready = sem("score_ready")
        added = sem("added")
        exp_done = sem("exp_done")
        prob_ps_ready = sem("prob_ps_ready")
        prob_copied = [sem(f"prob_copied{j}") for j in range(2)]
        rsum_ready = sem("rsum_ready")
        rsum_wide_ready = sem("rsum_wide_ready")
        out_ready = sem("out_ready")
        rsum_t_ready = sem("rsum_t_ready")
        attn_ready = sem("attn_ready")
        attn_stored = sh.attn_stored
        KQ_LOADS = 16 * 2 * NBLK

        def projections_stored(eng):
            for r in range(2):
                eng.wait_ge(sh.k_stored[r], 1 + 32 * 2 * B)
                eng.wait_ge(sh.v_stored[r], 1 + 16 * 3 * B)
            eng.wait_ge(sh.q_stored, 1 + 32 * B)

        block = ctx.enter_context(nc.Block())

        @block.sync
        def _(eng):
            for started in (*attn_stored,):
                eng.sem_inc(started, 1)
            def batch_group(i, n):
                return 2 * i + n // NG, n % NG

            def after_output(i, n, more):
                if n + 2 < GB or more:
                    eng.wait_ge(out_ready, 1 + GB * i + n + 1)
                    load_v(eng, sh, v_all, *batch_group(i, n + 2))
                b, g = batch_group(i, n)
                eng.wait_ge(attn_ready, 1 + GB * i + n + 1)
                eng.dma_start(attn_t[b, g * P:(g + 1) * P, :], attn[n % 2][:, :]).then_inc(attn_stored[n % 2], 16)

            def pair(i, more):
                for n in range(GB):
                    if n + 2 < GB or more:
                        eng.wait_ge(score_ready, UP * i + UG * (n + 1))
                        load_k(eng, sh, k_parts, *batch_group(i, n + 2))
                        load_q(eng, sh, q_parts, *batch_group(i, n + 2))
                    if n == GB - 1 and not more:
                        eng.wait_ge(w_lo_done, 1 + len(w_dram))
                        for p in range(2):
                            eng.wait_ge(attn_stored[p], 1 + 32)
                        load_attended(eng, sh, x, attn_t, 0, sh.at_loaded, sh.xr_loaded)
                    if n:
                        after_output(i, n - 1, more)
                if not more:
                    eng.wait_ge(sh.xb_ready, 1)
                    for p in range(2):
                        eng.wait_ge(attn_stored[p], 1 + 64)
                    load_attended(eng, sh, x, attn_t, 1, sh.at_loaded, sh.xr_loaded)
                after_output(i, GB - 1, more)

            load_q(eng, sh, q_parts, 0, 1)
            eng.dma_start(sh.bo_row[:, :], b_out.partition_broadcast(TW)).then_inc(sh.bo_loaded, 16)
            projections_stored(eng)
            with eng.Fori(0, B // 2 - 1) as i:
                pair(i, True)
            pair(B // 2 - 1, False)

        @block.gpsimd
        def _(eng):
            for started in (rsum_wide_ready, w_lo_done):
                eng.sem_inc(started, 1)

            def widen(i, n):
                eng.wait_ge(rsum_ready, GB * i + n + 1)
                eng.wait_ge(out_ready, 1 + GB * i + n)
                apart(eng, passed)
                eng.tensor_copy(rsum_wide[:, :, :, :],
                                rsum[:, :].rearrange("t (r c) -> t c r", c=TC).unsqueeze(3)
                                .broadcast_to([TW, TC, HG, D])).then_inc(rsum_wide_ready, 1)

            def load_weights(j):
                eng.wait_ge(w_lo_done, 1 + j)
                eng.dma_start(w_stage[:, :, :], w_dram[j].rearrange("(k p) o -> p k o", p=P)).then_inc(w_loaded, 16)

            def weights_high(j):
                eng.wait_ge(w_loaded, 16 * (j + 1))
                eng.tensor_scalar(w_hi[j][:, :, :], w_stage[:, :, :], 1.0, 0.0, ALU.mult, ALU.add)\
                   .then_inc(w_hi_done, 1)

            def weights_low(j):
                eng.wait_ge(w_hi_done, j + 1)
                eng.tensor_tensor(w_lo[j][:, :, :], w_stage[:, :, :], w_hi[j][:, :, :].bitcast(F32),
                                  ALU.subtract).then_inc(w_lo_done, 1)

            def pair(i, more):
                for n in range(GB):
                    widen(i, n)
                    if n == 0 and more:
                        load_mask(eng, sh, mask, 2 * i + 2, 0)
                        load_mask(eng, sh, mask, 2 * i + 3, 1)
                    if n == NG and more:
                        mask_bias(eng, sh, i + 1, 0, passed)
                    if not more and n == 2 * len(w_dram):
                        split_attended(eng, sh, sh.at_loaded, sh.xr_loaded, 1, 0, passed)
                        eng.wait_ge(sh.bo_loaded, 16)
                        add_output_bias(eng, sh)
                    if not more and n < 2 * len(w_dram):
                        j = n // 2
                        if n % 2 == 0:
                            weights_high(j)
                        else:
                            weights_low(j)
                            if j + 1 < len(w_dram):
                                load_weights(j + 1)
                if more:
                    eng.wait_ge(added, 1 + UP * (i + 1))
                    mask_bias(eng, sh, i + 1, 1, passed)

            load_weights(0)
            with eng.Fori(0, B // 2 - 1) as i:
                pair(i, True)
            pair(B // 2 - 1, False)
        @block.scalar
        def _(eng):
            for started in (prob_copied[1],):
                eng.sem_inc(started, 1)

            def exp(i, w):
                eng.wait_ge(added, 1 + UP * i + w + 1)
                nc.scalar.activation(scores[:, w % NSC, :], scores[:, w % NSC, :], ACT.Exp,
                                     bias=neg_max[:, w % UP:w % UP + 1], scale=-1.0,
                                     accum_out=sums[:, w % UP:w % UP + 1]).then_inc(exp_done, 1)

            def sums_out(i, n):
                eng.wait_ge(out_ready, 1 + GB * i + n + 1)
                nc.scalar.activation(rsum_t[:, :], out_ps[:, 256:256 + T], ACT.Copy).then_inc(rsum_t_ready, 1)

            def units(i, first, end, lookahead):
                for w in range(first, end):
                    n, h, c = w // UG, w // TC % HG, w % TC
                    if w % UG == 0:
                        eng.wait_ge(out_ready, 1 + GB * i + max(0, n - 1))
                    if w % UG == UG - 1 and n:
                        sums_out(i, n - 1)
                    eng.wait_ge(prob_ps_ready, 1 + 2 * (UP * i + w) + 2)
                    nc.scalar.activation(probs_t[n % 2][:, h, BT:ST, c * TW:(c + 1) * TW],
                                         prob_ps[(2 * (w % UP) + 1) % NPB][0:SW, 0:BT * TW]
                                         .rearrange("p (s t) -> p s t", s=BT),
                                         ACT.Copy).then_inc(prob_copied[1], 1)
                    if w + 2 < lookahead:
                        exp(i, w + 2)

            exp(0, 0)
            exp(0, 1)
            projections_stored(eng)
            units(0, 0, UG, UP)
            with eng.Fori(0, B // 2 - 1) as i:
                units(i, UG, UG + UP, UG + UP + 2)
            units(B // 2 - 1, UG, UP, UP)
            sums_out(B // 2 - 1, GB - 1)

        @block.vector
        def _(eng):
            for started in (added, prob_copied[0], attn_ready):
                eng.sem_inc(started, 1)

            def add_waits(i, w):
                if w % UB == 0:
                    eng.wait_ge(masked_ready[w // UB % 2], 1 + i + w // UP + 1)
                if w >= NSC:
                    eng.wait_ge(prob_ps_ready, 1 + 2 * (UP * i + w - NSC + 1))
                eng.wait_ge(score_ready, UP * i + w + 1)

            def add(w):
                nc.vector.tensor_tensor_reduce(
                    out=scores[:, w % NSC, :], in0=score_ps[w % 2][:, SCORE_AT:SCORE_AT + S],
                    in1=masked_bias[w // UB % 2][:, w % TC, :],
                    scale=1.0, scalar=FMAX, op0=ALU.add, op1=ALU.min,
                    accum_out=neg_max[:, w % UP:w % UP + 1]).then_inc(added, 1)

            def output(i, n):
                eng.wait_ge(rsum_t_ready, GB * i + n + 1)
                eng.wait_ge(attn_stored[n % 2], 1 + 16 * (NG * i + n // 2))
                nc.vector.tensor_tensor(attn[n % 2][:, :], out_ps[:, 0:T], rsum_t[:, :], ALU.mult)\
                    .then_inc(attn_ready, 1)

            def units(i, first, end, lookahead, last):
                for w in range(first, end):
                    n, h, c = w // UG, w // TC % HG, w % TC
                    if w + 2 < lookahead:
                        add(w + 2)
                    if w + 3 <= min(lookahead, last):
                        add_waits(i, w + 3)
                    if w % UG == 0:
                        eng.wait_ge(out_ready, 1 + GB * i + max(0, n - 1))
                    eng.wait_ge(prob_ps_ready, 1 + 2 * (UP * i + w) + 1)
                    nc.vector.tensor_copy(probs_t[n % 2][:, h, 0:BT, c * TW:(c + 1) * TW],
                                          prob_ps[2 * (w % UP) % NPB][0:SW, 0:BT * TW]
                                          .rearrange("p (s t) -> p s t", s=BT)).then_inc(prob_copied[0], 1)
                    if w % UG == UG - 2:
                        g = n % GB
                        eng.wait_ge(exp_done, UP * i + w + 2)
                        eng.wait_ge(rsum_wide_ready, 1 + GB * i + n)
                        nc.vector.reciprocal(rsum[:, :], sums[:, g * UG:(g + 1) * UG]).then_inc(rsum_ready, 1)
                    if w % UG == UG - 1 and n:
                        output(i, n - 1)

            for w in range(3):
                add_waits(0, w)
                if w < 2:
                    add(w)
            projections_stored(eng)
            units(0, 0, UG, UP, UP - 1)
            with eng.Fori(0, B // 2 - 1) as i:
                units(i, UG, UG + UP, UG + UP + 2, UG + UP + 2)
            units(B // 2 - 1, UG, UP, UP, UP - 1)
            output(B // 2 - 1, GB - 1)

        @block.tensor
        def _(eng):
            for started in (out_ready, prob_ps_ready):
                eng.sem_inc(started, 1)

            def score(i, w):
                n, h, c = w // UG, w // TC % HG, w % TC
                p = n % 2
                if w % UG == 0:
                    eng.wait_ge(kq_loaded[p], KQ_LOADS * (NG * i + n // 2 + 1))
                eng.wait_ge(added, 1 + UP * i + max(0, w - 1))
                for half in range(2):
                    at = SCORE_AT + SO[half]
                    last = nc.tensor.matmul(score_ps[w % 2][:, at:at + SH[half]],
                                            q_st[p][:, h, c * TW:(c + 1) * TW],
                                            k_st[p][:, h, SO[half]:SO[half] + SH[half]], start=True, stop=True)
                last.then_inc(score_ready, 1)

            def turn(i, w, j):
                q = 2 * (w % UP) + j
                if q < NPB:
                    before = 2 * (w // UP * UP) - (2, 1, 3)[q]
                else:
                    before = 2 * w + j - NPB
                eng.wait_ge(prob_copied[before % 2], 1 + UP * i + max(0, before // 2 + 1))
                for s in range(BT):
                    last = nc.tensor.transpose(prob_ps[q % NPB][0:SW, s * TW:(s + 1) * TW],
                                               scores[:, w % NSC, (BT * j + s) * SW:(BT * j + s + 1) * SW],
                                               ident[0:TW, 0:TW])
                last.then_inc(prob_ps_ready, 1)

            SHARE_AT = (0, 3, 6, 10, 14, 18, 22, ST * HG)
            SHARE = [range(a, b) for a, b in zip(SHARE_AT, SHARE_AT[1:])]

            def weigh(i, n, products):
                if products[0] == 0:
                    eng.wait_ge(v_loaded[n % 2], 16 * (NG * i + n // 2 + 1))
                    eng.wait_ge(attn_ready, 1 + GB * i + n)
                    for j in range(2):
                        eng.wait_ge(prob_copied[j], 1 + UP * i + UG * (n + 1))
                for s, h in (divmod(m, HG) for m in products):
                    nc.tensor.matmul(out_ps[h * D:(h + 1) * D, 0:T], v_g[n % 2][:, s, h * D:(h + 1) * D],
                                     probs_t[n % 2][:, h, s, :], start=(s == 0), stop=(s == ST - 1))

            def turn_sums(i, n):
                eng.wait_ge(rsum_wide_ready, 1 + GB * i + n + 1)
                for c in range(TC):
                    last = nc.tensor.transpose(out_ps[:, 256 + c * TW:256 + (c + 1) * TW],
                                               rsum_wide[:, c, :, :].rearrange("t r d -> t (r d)"),
                                               ident[0:TW, 0:TW])
                last.then_inc(out_ready, 1)

            def units(i, first, end, last):
                for w in range(first, end):
                    n, u = w // UG, w % UG
                    eng.wait_ge(exp_done, UP * i + w + 1)
                    turn(i, w, 0)
                    if w + 3 <= last:
                        score(i, w + 3)
                    turn(i, w, 1)
                    if n and u < len(SHARE):
                        weigh(i, n - 1, SHARE[u])
                    if n and u == len(SHARE) - 1:
                        turn_sums(i, n - 1)

            for w in range(3):
                score(0, w)
            units(0, 0, UG, UP - 1)
            with eng.Fori(0, B // 2 - 1) as i:
                units(i, UG, UG + UP, UG + UP + 2)
            units(B // 2 - 1, UG, UP, UP - 1)
            for share in SHARE:
                weigh(B // 2 - 1, GB - 1, share)
            turn_sums(B // 2 - 1, GB - 1)


def finish(nc, x, attn_t, protos, protos_t, f_bias, temp, out, sh):
    with ExitStack() as ctx:
        def sb(name, shape, dt=F32):
            return ctx.enter_context(nc.sbuf_tensor(name, shape, dt))

        def sem(name):
            return ctx.enter_context(nc.semaphore(name))

        def ps(name, shape):
            return ctx.enter_context(nc.psum_tensor(name, shape, F32))

        PM = P // RK
        MT = NP // PM
        pt_stage = sb("pt_stage", [P, KT, NP])
        pt_hi = sb("pt_hi", [P, KT, NP], F32R)
        pt_lo = sb("pt_lo", [P, KT, NP], F32R)
        protos_sb = sb("protos_sb", [NP, E])
        squares = sb("squares", [TW, E])
        p2 = sb("p2", [NP, 1])
        bst_raw = sb("bst_raw", [P, E])
        bst_hi = sb("bst_hi", [P, E], F32R)
        bst = sb("bst", [P, E], F32R)
        temp_col = sb("temp_col", [TW, 1])
        t_neg = sb("t_neg", [TW, 1])
        t_abs = sb("t_abs", [TW, 1])
        inv_t = sb("inv_t", [TW, 1])
        iota = sb("iota", [TW, NP])
        ident, w_hi, w_lo, at_hi, at_lo, xb = sh.ident, sh.w_hi, sh.w_lo, sh.at_hi, sh.at_lo, sh.xb
        at_ready, xb_ready = sh.at_ready, sh.xb_ready
        x1 = sb("x1", [TW, B, TC, E])
        y2 = sb("y2", [TW, TC, E])
        yt_hi = sb("yt_hi", [P, KT, T], F32R)
        yt_lo = sb("yt_lo", [P, KT, T], F32R)
        stats = sb("stats2", [TW, TC, 6])
        mv = sb("mv2", [TW, TC, 2])
        veps = sb("veps2", [TW, TC])
        sd = sb("sd2", [TW, TC])
        rstd = sb("rstd2", [TW, TC])
        nwt = sb("nwt2", [TW, 4, TC])
        x2 = sb("x2", [TW, TC])
        dot = sb("dot", [NP, T])
        d2 = sb("d2", [TW, TC, NP])
        dist = sb("dist", [TW, TC, NP])
        near = sb("near", [TW, TC, NP])
        top = sb("top", [TW, TC, 8])
        top_at = sb("top_at", [TW, TC, 8], mybir.dt.uint32)
        top_f = sb("top_f", [TW, TC, 2])
        gap = sb("gap", [TW, TC])
        ez = sb("ez", [TW, TC])
        ez1 = sb("ez1", [TW, TC])
        wt = sb("wt", [TW, 2, TC])
        pick = sb("pick", [TW, 2, TC, NP])
        route = sb("route", [TW, TC, NP])
        route_st = sb("route_st", [TW, TC, 4, NP], F32R)
        route_wide = sb("route_wide", [TW, TC, NP, RK])
        route_t = sb("route_t", [P, T], F32R)
        h_sb = sb("h_sb", [P, MT, T])
        gated = sb("gated", [P, MT, T])
        g_hi = sb("g_hi", [P, MT, T], F32R)
        g_lo = sb("g_lo", [P, MT, T], F32R)
        y_out = [sb(f"y_out{c}", [TW, E]) for c in range(TC)]
        big = [ps(f"big{c}", [P, 512]) for c in range(TC)]
        tr = [ps(f"tr{c}", [P, 512]) for c in range(TC)]
        dot_ps = ps("dot_ps", [P, 512])
        route_ps = ps("route_ps", [P, 512])
        h_ps = [ps(f"h_ps{j}", [P, 512]) for j in range(2)]

        small_loaded = sem("small_loaded")
        small_step = sem("small_step")
        small_ready = sem("small_ready")
        pt_ready = sem("pt_ready")
        p2_ready = sem("p2_ready")
        passed = sem("passed3")
        at_more_loaded = sem("at_more_loaded")
        xr_more_loaded = sem("xr_more_loaded")
        iota_ready = sem("iota_ready")
        o_ready = sem("o_ready")
        x1_ready = sem("x1_ready")
        ln_step = sem("ln_step3")
        veps_ready = sem("veps_ready3")
        sd_ready = sem("sd_ready3")
        y2_ready = sem("y2_ready")
        x2_ready = sem("x2_ready")
        yt_ps_ready = sem("yt_ps_ready")
        yt_hi_ready = sem("yt_hi_ready")
        yt_ready = sem("yt_ready")
        dot_ps_ready = sem("dot_ps_ready")
        dot_ready = sem("dot_ready")
        dot_t_ready = sem("dot_t_ready")
        d2_ready = sem("d2_ready")
        dist_ready = sem("dist_ready")
        top_step = sem("top_step")
        gap_ready = sem("gap_ready")
        ez_ready = sem("ez_ready")
        route_ready = sem("route_ready")
        route_st_ready = sem("route_st_ready")
        wide_ready = sem("wide_ready")
        route_ps_ready = sem("route_ps_ready")
        route_t_ready = sem("route_t_ready")
        wide_ps_ready = sem("wide_ps_ready")
        h_ps_ready = sem("h_ps_ready")
        h_ready = sem("h_ready")
        gated_ready = sem("gated_ready")
        g_hi_ready = sem("g_hi_ready")
        g_ready = sem("g_ready")
        y_ps_ready = sem("y_ps_ready")
        y_ready = sem("y_ready")
        y_stored = [sem(f"y_stored{c}") for c in range(TC)]
        TOPS = 10
        LAST = B - 1

        block = ctx.enter_context(nc.Block())

        @block.sync
        def _(eng):
            for started in (*y_stored,):
                eng.sem_inc(started, 1)
            def store(b):
                for c in range(TC):
                    eng.wait_ge(y_ready, 1 + TC * b + c + 1)
                    eng.dma_start(out[b, c * TW:(c + 1) * TW, :], y_out[c][:, :]).then_inc(y_stored[c], 16)

            eng.dma_start(pt_stage[:, :, :], protos_t.rearrange("(k p) n -> p k n", p=P)).then_inc(small_loaded, 16)
            eng.dma_start(protos_sb[:, :], protos).then_inc(small_loaded, 16)
            for r in range(4):
                eng.dma_start(bst_raw[r * NP:(r + 1) * NP, :], f_bias).then_inc(small_loaded, 16)
            eng.dma_start(temp_col[:, :], temp.partition_broadcast(TW)).then_inc(small_loaded, 16)
            with eng.Fori(0, B) as b:
                store(b)
            for c in range(TC):
                eng.wait_ge(y_stored[c], 1 + 16 * B)

        @block.gpsimd
        def _(eng):
            eng.iota(iota[:, :], [[1, NP]], 0, 0, allow_small_or_imprecise_dtypes=True).then_inc(iota_ready, 1)

            def split(b, at_loaded, xr_loaded, loads):
                eng.wait_ge(o_ready, 1 + TC * b)
                split_attended(eng, sh, at_loaded, xr_loaded, loads, b, passed)
                eng.wait_ge(x1_ready, 1 + TC * b)
                add_output_bias(eng, sh)

            def load(b):
                eng.wait_ge(xb_ready, b)
                load_attended(eng, sh, x, attn_t, b, at_more_loaded, xr_more_loaded)

            split(1, sh.at_loaded, sh.xr_loaded, 2)
            for p in range(2):
                eng.wait_ge(sh.attn_stored[p], 1 + 16 * B * NG // 2)
            load(2)
            with eng.Fori(2, B - 1) as b:
                split(b, at_more_loaded, xr_more_loaded, b - 1)
                load(b + 1)
            split(B - 1, at_more_loaded, xr_more_loaded, B - 2)

        @block.scalar
        def _(eng):
            for started in (wide_ready, g_hi_ready, x2_ready):
                eng.sem_inc(started, 1)
            def deviation(b):
                eng.wait_ge(veps_ready, b + 1)
                nc.scalar.activation(sd[:, :], veps[:, :], ACT.Sqrt).then_inc(sd_ready, 1)

            deviation(0)
            eng.wait_ge(small_loaded, 16 * 7)
            nc.scalar.activation(pt_hi[:, :, :], pt_stage[:, :, :], ACT.Copy).then_inc(small_step, 1)
            nc.scalar.activation(bst_hi[:, :], bst_raw[:, :], ACT.Copy).then_inc(small_step, 1)
            nc.scalar.activation(squares[0:NP, :], protos_sb[:, :], ACT.Square, accum_out=p2[:, :])\
                .then_inc(p2_ready, 1)
            eng.wait_ge(p2_ready, 1)

            def norm(b):
                eng.wait_ge(y2_ready, b + 1)
                for c in range(TC):
                    eng.wait_ge(yt_ps_ready, TC * b + c + 1)
                    nc.scalar.activation(yt_hi[:, :, c * TW:(c + 1) * TW],
                                         tr[c][:, 0:KT * TW].rearrange("p (k t) -> p k t", k=KT),
                                         ACT.Copy).then_inc(yt_hi_ready, 1)
                for c in range(TC):
                    eng.wait_ge(x2_ready, 1 + TC * b + c)
                    nc.scalar.activation(squares[:, :], y2[:, c, :], ACT.Square,
                                         accum_out=x2[:, c:c + 1]).then_inc(x2_ready, 1)

            def copy_h(b, j):
                eng.wait_ge(h_ps_ready, 2 * b + j + 1)
                nc.scalar.activation(h_sb[:, 2 * j:2 * j + 2, :],
                                     h_ps[j][:, 0:2 * T].rearrange("p (m t) -> p m t", m=2),
                                     ACT.Copy).then_inc(h_ready, 1)

            def distance_root(b):
                eng.wait_ge(d2_ready, b + 1)
                nc.scalar.activation(dist[:, :, :], d2[:, :, :], ACT.Sqrt).then_inc(dist_ready, 1)

            def second_weight(b):
                eng.wait_ge(gap_ready, b + 1)
                nc.scalar.activation(ez[:, :], gap[:, :], ACT.Exp, scale=inv_t[:, 0:1]).then_inc(ez_ready, 1)

            def widen_route(b):
                eng.wait_ge(route_ready, b + 1)
                nc.scalar.activation(route_wide[:, :, :, :],
                                     route[:, :, :].unsqueeze(3).broadcast_to([TW, TC, NP, RK]),
                                     ACT.Copy).then_inc(wide_ready, 1)

            def route_part(b):
                copy_h(b, 0)
                distance_root(b)
                copy_h(b, 1)
                second_weight(b)
                widen_route(b)

            def experts(b):
                eng.wait_ge(route_ps_ready, 1 + b + 1)
                nc.scalar.activation(route_t[:, :], route_ps[:, 0:T], ACT.Copy).then_inc(route_t_ready, 1)
                eng.wait_ge(gated_ready, b + 1)
                nc.scalar.activation(g_hi[:, :, :], gated[:, :, :], ACT.Copy).then_inc(g_hi_ready, 1)

            norm(0)
            distance_root(0)
            eng.wait_ge(small_ready, 1)
            second_weight(0)
            widen_route(0)
            deviation(1)
            copy_h(0, 0)
            copy_h(0, 1)
            norm(1)
            experts(0)
            route_part(1)
            with eng.Fori(1, LAST) as b:
                deviation(b + 1)
                norm(b + 1)
                experts(b)
                route_part(b + 1)
            eng.wait_ge(y_ps_ready, TC * LAST)
            experts(LAST)

        @block.vector
        def _(eng):
            for started in (x1_ready, y_ready):
                eng.sem_inc(started, 1)

            def small_first():
                eng.wait_ge(small_step, 2)
                nc.vector.tensor_tensor(pt_lo[:, :, :], pt_stage[:, :, :], pt_hi[:, :, :].bitcast(F32), ALU.subtract)\
                    .then_inc(pt_ready, 1)
                eng.wait_ge(p2_ready, 1)

            def small_later():
                for r in range(4):
                    rows = slice(r * NP, (r + 1) * NP)
                    if r % 2 == 0:
                        nc.vector.tensor_copy(bst[rows, :], bst_hi[rows, :].bitcast(F32))
                    else:
                        nc.vector.tensor_tensor(bst[rows, :], bst_raw[rows, :], bst_hi[rows, :].bitcast(F32),
                                                ALU.subtract)
                nc.vector.tensor_scalar(t_neg[:, :], temp_col[:, :], -1.0, 0.1, ALU.mult, ALU.max)\
                    .then_inc(small_step, 1)
                eng.wait_ge(small_step, 3)
                nc.vector.tensor_tensor(t_abs[:, :], temp_col[:, :], t_neg[:, :], ALU.max).then_inc(small_step, 1)
                eng.wait_ge(small_step, 4)
                nc.vector.reciprocal(inv_t[:, :], t_abs[:, :]).then_inc(small_ready, 1)
                eng.wait_ge(iota_ready, 1)

            def residual(b, c):
                if c == 0:
                    eng.wait_ge(xb_ready, b + 1)
                eng.wait_ge(o_ready, 1 + TC * b + c + 1)
                nc.vector.tensor_tensor(x1_of(b)[:, c, :], big[c][0:TW, :], xb[:, c, :], ALU.add)\
                    .then_inc(x1_ready, 1)

            def x1_of(b):
                return x1[:, bass.DynSlice(b, 1), :, :].rearrange("t b c e -> t (b c) e")

            def norm(b):
                eng.wait_ge(x1_ready, 1 + TC * (b + 1))
                layer_norm_stats(nc, eng, x1_of(b), stats, mv, veps, ln_step, 9 * b, passed)\
                    .then_inc(veps_ready, 1)

            def normalise(b):
                eng.wait_ge(sd_ready, b + 1)
                rsqrt_refined(nc, eng, sd, veps, rstd, nwt, ln_step, 9 * b + 4)
                for c in range(TC):
                    last = nc.vector.tensor_scalar(y2[:, c, :], x1_of(b)[:, c, :], mv[:, c, 0:1],
                                                   nwt[:, 3, c:c + 1], ALU.subtract, ALU.mult)
                last.then_inc(y2_ready, 1)

            def yt_low(b):
                for c in range(TC):
                    eng.wait_ge(yt_hi_ready, TC * b + c + 1)
                    nc.vector.tensor_tensor(yt_lo[:, :, c * TW:(c + 1) * TW],
                                            tr[c][:, 0:KT * TW].rearrange("p (k t) -> p k t", k=KT),
                                            yt_hi[:, :, c * TW:(c + 1) * TW].bitcast(F32), ALU.subtract)\
                        .then_inc(yt_ready, 1)

            def routing_dot(b):
                eng.wait_ge(dot_ps_ready, b + 1)
                nc.vector.tensor_scalar(dot[:, :], dot_ps[0:NP, 0:T], -2.0, p2[:, 0:1], ALU.mult, ALU.add)\
                    .then_inc(dot_ready, 1)

            def routing(b):
                n = TOPS * b
                eng.wait_ge(dot_t_ready, b + 1)
                eng.wait_ge(x2_ready, 1 + TC * (b + 1))
                for c in range(TC):
                    last = nc.vector.tensor_scalar(d2[:, c, :], dot_ps[0:TW, 256 + c * NP:256 + (c + 1) * NP],
                                                   x2[:, c:c + 1], 0.0, ALU.add, ALU.max)
                last.then_inc(d2_ready, 1)
                eng.wait_ge(dist_ready, b + 1)
                nc.vector.tensor_scalar(near[:, :, :], dist[:, :, :], -1.0, None, ALU.mult).then_inc(top_step, 1)
                eng.wait_ge(top_step, n + 1)
                apart(eng, passed)
                for c in range(TC):
                    nc.vector.max(top[:, c, :], near[:, c, :]).then_inc(top_step, 1)
                eng.wait_ge(top_step, n + 3)
                nc.vector.tensor_tensor(gap[:, :], top[:, :, 1], top[:, :, 0], ALU.subtract).then_inc(gap_ready, 1)
                for c in range(TC):
                    nc.vector.max_index(top_at[:, c, :], top[:, c, :], near[:, c, :]).then_inc(top_step, 1)
                eng.wait_ge(top_step, n + 5)
                nc.vector.tensor_copy(top_f[:, :, :], top_at[:, :, 0:2]).then_inc(top_step, 1)
                eng.wait_ge(ez_ready, b + 1)
                nc.vector.tensor_scalar(ez1[:, :], ez[:, :], 1.0, None, ALU.add).then_inc(top_step, 1)
                eng.wait_ge(top_step, n + 7)
                nc.vector.reciprocal(wt[:, 0, :], ez1[:, :]).then_inc(top_step, 1)
                eng.wait_ge(top_step, n + 8)
                nc.vector.tensor_tensor(wt[:, 1, :], wt[:, 0, :], ez[:, :], ALU.mult).then_inc(top_step, 1)
                eng.wait_ge(top_step, n + 9)
                for j in range(2):
                    for c in range(TC):
                        last = nc.vector.tensor_scalar(pick[:, j, c, :], iota[:, :], top_f[:, c, j:j + 1],
                                                       wt[:, j, c:c + 1], ALU.is_equal, ALU.mult)
                last.then_inc(top_step, 1)
                eng.wait_ge(top_step, n + 10)
                eng.wait_ge(wide_ready, 1 + b)
                nc.vector.tensor_tensor(route[:, :, :], pick[:, 0, :, :], pick[:, 1, :, :], ALU.add)\
                    .then_inc(route_ready, 1)
                eng.wait_ge(route_ready, b + 1)
                eng.wait_ge(route_ps_ready, 1 + b)
                two = [TW, TC, 2, NP]
                nc.vector.tensor_copy(route_st[:, :, 0:2, :], route[:, :, :].unsqueeze(2).broadcast_to(two))\
                    .then_inc(route_st_ready, 1)
                eng.wait_ge(route_st_ready, 2 * b + 1)
                nc.vector.tensor_tensor(route_st[:, :, 2:4, :], route[:, :, :].unsqueeze(2).broadcast_to(two),
                                        route_st[:, :, 0:2, :].bitcast(F32), ALU.subtract)\
                    .then_inc(route_st_ready, 1)

            def gate(b):
                eng.wait_ge(h_ready, 2 * b + 2)
                eng.wait_ge(g_hi_ready, 1 + b)
                for c in range(TC):
                    eng.wait_ge(wide_ps_ready, TC * b + c + 1)
                    last = nc.vector.tensor_tensor(gated[:, :, c * TW:(c + 1) * TW],
                                                   big[c][:, 0:MT * TW].rearrange("p (m t) -> p m t", m=MT),
                                                   h_sb[:, :, c * TW:(c + 1) * TW], ALU.mult)
                last.then_inc(gated_ready, 1)

            def gated_low(b):
                eng.wait_ge(g_hi_ready, 1 + b + 1)
                nc.vector.tensor_tensor(g_lo[:, :, :], gated[:, :, :], g_hi[:, :, :].bitcast(F32), ALU.subtract)\
                    .then_inc(g_ready, 1)

            def result(b, c):
                eng.wait_ge(y_ps_ready, TC * b + c + 1)
                eng.wait_ge(y_stored[c], 1 + 16 * b)
                nc.vector.tensor_tensor(y_out[c][:, :], h_ps[c][0:TW, :], x1_of(b)[:, c, :], ALU.add)\
                    .then_inc(y_ready, 1)

            residual(0, 0)
            residual(0, 1)
            norm(0)
            normalise(0)
            small_first()
            yt_low(0)
            routing_dot(0)
            small_later()
            residual(1, 0)
            routing(0)
            residual(1, 1)
            norm(1)
            normalise(1)

            def turn_of(b, before):
                if before:
                    residual(b + 1, 0)
                    residual(b + 1, 1)
                    norm(b + 1)
                    normalise(b + 1)
                    result(b - 1, 0)
                yt_low(b + 1)
                if before:
                    result(b - 1, 1)
                gate(b)
                gated_low(b)
                routing_dot(b + 1)
                routing(b + 1)

            turn_of(0, False)
            with eng.Fori(1, LAST) as b:
                turn_of(b, True)
            result(LAST - 1, 0)
            gate(LAST)
            gated_low(LAST)
            result(LAST - 1, 1)
            for c in range(TC):
                result(LAST, c)

        @block.tensor
        def _(eng):
            for started in (o_ready, route_ps_ready):
                eng.sem_inc(started, 1)
            def three_passes(out_ap, left, right, tiles, first=True, last=True):
                n = 0
                for k in range(tiles):
                    for a, c in ((0, 0), (0, 1), (1, 0)):
                        ins = nc.tensor.matmul(out_ap, left(a, k), right(c, k), start=(first and n == 0),
                                               stop=(last and n == 3 * tiles - 1))
                        n += 1
                return ins

            def w_of(j):
                return lambda a, k: (w_hi, w_lo)[a][j][:, k, :]

            def project_out(b, c, first=False):
                if c == 0:
                    eng.wait_ge(at_ready, b + 1)
                if not first:
                    eng.wait_ge(x1_ready, 1 + TC * (b - 1) + c + 1)
                    if not isinstance(b, int) or b > 1:
                        eng.wait_ge(gated_ready, b - 1)
                three_passes(big[c][0:TW, :], lambda a, k: (at_hi, at_lo)[a][:, k, c * TW:(c + 1) * TW], w_of(0), NG)\
                    .then_inc(o_ready, 1)

            def transpose_y(b):
                eng.wait_ge(y2_ready, b + 1)
                for c in range(TC):
                    for k in range(KT):
                        last = nc.tensor.transpose(tr[c][:, k * TW:(k + 1) * TW], y2[:, c, k * P:(k + 1) * P],
                                                   ident[0:TW, 0:TW])
                    last.then_inc(yt_ps_ready, 1)

            def distances(b):
                eng.wait_ge(yt_ready, TC * (b + 1))
                three_passes(dot_ps[0:NP, 0:T], lambda a, k: (pt_hi, pt_lo)[a][:, k, :],
                             lambda c, k: (yt_hi, yt_lo)[c][:, k, :], KT).then_inc(dot_ps_ready, 1)

            def down(b, j):
                for m in range(2):
                    tile = 2 * j + m
                    last = three_passes(h_ps[j][:, m * T:(m + 1) * T],
                                        lambda a, k: (w_hi, w_lo)[a][1][:, k, tile * P:(tile + 1) * P],
                                        lambda c, k: (yt_hi, yt_lo)[c][:, k, :], KT)
                last.then_inc(h_ps_ready, 1)

            def transpose_dot(b):
                eng.wait_ge(dot_ready, b + 1)
                apart(eng, passed)
                for c in range(TC):
                    last = nc.tensor.transpose(dot_ps[0:TW, 256 + c * NP:256 + (c + 1) * NP],
                                               dot[:, c * TW:(c + 1) * TW], ident[0:NP, 0:NP])
                last.then_inc(dot_t_ready, 1)

            def transpose_routes(b, before):
                eng.wait_ge(wide_ready, 1 + b + 1)
                for c in range(TC):
                    if before is not None:
                        eng.wait_ge(x1_ready, before + c + 1)
                    for m in range(MT):
                        last = nc.tensor.transpose(
                            big[c][:, m * TW:(m + 1) * TW],
                            route_wide[:, c, m * PM:(m + 1) * PM, :].rearrange("t n r -> t (n r)"),
                            ident[0:TW, 0:TW])
                    last.then_inc(wide_ps_ready, 1)
                eng.wait_ge(route_st_ready, 2 * b + 2)
                for c in range(TC):
                    last = nc.tensor.transpose(route_ps[:, c * TW:(c + 1) * TW],
                                               route_st[:, c, :, :].rearrange("t r n -> t (r n)").bitcast(F32),
                                               ident[0:TW, 0:TW])
                last.then_inc(route_ps_ready, 1)

            def up(b, c):
                if c == 0:
                    eng.wait_ge(route_t_ready, b + 1)
                    eng.wait_ge(g_ready, b + 1)
                three_passes(h_ps[c][0:TW, :], lambda a, k: (g_hi, g_lo)[a][:, k, c * TW:(c + 1) * TW],
                             w_of(2), MT, last=False)
                nc.tensor.matmul(h_ps[c][0:TW, :], route_t[:, c * TW:(c + 1) * TW], bst[:, :],
                                 start=False, stop=True).then_inc(y_ps_ready, 1)

            def turn_of(b, before):
                if before:
                    for c in range(TC):
                        project_out(b + 1, c)
                eng.wait_ge(h_ready, 2 * b + 2)
                if before:
                    for c in range(TC):
                        up(b - 1, c)
                transpose_y(b + 1)
                transpose_routes(b, 1 + TC * (b + 1))
                distances(b + 1)
                if before:
                    eng.wait_ge(y_ready, 1 + TC * b)
                down(b + 1, 0)
                transpose_dot(b + 1)
                down(b + 1, 1)

            for c in range(TC):
                project_out(0, c, True)
            transpose_y(0)
            eng.wait_ge(pt_ready, 1)
            distances(0)
            project_out(1, 0)
            transpose_dot(0)
            project_out(1, 1)
            for j in range(2):
                down(0, j)
            eng.wait_ge(small_ready, 1)
            turn_of(0, False)
            with eng.Fori(1, LAST) as b:
                turn_of(b, True)
            eng.wait_ge(h_ready, 2 * LAST + 2)
            up(LAST - 1, 0)
            transpose_routes(LAST, None)
            up(LAST - 1, 1)
            eng.wait_ge(y_ready, 1 + TC * LAST)
            for c in range(TC):
                up(LAST, c)


def build(nc, x, ctx_t, bias, mask, w_in_t, b_in, bv, w_out_t, b_out, protos, protos_t, fb_t, fa_t, f_bias, temp,
          out):
    q_parts = nc.dram_tensor("q_parts", [B, 2, E, T], F32, kind="Internal").ap()
    k_parts = nc.dram_tensor("k_parts", [B, 2, E, S], F32, kind="Internal").ap()
    v_all = nc.dram_tensor("v_all", [B, S, E], F32, kind="Internal").ap()
    attn_t = nc.dram_tensor("attn_t", [B, E, T], F32, kind="Internal").ap()
    with ExitStack() as ctx:
        sh = Shared(nc, ctx)
        with ExitStack() as until_attended:
            sh.until_attended(nc, until_attended)
            project(nc, x, ctx_t, w_in_t, b_in, bv, bias, mask, q_parts, k_parts, v_all, sh)
            attend(nc, mask, x, b_out, q_parts, k_parts, v_all, attn_t, (w_out_t, fb_t, fa_t), sh)
        finish(nc, x, attn_t, protos, protos_t, f_bias, temp, out, sh)


def kernel(**inputs):
    import concourse.bacc as bacc
    from concourse.bass_utils import run_bass_kernel_spmd

    w_in, b_in = inputs["L0_xattn_in_proj_w"], inputs["L0_xattn_in_proj_b"]
    fa, fb = inputs["L0_ffn_A"], inputs["L0_ffn_B"]
    laid = {
        "x": inputs["x"],
        "ctx_t": inputs["ctx_1024"].transpose(0, 2, 1),
        "bias": inputs["fside_1xSxS2_0"].reshape(T, S),
        "mask": inputs["mask_BxS2_bk0"],
        "w_in_t": w_in.T,
        "b_in": b_in.reshape(3 * KT, P).T,
        "bv": b_in[2 * E:],
        "w_out_t": inputs["L0_xattn_out_proj_w"].T,
        "b_out": inputs["L0_xattn_out_proj_b"],
        "protos": inputs["L0_ffn_prototypes"],
        "protos_t": inputs["L0_ffn_prototypes"].T,
        "fb_t": fb.reshape(NP * RK, E).T,
        "fa_t": fa.transpose(0, 2, 1).reshape(NP * RK, E),
        "f_bias": inputs["L0_ffn_bias"],
        "temp": inputs["L0_ffn_temp"].reshape(1),
    }
    nc = bacc.Bacc("TRN2", target_bir_lowering=False, num_devices=1)
    arrays, args = {}, []
    for name, a in laid.items():
        a = np.ascontiguousarray(a)
        arrays[f"in_{name}"] = a
        args.append(nc.dram_tensor(f"in_{name}", a.shape, mybir.dt.from_np(a.dtype), kind="ExternalInput").ap())
    out = nc.dram_tensor("out", (B, T, E), F32, kind="ExternalOutput").ap()
    build(nc, *args, out)
    r = run_bass_kernel_spmd(nc, [arrays], core_ids=[0])
    return r.results[0]["out"]
```
